# Optimizing a Trainium2 kernel written in Bass

```python
import numpy as np
import jax
import jax.numpy as jnp

def _softmax(x, axis=-1):
    return jax.nn.softmax(x, axis=axis)

def _gelu(x):
    return jax.nn.gelu(x, approximate=True)

def _silu(x):
    return jax.nn.silu(x)

def _sigmoid(x):
    return jax.nn.sigmoid(x)

def _layernorm(x, axis=-1, eps=1e-05):
    m = jnp.mean(x, axis=axis, keepdims=True)
    v = jnp.var(x, axis=axis, keepdims=True)
    return (x - m) / jnp.sqrt(v + eps)

def _scatter_add(tgt, idx, src, axis=0):
    return tgt.at[idx].add(src)

def _segment_sum(src, seg, n):
    return jax.ops.segment_sum(src, seg, n)
kernel_name = 'mk_adaln_d1_jaxref_r8_7fcaa9'

def setup_inputs(seed: int=0):
    np.random.seed(seed)
    _w = jnp.asarray

    def _L0_attn_setup():
        import jax, jax.numpy as jnp
        import numpy as np
        HID = 256
        NK, DK = (16, 128)
        NV, DV = (32, 128)
        KC = 4
        P = NV // NK
        SV = P * DV
        QD = NK * DK
        VD = NV * DV
        QKV = QD + QD + VD
        B, T = (2, 256)
        EPS_NORM = 1e-12
        EPS_RMS = 1e-06

        def _l2norm(x):
            n = jnp.sqrt(jnp.sum(x * x, axis=-1, keepdims=True))
            return x / jnp.maximum(n, EPS_NORM)

        def _reference_tuple_inner(x, W_qkv, W_z, W_b, W_a, conv_w, dt_bias, A_log, norm_w, W_out):
            Bq, Tq, _ = x.shape
            qkv = jnp.einsum('btc,dc->btd', x, W_qkv)
            z = jnp.einsum('btc,dc->btd', x, W_z)
            beta = jax.nn.sigmoid(jnp.einsum('btc,hc->bth', x, W_b))
            dt = jax.nn.softplus(jnp.einsum('btc,hc->bth', x, W_a) + dt_bias)
            decay = jnp.exp(-dt * jnp.exp(A_log))
            xp = jnp.pad(qkv, ((0, 0), (KC - 1, 0), (0, 0)))
            qkv_c = sum((xp[:, j:j + Tq, :] * conv_w[:, j] for j in range(KC)))
            new_conv_buf = jnp.transpose(xp[:, -(KC - 1):, :], (0, 2, 1))
            q = _l2norm(qkv_c[..., :QD].reshape(Bq, Tq, NK, DK))
            k = _l2norm(qkv_c[..., QD:2 * QD].reshape(Bq, Tq, NK, DK))
            v = qkv_c[..., 2 * QD:].reshape(Bq, Tq, NK, P, DV)
            beta_r = beta.reshape(Bq, Tq, NK, P)
            decay_r = decay.reshape(Bq, Tq, NK, P)
            qT = jnp.swapaxes(q, 0, 1)
            kT = jnp.swapaxes(k, 0, 1)
            vT = jnp.swapaxes(v, 0, 1)
            bT = jnp.swapaxes(beta_r, 0, 1)
            dT = jnp.swapaxes(decay_r, 0, 1)

            def step(S, inp):
                q_t, k_t, v_t, b_t, d_t = inp
                Sk = jnp.einsum('bhi,bhipj->bhpj', k_t, S)
                dv = b_t[..., None] * (v_t - Sk)
                upd = jnp.einsum('bhi,bhpj->bhipj', k_t, dv)
                S = S * d_t[:, :, None, :, None] + upd
                o = jnp.einsum('bhi,bhipj->bhpj', q_t, S)
                return (S, o)
            S0 = jnp.zeros((Bq, NK, DK, P, DV), x.dtype)
            S_final, outs = jax.lax.scan(step, S0, (qT, kT, vT, bT, dT))
            out = jnp.swapaxes(outs, 0, 1).reshape(Bq, Tq, NV, DV)
            rms = jax.lax.rsqrt(jnp.mean(out * out, axis=-1, keepdims=True) + EPS_RMS)
            out = out * rms * norm_w
            out = out.reshape(Bq, Tq, VD) * jax.nn.silu(z)
            y = jnp.einsum('btd,cd->btc', out, W_out)
            return (y, S_final.reshape(Bq, NK, DK, SV), new_conv_buf)
        key = jax.random.key(seed)
        ks = jax.random.split(key, 8)
        lin = lambda k, o, i: jax.random.normal(k, (o, i), jnp.float32) / np.sqrt(i).astype(np.float32)
        return {'x': jax.random.normal(ks[0], (B, T, HID), jnp.float32), 'W_qkv': lin(ks[1], QKV, HID), 'W_z': lin(ks[2], VD, HID), 'W_b': lin(ks[3], NV, HID), 'W_a': lin(ks[4], NV, HID), 'conv_w': jax.random.normal(ks[5], (QKV, KC), jnp.float32) * 0.1, 'dt_bias': jnp.zeros((NV,), jnp.float32), 'A_log': jnp.zeros((NV,), jnp.float32), 'norm_w': jnp.ones((DV,), jnp.float32), 'W_out': lin(ks[6], HID, VD)}
    _L0_attn_in = _L0_attn_setup()

    def _L0_ffn_setup():
        import jax, jax.numpy as jnp
        import numpy as np

        def _sparsify_2to4(h):
            B, S, I = h.shape
            g = h.reshape(B, S, I // 4, 4)
            a = jnp.abs(g)
            _, idx = jax.lax.top_k(a, 2)
            pos = jnp.arange(4)
            mask = (pos == idx[..., 0:1]) | (pos == idx[..., 1:2])
            return (g * mask.astype(g.dtype)).reshape(B, S, I)
        key = jax.random.key(seed)
        k1, k2, k3, k4 = jax.random.split(key, 4)
        B, S, H, I = (4, 256, 256, 1024)
        x = jax.random.normal(k1, (B, S, H), dtype=jnp.float32)
        w_gate = jax.random.normal(k2, (H, I), dtype=jnp.float32) / np.sqrt(H)
        w_up = jax.random.normal(k3, (H, I), dtype=jnp.float32) / np.sqrt(H)
        w_down = jax.random.normal(k4, (I, H), dtype=jnp.float32) / np.sqrt(I)
        return {'x': x, 'w_gate': w_gate, 'w_up': w_up, 'w_down': w_down}
    _L0_ffn_in = _L0_ffn_setup()
    _L0_c = _w((lambda *s: np.random.randn(*s).astype(np.float32) * 0.05)(8, 256))
    _L0_wmod = _w((lambda *s: np.random.randn(*s).astype(np.float32) * 0.05)(256, 6 * 256) * 256 ** (-0.5))
    _d = {'L0_attn_x': _L0_attn_in['x'], 'L0_attn_W_qkv': _L0_attn_in['W_qkv'], 'L0_attn_W_z': _L0_attn_in['W_z'], 'L0_attn_W_b': _L0_attn_in['W_b'], 'L0_attn_W_a': _L0_attn_in['W_a'], 'L0_attn_conv_w': _L0_attn_in['conv_w'], 'L0_attn_dt_bias': _L0_attn_in['dt_bias'], 'L0_attn_A_log': _L0_attn_in['A_log'], 'L0_attn_norm_w': _L0_attn_in['norm_w'], 'L0_attn_W_out': _L0_attn_in['W_out'], 'L0_ffn_w_gate': _L0_ffn_in['w_gate'], 'L0_ffn_w_up': _L0_ffn_in['w_up'], 'L0_ffn_w_down': _L0_ffn_in['w_down'], 'L0_c': _L0_c, 'L0_wmod': _L0_wmod}
    _x0 = _d['L0_attn_x']
    _d['L0_attn_x'] = jax.random.normal(jax.random.fold_in(jax.random.key(seed), 1), (8, 256, 256), dtype=_x0.dtype)
    del _x0
    return _d

def reference(L0_attn_x, L0_attn_W_qkv, L0_attn_W_z, L0_attn_W_b, L0_attn_W_a, L0_attn_conv_w, L0_attn_dt_bias, L0_attn_A_log, L0_attn_norm_w, L0_attn_W_out, L0_ffn_w_gate, L0_ffn_w_up, L0_ffn_w_down, L0_c, L0_wmod):

    def _L0_attn_ref(x, W_qkv, W_z, W_b, W_a, conv_w, dt_bias, A_log, norm_w, W_out):
        import jax, jax.numpy as jnp
        import numpy as np
        HID = 256
        NK, DK = (16, 128)
        NV, DV = (32, 128)
        KC = 4
        P = NV // NK
        SV = P * DV
        QD = NK * DK
        VD = NV * DV
        QKV = QD + QD + VD
        B, T = (2, 256)
        EPS_NORM = 1e-12
        EPS_RMS = 1e-06

        def _l2norm(x):
            n = jnp.sqrt(jnp.sum(x * x, axis=-1, keepdims=True))
            return x / jnp.maximum(n, EPS_NORM)

        def _reference_tuple_inner(x, W_qkv, W_z, W_b, W_a, conv_w, dt_bias, A_log, norm_w, W_out):
            Bq, Tq, _ = x.shape
            qkv = jnp.einsum('btc,dc->btd', x, W_qkv)
            z = jnp.einsum('btc,dc->btd', x, W_z)
            beta = jax.nn.sigmoid(jnp.einsum('btc,hc->bth', x, W_b))
            dt = jax.nn.softplus(jnp.einsum('btc,hc->bth', x, W_a) + dt_bias)
            decay = jnp.exp(-dt * jnp.exp(A_log))
            xp = jnp.pad(qkv, ((0, 0), (KC - 1, 0), (0, 0)))
            qkv_c = sum((xp[:, j:j + Tq, :] * conv_w[:, j] for j in range(KC)))
            new_conv_buf = jnp.transpose(xp[:, -(KC - 1):, :], (0, 2, 1))
            q = _l2norm(qkv_c[..., :QD].reshape(Bq, Tq, NK, DK))
            k = _l2norm(qkv_c[..., QD:2 * QD].reshape(Bq, Tq, NK, DK))
            v = qkv_c[..., 2 * QD:].reshape(Bq, Tq, NK, P, DV)
            beta_r = beta.reshape(Bq, Tq, NK, P)
            decay_r = decay.reshape(Bq, Tq, NK, P)
            qT = jnp.swapaxes(q, 0, 1)
            kT = jnp.swapaxes(k, 0, 1)
            vT = jnp.swapaxes(v, 0, 1)
            bT = jnp.swapaxes(beta_r, 0, 1)
            dT = jnp.swapaxes(decay_r, 0, 1)

            def step(S, inp):
                q_t, k_t, v_t, b_t, d_t = inp
                Sk = jnp.einsum('bhi,bhipj->bhpj', k_t, S)
                dv = b_t[..., None] * (v_t - Sk)
                upd = jnp.einsum('bhi,bhpj->bhipj', k_t, dv)
                S = S * d_t[:, :, None, :, None] + upd
                o = jnp.einsum('bhi,bhipj->bhpj', q_t, S)
                return (S, o)
            S0 = jnp.zeros((Bq, NK, DK, P, DV), x.dtype)
            S_final, outs = jax.lax.scan(step, S0, (qT, kT, vT, bT, dT))
            out = jnp.swapaxes(outs, 0, 1).reshape(Bq, Tq, NV, DV)
            rms = jax.lax.rsqrt(jnp.mean(out * out, axis=-1, keepdims=True) + EPS_RMS)
            out = out * rms * norm_w
            out = out.reshape(Bq, Tq, VD) * jax.nn.silu(z)
            y = jnp.einsum('btd,cd->btc', out, W_out)
            return (y, S_final.reshape(Bq, NK, DK, SV), new_conv_buf)
        return _reference_tuple_inner(x, W_qkv, W_z, W_b, W_a, conv_w, dt_bias, A_log, norm_w, W_out)[0]

    def _L0_ffn_ref(x, w_gate, w_up, w_down):
        import jax, jax.numpy as jnp
        import numpy as np

        def _sparsify_2to4(h):
            B, S, I = h.shape
            g = h.reshape(B, S, I // 4, 4)
            a = jnp.abs(g)
            _, idx = jax.lax.top_k(a, 2)
            pos = jnp.arange(4)
            mask = (pos == idx[..., 0:1]) | (pos == idx[..., 1:2])
            return (g * mask.astype(g.dtype)).reshape(B, S, I)
        h = jax.nn.silu(jnp.einsum('bsh,hi->bsi', x, w_gate)) * jnp.einsum('bsh,hi->bsi', x, w_up)
        h_sparse = _sparsify_2to4(h)
        return jnp.einsum('bsi,ih->bsh', h_sparse, w_down)
    x = L0_attn_x
    mod = (_silu(L0_c) @ L0_wmod).reshape(L0_c.shape[0], 6, 1, -1)
    sa, ca, ga, sb, cb, gb = (mod[:, 0], mod[:, 1], mod[:, 2], mod[:, 3], mod[:, 4], mod[:, 5])
    ga = (2 * (ga >= 0) - 1) * jnp.maximum(jnp.abs(ga), 0.25)
    gb = (2 * (gb >= 0) - 1) * jnp.maximum(jnp.abs(gb), 0.25)
    h = _layernorm(x, axis=-1) * (1 + ca) + sa
    x = x + ga * _L0_attn_ref(h, L0_attn_W_qkv, L0_attn_W_z, L0_attn_W_b, L0_attn_W_a, L0_attn_conv_w, L0_attn_dt_bias, L0_attn_A_log, L0_attn_norm_w, L0_attn_W_out)
    h = _layernorm(x, axis=-1) * (1 + cb) + sb
    x = x + gb * _L0_ffn_ref(h, L0_ffn_w_gate, L0_ffn_w_up, L0_ffn_w_down)
    return x

_drawn_inputs = setup_inputs


def setup_inputs(seed=0):
    import zlib

    import numpy as np

    out = dict(_drawn_inputs(seed))
    spreads = {'L0_attn_dt_bias': (0.0, 0.8), 'L0_attn_A_log': (0.0, 0.8), 'L0_attn_norm_w': (1.0, 0.539)}
    factors = {}
    for name, (base, spread) in spreads.items():
        noise = np.random.default_rng([zlib.crc32(name.encode()), seed]).standard_normal(out[name].shape)
        drawn = base * np.exp(spread * noise) if base else spread * noise
        out[name] = jnp.asarray(drawn.astype(out[name].dtype))
    for name, factor in factors.items():
        out[name] = (out[name] * factor).astype(out[name].dtype)
    return out
```

```python
from contextlib import ExitStack

import concourse.bass as bass
from concourse import mybir

ALU = mybir.AluOpType
ACT = mybir.ActivationFunctionType
AXX = mybir.AxisListType.X
F32 = mybir.dt.float32
F16 = mybir.dt.float16

P = 128
B, T, C = 8, 256, 256
NK, PV = 16, 2
NV = NK * PV
TAPS = 4
FF = 1024
CK = C // P
BG = 2
NB = B // BG
TL = BG * T // P
CH = T // P
TOK = BG * T
U = TL * PV
GU = CH * PV
QKV_BLK = 4
LEVELS = (2, 4, 8, 16, 32, 64)
NEG = -30000.0
EPS_LN, EPS_RMS, EPS_K2 = 1e-5, 1e-6, 1e-24
GUARD = 0.25
BETA, GLOG, EG, NEGP, BSUF, KINDS = 0, 1, 2, 3, 4, 5


def adaln_deltanet_ffn(nc, x, wqkv, wz, wout, nw, wba, dtb, alog, wgate, wup, wdown, cT, wmod, out):
    with ExitStack() as ctx:
        def sb(name, shape, dt=F32):
            return ctx.enter_context(nc.sbuf_tensor(name, shape, dt))

        def sem(name):
            return ctx.enter_context(nc.semaphore(name))

        bank = [ctx.enter_context(nc.psum_tensor(f"bank{i}", [P, 512], F32)) for i in range(8)]
        bank_y = bank[0:2]
        bank_p = bank[2:4]
        bank_a = (bank[4], bank[6])
        bank_b = (bank[5], bank[7])

        ident = sb("ident", [P, P])
        ident16 = sb("ident16", [P, P], F16)
        twoI = sb("twoI", [P, P])
        le = sb("le", [P, P])
        lt = sb("lt", [P, P])
        gt = sb("gt", [P, P])
        neg16 = sb("neg16", [P, P], F16)
        ones = sb("ones", [P, P])
        zero16 = sb("zero16", [P, 512], F16)
        mhalf = sb("mhalf", [P, 16])
        eps = sb("eps", [P, 2, 8])
        blockrows = sb("blockrows", [P, 6, P], F16)
        same = sb("same", [P, 8, P], F16)
        mask = sb("mask", [P, 7, P], F16)
        maskT1 = sb("maskT1", [P, P], F16)
        wg_sb = sb("wg_sb", [P, CK, FF])
        wu_sb = sb("wu_sb", [P, CK, FF])
        wd_sb = sb("wd_sb", [P, FF // P, C])
        wba_sb = sb("wba_sb", [P, CK, 2 * NV])
        wmod_sb = sb("wmod_sb", [P, CK, 6 * C])
        nw_sb = sb("nw_sb", [P, 1])
        rows = sb("rows", [1, 2 * NV])
        dtb_b = sb("dtb_b", [P, NV])
        expA = sb("expA", [P, NV])
        cT_sb = sb("cT_sb", [P, CK, B])
        c_th = sb("c_th", [P, CK, B])
        silu_c = sb("silu_c", [P, CK, B])
        silu_cb = sb("silu_cb", [P, CK, B, P])
        modT = sb("modT", [P, CK * 6, B])
        gates = sb("gates", [P, B, 2, C])
        xs = sb("xs", [P, TL, C])
        x2 = sb("x2", [P, TL, C])
        stats = sb("stats", [P, TL, 6])
        mv = sb("mv", [P, TL, 2])
        ve = sb("ve", [P, TL])
        rstd = sb("rstd", [P, TL])
        xn = sb("xn", [P, TL, C])
        modc = sb("modc", [P, CK * 6, BG])
        hT = sb("hT", [P, CK, TOK])
        ba = sb("ba", [P, TL, 2 * NV])
        ba_t = sb("ba_t", [P, 4, TL, NV])
        cols = sb("cols", [P, KINDS, TL, NV])
        NQ = QKV_BLK * P
        wq_sb = sb("wq_sb", [P, CK * NQ + QKV_BLK * TAPS])
        wz_sb = sb("wz_sb", [P, CK, PV * P])
        wo_sb = sb("wo_sb", [P, PV, C])
        wo_n = sb("wo_n", [P, PV, C])
        wconv = wq_sb[:, CK * NQ:].rearrange("p (b j) -> p b j", j=TAPS)
        cg = sb("cg", [P, 2, TL, PV])
        g_le = sb("g_le", [P, U, P])
        e_raw = sb("e_raw", [P, U, P])
        e_b = sb("e_b", [P, U, P + 1])
        cc = sb("cc", [P, QKV_BLK, BG, T])
        sq = sb("sq", [P, 2, TOK])
        ck = sb("ck", [P, KINDS, TL, PV])
        n2 = sb("n2", [P, 2 * TL])
        rn = sb("rn", [P, 2 * TL])
        kn = sb("kn", [P, TL, P])
        knT = sb("knT", [P, TOK])
        qT = sb("qT", [P, TOK])
        v = sb("v", [P, TL, PV, P])
        at = sb("at", [P, U, P])
        pt = sb("pt", [P, U, P])
        a_hi = sb("a_hi", [P, U, P], F16)
        a_lo = sb("a_lo", [P, U, P], F16)
        f_hi = sb("f_hi", [P, U, P], F16)
        inv = sb("inv", [P, U, P], F16)
        invT = sb("invT", [P, U, P], F16)
        ym = sb("ym", [P, U, P], F16)
        tt = sb("tt", [P, U, P])
        u0 = sb("u0", [P, BG, PV, P])
        us = sb("us", [P, BG, PV, P])
        st = sb("st", [P, BG, PV * P])
        rr = sb("rr", [P, BG, PV, P])
        u1 = sb("u1", [P, BG, PV, P])
        qs = sb("qs", [P, BG, PV, P])
        o = sb("o", [P, TL, PV, P])
        oss = sb("oss", [P, TL, PV])
        osc = sb("osc", [P, 4, TL, PV])
        zth = sb("zth", [P, TL, PV * P])
        zg = sb("zg", [P, TL, PV, P])
        go = sb("go", [P, TL, PV, P])
        goT = sb("goT", [P, U, P])
        osq = goT
        g_sign = zth[:, 0:2].rearrange("p t d -> p (t d)")
        g_abs = zth[:, 2:4].rearrange("p t d -> p (t d)")
        g_sb = go[:, 0:2].rearrange("p t v d -> p (t v d)")
        f_th = at[:].rearrange("p u s -> p (u s)")
        f_h = tt[:].rearrange("p u s -> p (u s)")
        f_a = pt[:].rearrange("p u s -> p (u s)")
        f_s = go[:].rearrange("p t v d -> p (t v d)")
        f_sT = v[:].rearrange("p t v d -> p (t v) d")
        f_c1 = sb("f_c1", [P, FF // 4, 3], F16)
        f_c2 = sb("f_c2", [P, FF // 4, 2], F16)
        f_c3 = sb("f_c3", [P, FF // 4], F16)
        f_w = sb("f_w", [P, 2, 4, FF // 4], F16)
        yo = sb("yo", [P, C])

        S = {}

        FREE = ("a_ready", "ahi_ready", "alo_ready", "ck_ready", "conv_step", "decay_beta", "decay_ps",
            "down_ps", "f_h_ready", "f_ready", "f_sT_ps", "f_silu", "goT_ready", "go_ready",
            "hT_ready", "h_ps", "kt_ps", "o0_ps", "o0_ready", "o1_ps", "o1_ready",
            "osc_ready", "osq_ready", "out_dma", "pt_ready", "q_copied", "qs_ps", "qs_ready",
            "r_ready", "rn_ready", "s_ps", "sq_ready", "ss_ps", "t_ps", "u0_ps",
            "u1_ps", "us_ready", "vt_ps", "wo_ready", "x2_ready", "xnT_ps", "y_sum",
            "yo_mul", "yo_ready", "z_gate", "z_ps")

        def sig(name):
            if name not in S:
                S[name] = sem(name)
            return S[name]

        x_t = x.rearrange("(n t p) c -> n p t c", p=P, t=TL)
        out_t = out.rearrange("(n t p) c -> n t p c", p=P, t=TL)

        def units(tensor, g):
            return tensor[:, GU * g:GU * g + GU, :]

        def grid(ap):
            return ap.rearrange("p (u s) -> p u s", s=P)

        block = ctx.enter_context(nc.Block())

        @block.sync
        def _(sp):
            sp.dma_start(cT_sb[:], cT).then_inc(sig("setup_dma"), 16)
            sp.dma_start(wmod_sb[:], wmod).then_inc(sig("setup_dma"), 16)
            sp.dma_start(rows[0:1, 0:NV], dtb).then_inc(sig("setup_dma"), 16)
            sp.dma_start(rows[0:1, NV:2 * NV], alog).then_inc(sig("setup_dma"), 16)
            sp.dma_start(nw_sb[:], nw).then_inc(sig("setup_dma"), 16)
            sp.dma_start(wba_sb[:], wba).then_inc(sig("setup_dma"), 16)
            with sp.Fori(0, NB) as bp:
                sp.wait_ge(sig("x2_ready"), bp * TL + 1)
                sp.dma_start(xs[:], x_t[bass.ds(bp, 1)].rearrange("a p t c -> p (a t) c")).then_inc(sig("x_dma"), 16)

                def load_qkv(j, kh):
                    sp.wait_ge(sig("conv_step"), j * 12 + 1)
                    src = wqkv[kh] if isinstance(kh, int) else wqkv[bass.ds(kh, 1)].rearrange("a p n -> p (a n)")
                    sp.dma_start(wq_sb[:], src).then_inc(sig("wq_dma"), 16)

                def load_zo(j, kh):
                    sp.wait_ge(sig("z_ps"), j * 2 + 1)
                    s1 = wz[kh] if isinstance(kh, int) else wz[bass.ds(kh, 1)].rearrange("a p k n -> p (a k) n")
                    sp.dma_start(wz_sb[:], s1).then_inc(sig("wz_dma"), 16)
                    sp.wait_ge(sig("wo_ready"), j + 1)
                    s2 = wout[kh] if isinstance(kh, int) else wout[bass.ds(kh, 1)].rearrange("a p k n -> p (a k) n")
                    sp.dma_start(wo_sb[:], s2).then_inc(sig("wo_dma"), 16)

                load_qkv(bp * NK, 0)
                with sp.Fori(0, NK - 1) as kh:
                    load_qkv(bp * NK + kh + 1, kh + 1)
                    load_zo(bp * NK + kh, kh)
                load_zo(bp * NK + (NK - 1), NK - 1)

        @block.gpsimd
        def _(pool):
            gp = nc.gpsimd
            for name in FREE:
                pool.sem_inc(sig(name), 1)
            cst = sig("pool_const")
            n = [0]

            def done(ins):
                n[0] += 1
                ins.then_inc(cst, 1)
                pool.wait_ge(cst, n[0])

            done(gp.memset(ones[:], 1.0))
            gp.memset(mhalf[:], -0.5).then_inc(cst, 1)
            gp.memset(eps[:, 0], EPS_LN).then_inc(cst, 1)
            gp.memset(eps[:, 1], P * EPS_RMS).then_inc(cst, 1)
            gp.memset(twoI[:], 2.0).then_inc(cst, 1)
            gp.memset(zero16[:], 0.0).then_inc(cst, 1)
            gp.memset(e_b[:], 0.0).then_inc(cst, 1)
            gp.memset(blockrows[:], 1.0).then_inc(cst, 1)
            n[0] += 7
            pool.wait_ge(cst, n[0])
            gp.affine_select(out=ident[:], in_=ones[:], compare_op=ALU.is_equal, fill=0.0, base=0,
                             pattern=[[-1, P]], channel_multiplier=1).then_inc(cst, 1)
            gp.affine_select(out=ident16[:], in_=ones[:], compare_op=ALU.is_equal, fill=0.0, base=0,
                             pattern=[[-1, P]], channel_multiplier=1).then_inc(cst, 1)
            gp.affine_select(out=twoI[:], in_=twoI[:], compare_op=ALU.is_equal, fill=0.0, base=0,
                             pattern=[[-1, P]], channel_multiplier=1).then_inc(cst, 1)
            gp.affine_select(out=le[:], in_=ones[:], compare_op=ALU.is_ge, fill=0.0, base=0,
                             pattern=[[1, P]], channel_multiplier=-1).then_inc(cst, 1)
            gp.affine_select(out=lt[:], in_=ones[:], compare_op=ALU.is_gt, fill=0.0, base=0,
                             pattern=[[1, P]], channel_multiplier=-1).then_inc(cst, 1)
            gp.affine_select(out=gt[:], in_=ones[:], compare_op=ALU.is_gt, fill=0.0, base=0,
                             pattern=[[-1, P]], channel_multiplier=1).then_inc(cst, 1)
            gp.affine_select(out=neg16[:], in_=zero16[:, 0:P], compare_op=ALU.is_ge, fill=NEG, base=0,
                             pattern=[[1, P]], channel_multiplier=-1).then_inc(cst, 1)
            n[0] += 7
            pool.wait_ge(cst, n[0])
            for i, size in enumerate(LEVELS):
                done(gp.affine_select(out=blockrows[:, i, :], in_=blockrows[:, i, :], compare_op=ALU.is_ge, fill=0.0,
                                      base=0, pattern=[[1, P]], channel_multiplier=-size))
                ins = gp.affine_select(out=blockrows[:, i, :], in_=blockrows[:, i, :], compare_op=ALU.is_ge, fill=0.0,
                                       base=size - 1, pattern=[[-1, P]], channel_multiplier=size)
                ins.then_inc(sig("blockrows_ready"), 1)
            pool.wait_ge(sig("blockrows_ready"), len(LEVELS))
            gp.tensor_copy(same[:, 0, :], ident16[:]).then_inc(sig("same_ends"), 1)
            gp.tensor_copy(same[:, 7, :], ones[:]).then_inc(sig("same_ends"), 1)
            pool.wait_ge(sig("mask_diff"), 7)
            for i in range(7):
                gp.affine_select(out=mask[:, i, :], in_=mask[:, i, :], compare_op=ALU.is_ge, fill=0.0, base=0,
                                 pattern=[[-1, P]], channel_multiplier=1).then_inc(sig("mask_low"), 1)
            gp.affine_select(out=maskT1[:], in_=same[:, 1, :], compare_op=ALU.is_ge, fill=0.0, base=0,
                             pattern=[[1, P]], channel_multiplier=-1).then_inc(sig("mask_low"), 1)

            def layernorm_rstd(n):
                pool.wait_ge(sig("ln_aggr"), n * TL + TL)
                gp.tensor_tensor(ve[:], mv[:, :, 1], eps[:, 0, 0:TL], ALU.add).then_inc(sig("ln_eps"), 1)
                pool.wait_ge(sig("ln_eps"), n + 1)
                gp.tensor_tensor(rstd[:], ve[:], mhalf[:, 0:TL], ALU.pow).then_inc(sig("ln_rstd"), 1)

            def decay_and_squares(J):
                for g in range(BG):
                    pool.wait_ge(sig("decay_exp"), J * 2 + g + 1)
                    pool.wait_ge(sig("a_ready"), J * 2 + 1)
                    pool.wait_ge(sig("pt_ready"), J * 2 + 1)
                    gp.tensor_tensor(units(e_b, g)[:, :, 1:P + 1], units(e_raw, g),
                                     cg[:, 0].rearrange("p t v -> p (t v)")[:, GU * g:GU * g + GU].unsqueeze(2)
                                     .broadcast_to([P, GU, P]), ALU.mult).then_inc(sig("decay_beta"), 1)
                pool.wait_ge(sig("conv_step"), J * 12 + 6 + 1)
                pool.wait_ge(sig("ss_ps"), J + 1)
                kq = cc[:, 0:2].rearrange("p b g t -> p b (g t)")
                gp.tensor_tensor(sq[:], kq, kq, ALU.mult).then_inc(sig("sq_ready"), 1)

            def head(j, J):
                pool.wait_ge(sig("ss_max"), j + 1)
                pool.wait_ge(sig("osc_ready"), j * 5 + 1)
                pool.wait_ge(sig("qs_ps"), j * 2 + 1)
                pool.wait_ge(sig("conv_step"), j * 12 + 6 + 1)
                gp.tensor_tensor(rn[:], n2[:], mhalf[:, 0:2 * TL], ALU.pow).then_inc(sig("rn_ready"), 1)
                gp.tensor_copy(qT[:], cc[:, 1].rearrange("p g t -> p (g t)")).then_inc(sig("q_copied"), 1)
                if J is not None:
                    decay_and_squares(J)
                pool.wait_ge(sig("oss_ready"), j * 2 + 2)
                pool.wait_ge(sig("go_ready"), j * 8 + 1)
                qn = rn[:, TL:2 * TL].unsqueeze(2).broadcast_to([P, TL, PV])
                cnt = sig("osc_ready")
                gp.tensor_tensor(osc[:, 0], oss[:], qn, ALU.mult).then_inc(cnt, 1)
                pool.wait_ge(sig("osc_ready"), j * 5 + 1 + 1)
                gp.tensor_tensor(osc[:, 1], osc[:, 0], qn, ALU.mult).then_inc(cnt, 1)
                pool.wait_ge(sig("osc_ready"), j * 5 + 2 + 1)
                gp.tensor_tensor(osc[:, 2], osc[:, 1], eps[:, 1, 0:U].rearrange("p (t v) -> p t v", v=PV), ALU.add).then_inc(cnt, 1)
                pool.wait_ge(sig("osc_ready"), j * 5 + 3 + 1)
                gp.tensor_tensor(osc[:, 0], osc[:, 2], mhalf[:, 0:U].rearrange("p (t v) -> p t v", v=PV),
                                 ALU.pow).then_inc(cnt, 1)
                pool.wait_ge(sig("osc_ready"), j * 5 + 4 + 1)
                gp.tensor_tensor(osc[:, 3], osc[:, 0], qn, ALU.mult).then_inc(cnt, 1)

            with pool.Fori(0, NB) as bp:
                layernorm_rstd(bp * 2)
                decay_and_squares(bp * NK)
                with pool.Fori(bp * NK, bp * NK + NK - 1) as j:
                    head(j, j + 1)
                head(bp * NK + (NK - 1), None)
                layernorm_rstd(bp * 2 + 1)

        @block.tensor
        def _(pe):
            mm = nc.tensor.matmul

            def m(o_, l_, r_, start=True, stop=True):
                return mm(o_, l_, r_, start=start, stop=stop, skip_group_check=True)

            pe.wait_ge(sig("blockrows_ready"), len(LEVELS))
            for i in range(len(LEVELS)):
                ins = m(bank[i // 4][:, P * (i % 4):P * (i % 4) + P], blockrows[:, i, :], blockrows[:, i, :])
            ins.then_inc(sig("same_ps"), 1)
            pe.wait_ge(sig("setup_dma"), 96)
            m(bank[2][:, 0:2 * NV], ones[0:1, :], rows[:]).then_inc(sig("rows_ps"), 1)
            pe.wait_ge(sig("silu_c"), 3)
            for i in range(6):
                for k in range(CK):
                    for kk in range(CK):
                        ins = m(bank[3][:, (k * 6 + i) * B:(k * 6 + i + 1) * B],
                                wmod_sb[:, kk, i * C + k * P:i * C + k * P + P], silu_c[:, kk, :],
                                start=(kk == 0), stop=(kk == CK - 1))
            ins.then_inc(sig("mod_ps"), 1)
            for b in range(B):
                if b >= 2:
                    pe.wait_ge(sig("gates_ready"), 2 * (b - 1))
                for h, i in enumerate((2, 5)):
                    for kk in range(CK):
                        ins = m(bank[4 + b % 2][:, h * C:h * C + C], silu_cb[:, kk, b, :],
                                wmod_sb[:, kk, i * C:i * C + C], start=(kk == 0), stop=(kk == CK - 1))
                ins.then_inc(sig("gates_ps"), 1)

            def transpose_h(n):
                pe.wait_ge(sig("xn_ready"), n * TL + TL)
                for k in range(CK):
                    for t in range(TL):
                        ins = nc.tensor.transpose(bank_p[k][:, t * P:t * P + P], xn[:, t, k * P:k * P + P], ident[:])
                    ins.then_inc(sig("xnT_ps"), 1)

            def beta_decay(bp):
                pe.wait_ge(sig("hT_ready"), bp * 8 + 4 + 1)
                for t in range(TL):
                    for k in range(CK):
                        ins = m(bank[4][:, t * 2 * NV:(t + 1) * 2 * NV], hT[:, k, t * P:t * P + P], wba_sb[:, k, :],
                                start=(k == 0), stop=(k == CK - 1))
                ins.then_inc(sig("ba_ps"), 1)
                pe.wait_ge(sig("g_ready"), bp + 1)
                gl = cols[:, GLOG].rearrange("p t h -> p (t h)")
                m(bank[5][:, 0:P], le[:], gl)
                m(bank[5][:, P:2 * P], lt[:], gl)
                m(bank[5][:, 2 * P:3 * P], gt[:], gl).then_inc(sig("cum_ps"), 1)
                for g in range(BG):
                    ins = m(bank_y[g][:], zero16[:, 0:P], zero16[:])

            def decay(J, zprev):
                for g in range(BG):
                    if zprev is not None:
                        pe.wait_ge(sig("z_gate"), zprev * 2 + 1)
                        pe.wait_ge(sig("o0_ready"), zprev * 2 + 1)
                    pe.wait_ge(sig("g_le_ready"), J * 2 + g + 1)
                    rhs = units(g_le, g).rearrange("p u s -> p (u s)")
                    m(bank_p[g][:], gt[:], rhs, stop=False)
                    m(grid(bank_p[g][:]), ident16[:], neg16[:].unsqueeze(1).broadcast_to([P, GU, P]),
                      start=False).then_inc(sig("decay_ps"), 1)

            def project(J, i):
                if i == 0:
                    pe.wait_ge(sig("wq_dma"), J * 16 + 16)
                if i < 2:
                    pe.wait_ge(sig("decay_exp"), J * 2 + i + 1)
                else:
                    pe.wait_ge(sig("conv_step"), J * 12 + 3 * (i - 1) + 1)
                for k in range(CK):
                    ins = m(bank_p[i % 2][:], wq_sb[:, k * NQ + i * P:k * NQ + i * P + P], hT[:, k, :],
                            start=(k == 0), stop=(k == CK - 1))
                ins.then_inc(sig("proj_ps"), 1)

            def z_part(j, J, i):
                if i == 0:
                    pe.wait_ge(sig("wz_dma"), j * 16 + 16)
                pe.wait_ge(sig("conv_step"), (J if J is not None else j) * 12 + (9 if i == 0 else 12) + 1)
                for c in range(2):
                    t = 2 * i + c
                    for k in range(CK):
                        ins = m(bank_p[i][:, c * 256:c * 256 + 256], hT[:, k, t * P:t * P + P], wz_sb[:, k, :],
                                start=(k == 0), stop=(k == CK - 1))
                ins.then_inc(sig("z_ps"), 1)

            def head(j, J):
                pe.wait_ge(sig("qs_ready"), j * 4 + 1)
                pe.wait_ge(sig("sq_ready"), j + 1 + 1)
                for b in range(2):
                    for t in range(TL):
                        ins = m(bank_b[0][:, b * TL + t:b * TL + t + 1], sq[:, b, t * P:t * P + P], ones[:, 0:1])
                ins.then_inc(sig("ss_ps"), 1)
                pe.wait_ge(sig("conv_step"), j * 12 + 12 + 1)
                pe.wait_ge(sig("goT_ready"), j * 2 + 1)
                ccf = cc[:].rearrange("p b g t -> p b (g t)")
                for t in range(TL):
                    ins = nc.tensor.transpose(bank_a[0][:, t * P:t * P + P], ccf[:, 0, t * P:t * P + P], ident[:])
                ins.then_inc(sig("kt_ps"), 1)
                for p_, bk in enumerate((bank_a[1], bank_b[1])):
                    for t in range(TL):
                        ins = nc.tensor.transpose(bk[:, t * P:t * P + P], ccf[:, 2 + p_, t * P:t * P + P], ident[:])
                    ins.then_inc(sig("vt_ps"), 1)
                pe.wait_ge(sig("kn_ready"), j + 1)
                for t in range(TL):
                    ins = nc.tensor.transpose(bank_b[0][:, t * P:t * P + P], kn[:, t, :], ident[:])
                ins.then_inc(sig("knT_ps"), 1)
                pe.wait_ge(sig("knT_ready"), j + 1)
                for t in range(TL):
                    ks_ = knT[:, t * P:t * P + P]
                    ins = m(bank_a[0][:, t * P:t * P + P], ks_, ks_)
                ins.then_inc(sig("kk_ps"), 1)
                pe.wait_ge(sig("q_copied"), j + 1 + 1)
                for t in range(TL):
                    ins = m(bank_b[0][:, t * P:t * P + P], knT[:, t * P:t * P + P], qT[:, t * P:t * P + P])
                ins.then_inc(sig("qk_ps"), 1)

                for g in range(BG):
                    pe.wait_ge(sig("f_ready"), j * 2 + g + 1 + 1)
                    if g == 0:
                        pe.wait_ge(sig("a_ready"), j * 2 + 2 + 1)
                    else:
                        pe.wait_ge(sig("v_ready"), j * 2 + 2)
                    for i in range(GU):
                        ins = m(bank_a[g][:, i * P:i * P + P], units(f_hi, g)[:, i, :], ident16[:])
                    ins.then_inc(sig("f_ps"), 1)
                if J is not None:
                    decay(J, j)
                for l in range(6):
                    for g in range(BG):
                        c0 = j * 12 + 2 * l + g
                        if l == 0:
                            pe.wait_ge(sig("x1_ready"), j * 2 + g + 1)
                        else:
                            pe.wait_ge(sig("x_ready"), c0 - 1)
                        for i in range(GU):
                            ins = m(bank_a[g][:, i * P:i * P + P], units(f_hi, g)[:, i, :], units(inv, g)[:, i, :])
                        ins.then_inc(sig("y_ps"), 1)
                    if J is not None and l < 4:
                        project(J, l)
                    if l == 4:
                        z_part(j, J, 0)
                    if l == 5:
                        z_part(j, J, 1)
                    for g in range(BG):
                        c0 = j * 12 + 2 * l + g
                        if l == 0:
                            pe.wait_ge(sig("xt1_ready"), j * 2 + g + 1)
                            if g == 0:
                                pe.wait_ge(sig("pt_ready"), j * 2 + 2 + 1)
                        else:
                            pe.wait_ge(sig("xt_ready"), c0 - 1)
                        pe.wait_ge(sig("ym_ready"), c0 + 1)
                        for i in range(GU):
                            ins = m(bank_b[g][:, i * P:i * P + P], units(ym, g)[:, i, :], units(invT, g)[:, i, :])
                        ins.then_inc(sig("xt_ps"), 1)
                        for i in range(GU):
                            ins = m(bank_a[g][:, i * P:i * P + P], units(invT, g)[:, i, :], units(ym, g)[:, i, :])
                        ins.then_inc(sig("x_ps"), 1)
                for g in range(BG):
                    pe.wait_ge(sig("x_ready"), j * 12 + 11 + g)
                    for i in range(GU):
                        o_ = bank_a[g][:, i * P:i * P + P]
                        xi = units(inv, g)[:, i, :]
                        m(o_, units(a_hi, g)[:, i, :], xi, stop=False)
                        m(o_, units(a_lo, g)[:, i, :], xi, start=False, stop=False)
                        ins = m(o_, ident16[:], xi, start=False)
                    ins.then_inc(sig("h_ps"), 1)
                for g in range(BG):
                    pe.wait_ge(sig("xt_ready"), j * 12 + 11 + g)
                    pe.wait_ge(sig("h_ready"), j * 2 + g + 1)
                    for i in range(GU):
                        ins = m(bank_b[g][:, i * P:i * P + P], units(ym, g)[:, i, :], units(invT, g)[:, i, :])
                    ins.then_inc(sig("t_ps"), 1)
                for g in range(BG):
                    pe.wait_ge(sig("t_ready"), j * 2 + g + 1)
                    for p_ in range(PV):
                        ins = m(bank_a[g][:, p_ * P:p_ * P + P], tt[:, GU * g + p_, :], v[:, CH * g, p_, :])
                    ins.then_inc(sig("u0_ps"), 1)
                for g in range(BG):
                    pe.wait_ge(sig("u0_ready"), j * 2 + g + 1)
                    pe.wait_ge(sig("z_gate"), j * 2 + 2 + 1)
                    for p_ in range(PV):
                        ins = m(bank_p[g][:, p_ * P:p_ * P + P], pt[:, GU * g + p_, :], u0[:, g, p_, :])
                    ins.then_inc(sig("o0_ps"), 1)
                for g in range(BG):
                    pe.wait_ge(sig("us_ready"), j * 2 + g + 1 + 1)
                    m(bank_a[g][:, 256:512], kn[:, CH * g, :],
                      us[:, g].rearrange("p v d -> p (v d)")).then_inc(sig("s_ps"), 1)
                for g in range(BG):
                    pe.wait_ge(sig("s_ready"), j * 2 + g + 1)
                    t1 = (CH * g + 1) * P
                    m(bank_b[g][:, 0:256], knT[:, t1:t1 + P], st[:, g])
                    m(bank_b[g][:, 256:512], qT[:, t1:t1 + P], st[:, g]).then_inc(sig("qs_ps"), 1)
                for g in range(BG):
                    pe.wait_ge(sig("r_ready"), j * 4 + 2 * g + 2 + 1)
                    for p_ in range(PV):
                        ins = m(bank_a[g][:, 256 + p_ * P:256 + p_ * P + P], tt[:, GU * g + PV + p_, :], rr[:, g, p_, :])
                    ins.then_inc(sig("u1_ps"), 1)
                for g in range(BG):
                    pe.wait_ge(sig("u1_ready"), j * 2 + g + 1)
                    for p_ in range(PV):
                        ins = m(bank_a[g][:, p_ * P:p_ * P + P], pt[:, GU * g + PV + p_, :], u1[:, g, p_, :])
                    ins.then_inc(sig("o1_ps"), 1)
                for g in range(BG):
                    pe.wait_ge(sig("go_ready"), j * 8 + 4 * g + 4 + 1)
                    for i in range(GU):
                        ins = nc.tensor.transpose(bank_a[g][:, i * P:i * P + P], go[:, CH * g + i // PV, i % PV, :],
                                                  ident[:])
                    ins.then_inc(sig("goT_ps"), 1)
                pe.wait_ge(sig("wo_ready"), j + 1 + 1)
                for g in range(BG):
                    pe.wait_ge(sig("goT_ready"), j * 2 + g + 1 + 1)
                    for i in range(GU):
                        c_ = i // PV
                        ins = m(bank_y[g][:, c_ * C:c_ * C + C], goT[:, GU * g + i, :], wo_n[:, i % PV, :],
                                start=False, stop=False)
                ins.then_inc(sig("y_sum"), 1)

            def ffn(bp):
                for t in range(TL):
                    n_ = bp * TL + t
                    if t == 0:
                        pe.wait_ge(sig("hT_ready"), bp * 8 + 8 + 1)
                        pe.wait_ge(sig("ffn_w_dma"), 48)
                    pe.wait_ge(sig("f_h_ready"), n_ * 2 + 1)
                    for w_, bk in ((wg_sb, (bank[2], bank[3])), (wu_sb, (bank[4], bank[5]))):
                        for hf in range(2):
                            for k in range(CK):
                                ins = m(bk[hf][:], hT[:, k, t * P:t * P + P], w_[:, k, hf * 512:hf * 512 + 512],
                                        start=(k == 0), stop=(k == CK - 1))
                    ins.then_inc(sig("gu_ps"), 1)
                    pe.wait_ge(sig("f_s_ready"), n_ * 4 + 4)
                    for hf in range(2):
                        for i in range(4):
                            c_ = (hf * 4 + i) * P
                            ins = nc.tensor.transpose(bank[6 + hf][:, i * P:i * P + P], f_s[:, c_:c_ + P], ident[:])
                        ins.then_inc(sig("f_sT_ps"), 1)
                    pe.wait_ge(sig("f_sT_ready"), n_ * 2 + 2)
                    pe.wait_ge(sig("x2_ready"), bp * TL + TL + 1)
                    pe.wait_ge(sig("yo_mul"), n_ + 1)
                    for i in range(FF // P):
                        ins = m(bank[0][:, 0:C], f_sT[:, i, :], wd_sb[:, i, :], start=(i == 0), stop=(i == FF // P - 1))
                    ins.then_inc(sig("down_ps"), 1)

            with pe.Fori(0, NB) as bp:
                pe.wait_ge(sig("gates_ready"), 2 * B)
                pe.wait_ge(sig("dtb_ready"), 1)
                pe.wait_ge(sig("expA_ready"), 1)
                pe.wait_ge(sig("modT_ready"), 1)
                pe.wait_ge(sig("same_ready"), len(LEVELS))
                pe.wait_ge(sig("f_h_ready"), bp * TL * 2 + 1)
                transpose_h(bp * 2)
                pe.wait_ge(sig("yo_mul"), bp * TL + 1)
                beta_decay(bp)
                decay(bp * NK, None)
                for i in range(4):
                    project(bp * NK, i)
                with pe.Fori(bp * NK, bp * NK + NK - 1) as j:
                    head(j, j + 1)
                head(bp * NK + (NK - 1), None)
                transpose_h(bp * 2 + 1)
                ffn(bp)

        @block.scalar
        def _(act):
            A = nc.scalar.activation

            act.dma_start(wg_sb[:], wgate).then_inc(sig("ffn_w_dma"), 16)
            act.dma_start(wu_sb[:], wup).then_inc(sig("ffn_w_dma"), 16)
            act.dma_start(wd_sb[:], wdown).then_inc(sig("ffn_w_dma"), 16)
            act.wait_ge(sig("setup_dma"), 96)
            A(c_th[:], cT_sb[:], ACT.Tanh, scale=0.5).then_inc(sig("c_tanh"), 1)
            act.wait_ge(sig("rows_ps"), 1)
            A(expA[:], bank[2][:, NV:2 * NV], ACT.Exp).then_inc(sig("expA_ready"), 1)
            A(dtb_b[:], bank[2][:, 0:NV], ACT.Copy).then_inc(sig("dtb_ready"), 1)

            def h_rows(n, which):
                act.wait_ge(sig("modc_ready"), n + 1)
                for k in range(CK):
                    act.wait_ge(sig("xnT_ps"), n * 2 + k + 1 + 1)
                    for g in range(BG):
                        A(hT[:, k, g * T:g * T + T], bank_p[k][:, g * T:g * T + T], ACT.Identity,
                          scale=modc[:, k * 6 + which + 1, g:g + 1],
                          bias=modc[:, k * 6 + which, g:g + 1]).then_inc(sig("hT_ready"), 1)

            def beta_decay(bp):
                act.wait_ge(sig("ba_neg"), bp * 2 + 2)
                A(ba_t[:, 0], ba_t[:, 1], ACT.Exp).then_inc(sig("ba_exp"), 1)
                A(ba_t[:, 2], ba[:, :, 0:NV], ACT.Exp, scale=-1.0).then_inc(sig("ba_exp"), 1)
                act.wait_ge(sig("ba_exp"), bp * 2 + 1)
                A(ba_t[:, 1], ba_t[:, 0], ACT.Ln, bias=1.0).then_inc(sig("ba_ln"), 1)
                act.wait_ge(sig("cum_ps"), bp + 1)
                act.wait_ge(sig("ck_ready"), bp * NK + 1)
                cum = bank[5][:, 0:3 * P].rearrange("p (k t h) -> p k t h", k=3, t=TL)
                A(cols[:, EG:EG + 3], cum, ACT.Exp).then_inc(sig("cum_exp"), 1)

            def decay_exp(J):
                for g in range(BG):
                    act.wait_ge(sig("decay_ps"), J * 2 + g + 1 + 1)
                    act.wait_ge(sig("decay_beta"), J * 2 + 1)
                    A(units(e_raw, g), grid(bank_p[g][:]), ACT.Exp).then_inc(sig("decay_exp"), 1)

            def tap_last(J, i):
                act.wait_ge(sig("proj_ps"), J * 4 + i + 1)
                if i == 0:
                    act.wait_ge(sig("kt_ps"), J + 1)
                    act.wait_ge(sig("sq_ready"), J + 1)
                elif i == 1:
                    act.wait_ge(sig("q_copied"), J + 1)
                else:
                    act.wait_ge(sig("vt_ps"), J * 2 + 1)
                A(cc[:, i].rearrange("p g t -> p (g t)"), bank_p[i % 2][:], ACT.Copy,
                  scale=wconv[:, i, 3:4]).then_inc(sig("tap_last"), 1)

            def z_tanh(j, i):
                act.wait_ge(sig("z_ps"), j * 2 + i + 1 + 1)
                act.wait_ge(sig("z_gate"), j * 2 + 1)
                A(zth[:, 2 * i:2 * i + 2].rearrange("p t d -> p (t d)"), bank_p[i][:], ACT.Tanh,
                  scale=0.5).then_inc(sig("z_tanh"), 1)

            def head(j, J):
                act.wait_ge(sig("u0_ps"), j * 2 + 1)
                act.wait_ge(sig("r_ready"), j * 4 + 1)
                for p_, bk in enumerate((bank_a[1], bank_b[1])):
                    act.wait_ge(sig("vt_ps"), j * 2 + p_ + 1 + 1)
                    A(v[:, :, p_, :], grid(bk[:]), ACT.Copy).then_inc(sig("v_ready"), 1)
                act.wait_ge(sig("knT_ps"), j + 1)
                act.wait_ge(sig("qs_ps"), j * 2 + 1)
                A(knT[:], bank_b[0][:], ACT.Copy).then_inc(sig("knT_ready"), 1)
                for g in range(BG):
                    act.wait_ge(sig("a_ready"), j * 2 + g + 1 + 1)
                    act.wait_ge(sig("h_ps"), j * 2 + 1)
                    act.wait_ge(sig("f_ready"), j * 2 + 1)
                    act.wait_ge(sig("alo_ready"), j * 2 + 1)
                    A(units(a_hi, g), units(at, g), ACT.Copy).then_inc(sig("ahi_ready"), 1)
                if J is not None:
                    decay_exp(J)
                for l in range(6):
                    if J is not None and l < 4:
                        tap_last(J, l)
                    if l >= 4:
                        z_tanh(j, l - 4)
                    for g in range(BG):
                        c0 = j * 12 + 2 * l + g
                        act.wait_ge(sig("x_ps"), c0 + 1)
                        A(units(inv, g), grid(bank_a[g][:]), ACT.Copy).then_inc(sig("x_ready"), 1)
                        A(units(invT, g), grid(bank_b[g][:]), ACT.Copy).then_inc(sig("xt_ready"), 1)
                for g in range(BG):
                    act.wait_ge(sig("t_ps"), j * 2 + g + 1 + 1)
                    act.wait_ge(sig("u1_ps"), j * 2 + 1)
                    A(units(tt, g), grid(bank_b[g][:]), ACT.Copy).then_inc(sig("t_ready"), 1)
                for g in range(BG):
                    act.wait_ge(sig("u0_ps"), j * 2 + g + 1 + 1)
                    act.wait_ge(sig("o0_ps"), j * 2 + 1)
                    A(u0[:, g].rearrange("p v d -> p (v d)"), bank_a[g][:, 0:256], ACT.Copy).then_inc(sig("u0_ready"), 1)
                for g in range(BG):
                    act.wait_ge(sig("s_ps"), j * 2 + g + 1 + 1)
                    act.wait_ge(sig("qs_ps"), j * 2 + 1)
                    A(st[:, g], bank_a[g][:, 256:512], ACT.Copy).then_inc(sig("s_ready"), 1)
                for g in range(BG):
                    act.wait_ge(sig("o0_ps"), j * 2 + g + 1 + 1)
                    act.wait_ge(sig("go_ready"), j * 8 + 1)
                    A(o[:, CH * g].rearrange("p v d -> p (v d)"), bank_p[g][:, 0:256], ACT.Copy).then_inc(sig("o0_ready"), 1)
                for g in range(BG):
                    act.wait_ge(sig("qs_ps"), j * 2 + g + 1 + 1)
                    act.wait_ge(sig("r_ready"), j * 4 + 2 * g + 2 + 1)
                    act.wait_ge(sig("o1_ready"), j * 2 + 1)
                    for p_ in range(PV):
                        A(qs[:, g, p_], bank_b[g][:, 256 + p_ * P:256 + p_ * P + P], ACT.Copy,
                          scale=ck[:, EG, CH * g + 1, p_:p_ + 1]).then_inc(sig("qs_ready"), 1)
                for g in range(BG):
                    act.wait_ge(sig("u1_ps"), j * 2 + g + 1 + 1)
                    act.wait_ge(sig("o1_ps"), j * 2 + 1)
                    A(u1[:, g].rearrange("p v d -> p (v d)"), bank_a[g][:, 256:512], ACT.Copy).then_inc(sig("u1_ready"), 1)
                for g in range(BG):
                    act.wait_ge(sig("o1_ready"), j * 2 + g + 1 + 1)
                    act.wait_ge(sig("o0_ready"), j * 2 + g + 1 + 1)
                    act.wait_ge(sig("y_sum"), j + 1)
                    A(units(osq, g), o[:, CH * g:CH * g + CH].rearrange("p t v d -> p (t v) d"),
                      ACT.Square).then_inc(sig("osq_ready"), 1)
                for g in range(BG):
                    act.wait_ge(sig("goT_ps"), j * 2 + g + 1)
                    act.wait_ge(sig("oss_ready"), j * 2 + g + 1)
                    A(units(goT, g), grid(bank_a[g][:]), ACT.Copy).then_inc(sig("goT_ready"), 1)

            def ffn(bp):
                for t in range(TL):
                    n_ = bp * TL + t
                    act.wait_ge(sig("gu_ps"), n_ + 1)
                    act.wait_ge(sig("f_silu"), n_ * 2 + 1)
                    for hf in range(2):
                        A(f_th[:, hf * 512:hf * 512 + 512], bank[2 + hf][:], ACT.Tanh,
                          scale=0.5).then_inc(sig("f_tanh"), 1)
                    act.wait_ge(sig("down_ps"), n_ + 1)
                    for hf in range(2):
                        act.wait_ge(sig("f_sT_ps"), n_ * 2 + hf + 1 + 1)
                        A(f_sT[:, 4 * hf:4 * hf + 4], grid(bank[6 + hf][:]), ACT.Copy).then_inc(sig("f_sT_ready"), 1)
                    act.wait_ge(sig("yo_ready"), n_ + 1 + 1)
                    act.dma_start(out_t[bass.ds(bp, 1)].rearrange("a t p c -> p (a t) c")[:, t, :],
                                  yo[:]).then_inc(sig("out_dma"), 16)

            with act.Fori(0, NB) as bp:
                h_rows(bp * 2, 0)
                beta_decay(bp)
                decay_exp(bp * NK)
                for i in range(4):
                    tap_last(bp * NK, i)
                with act.Fori(bp * NK, bp * NK + NK - 1) as j:
                    head(j, j + 1)
                head(bp * NK + (NK - 1), None)
                h_rows(bp * 2 + 1, 3)
                ffn(bp)
            act.wait_ge(sig("out_dma"), NB * TL * 16 + 1)

        @block.vector
        def _(dve):
            V = nc.vector

            dve.wait_ge(sig("same_ps"), 1)
            dve.wait_ge(sig("same_ends"), 2)
            for i in range(len(LEVELS)):
                V.tensor_copy(same[:, i + 1, :], bank[i // 4][:, P * (i % 4):P * (i % 4) + P]).then_inc(sig("same_ready"), 1)
            dve.wait_ge(sig("same_ready"), len(LEVELS))
            for i in range(7):
                V.tensor_tensor(mask[:, i, :], same[:, i + 1, :], same[:, i, :], ALU.subtract).then_inc(sig("mask_diff"), 1)
            dve.wait_ge(sig("mask_low"), 8)
            for i in range(7):
                V.tensor_tensor(mask[:, i, :], mask[:, i, :], ident16[:], ALU.add).then_inc(sig("mask_ready"), 1)
            dve.wait_ge(sig("c_tanh"), 1)
            V.tensor_scalar(c_th[:], c_th[:], 1.0, 0.5, ALU.add, ALU.mult).then_inc(sig("silu_c"), 1)
            dve.wait_ge(sig("silu_c"), 1)
            V.tensor_tensor(silu_c[:], c_th[:], cT_sb[:], ALU.mult).then_inc(sig("silu_c"), 1)
            dve.wait_ge(sig("silu_c"), 2)
            V.tensor_copy(silu_cb[:].rearrange("p k b t -> p (k b) t"),
                          silu_c[:].rearrange("p k b -> p (k b)").unsqueeze(2).broadcast_to([P, CK * B, P])).then_inc(sig("silu_c"), 1)
            dve.wait_ge(sig("mod_ps"), 1)
            V.tensor_copy(modT[:], bank[3][:, 0:CK * 6 * B].rearrange("p (m b) -> p m b", b=B)).then_inc(sig("modT_ready"), 1)
            dve.wait_ge(sig("modT_ready"), 1)
            for k in range(CK):
                for i in (1, 4):
                    r = modT[:, k * 6 + i, :]
                    V.tensor_scalar(r, r, 1.0, None, ALU.add).then_inc(sig("modT_ready"), 1)
            for b in range(B):
                dve.wait_ge(sig("gates_ps"), b + 1)
                gp_ = bank[4 + b % 2][:]
                if b >= 1:
                    dve.wait_ge(sig("gates_ready"), 2 * b)
                V.tensor_copy(g_sb, gp_).then_inc(sig("gates_parts"), 1)
                V.tensor_scalar(g_sign, gp_, 0.0, 2.0, ALU.is_ge, ALU.mult).then_inc(sig("gates_parts"), 1)
                dve.wait_ge(sig("gates_parts"), 4 * b + 2)
                V.scalar_tensor_tensor(g_abs, g_sb, -1.0, g_sb, ALU.mult, ALU.max).then_inc(sig("gates_parts"), 1)
                V.tensor_scalar(g_sign, g_sign, -1.0, None, ALU.add).then_inc(sig("gates_parts"), 1)
                dve.wait_ge(sig("gates_parts"), 4 * b + 4)
                V.scalar_tensor_tensor(gates[:, b].rearrange("p h c -> p (h c)"), g_abs, GUARD, g_sign,
                                       ALU.max, ALU.mult).then_inc(sig("gates_ready"), 1)
                dve.wait_ge(sig("gates_ready"), 2 * b + 1)
                V.tensor_scalar(gates[:, b, 1], gates[:, b, 1], 0.5, None, ALU.mult).then_inc(sig("gates_ready"), 1)
            dve.wait_ge(sig("gates_ready"), 2 * B)
            dve.wait_ge(sig("mask_ready"), 7)
            dve.wait_ge(sig("modT_ready"), 5)

            def layernorm(n, src, bp, x2_count):
                if x2_count is None:
                    dve.wait_ge(sig("x_dma"), bp * 16 + 16)
                else:
                    dve.wait_ge(sig("x2_ready"), x2_count + 1)
                for t in range(TL):
                    V.bn_stats(stats[:, t, :], src[:, t, :]).then_inc(sig("ln_stats"), 1)
                dve.wait_ge(sig("ln_stats"), n * TL + TL)
                dve.wait_ge(sig("hT_ready"), n * 4 + 1)
                V.tensor_scalar(modc[:], modT[:, :, bass.ds(bp * BG, BG)], 1.0, None,
                                ALU.mult).then_inc(sig("modc_ready"), 1)
                for t in range(TL):
                    V.bn_aggr(mv[:, t, :], stats[:, t, :]).then_inc(sig("ln_aggr"), 1)
                dve.wait_ge(sig("ln_rstd"), n + 1)
                dve.wait_ge(sig("xnT_ps"), n * 2 + 1)
                for t in range(TL):
                    V.tensor_scalar(xn[:, t, :], src[:, t, :], mv[:, t, 0:1], rstd[:, t:t + 1], ALU.subtract,
                                    ALU.mult).then_inc(sig("xn_ready"), 1)

            def beta_decay(bp):
                dve.wait_ge(sig("ba_ps"), bp + 1)
                V.tensor_copy(ba[:], bank[4][:, 0:TL * 2 * NV].rearrange("p (t h) -> p t h", t=TL)).then_inc(sig("ba_ready"), 1)
                dve.wait_ge(sig("ba_ready"), bp * 2 + 1)
                dve.wait_ge(sig("dtb_ready"), 1)
                dve.wait_ge(sig("expA_ready"), 1)
                av = ba[:, :, NV:2 * NV]
                V.tensor_tensor(av, av, dtb_b[:].unsqueeze(1).broadcast_to([P, TL, NV]), ALU.add).then_inc(sig("ba_ready"), 1)
                dve.wait_ge(sig("ba_ready"), bp * 2 + 2)
                V.scalar_tensor_tensor(ba_t[:, 1], av, -1.0, av, ALU.mult, ALU.min).then_inc(sig("ba_neg"), 1)
                V.tensor_scalar(ba_t[:, 3], av, 0.0, None, ALU.max).then_inc(sig("ba_neg"), 1)
                dve.wait_ge(sig("ba_exp"), bp * 2 + 2)
                V.tensor_scalar(ba_t[:, 2], ba_t[:, 2], 1.0, None, ALU.add).then_inc(sig("ba_one"), 1)
                dve.wait_ge(sig("ba_one"), bp + 1)
                dve.wait_ge(sig("ba_neg"), bp * 2 + 2)
                V.reciprocal(cols[:, BETA], ba_t[:, 2]).then_inc(sig("beta_ready"), 1)
                dve.wait_ge(sig("ba_ln"), bp + 1)
                V.tensor_tensor(ba_t[:, 3], ba_t[:, 3], ba_t[:, 1], ALU.add).then_inc(sig("dt_ready"), 1)
                dve.wait_ge(sig("dt_ready"), bp + 1)
                V.scalar_tensor_tensor(cols[:, GLOG], ba_t[:, 3], -1.0,
                                       expA[:].unsqueeze(1).broadcast_to([P, TL, NV]), ALU.mult,
                                       ALU.mult).then_inc(sig("g_ready"), 1)
                dve.wait_ge(sig("cum_exp"), bp + 1)
                V.tensor_scalar(cols[:, NEGP], cols[:, NEGP], -1.0, None, ALU.mult).then_inc(sig("cols_ready"), 1)
                dve.wait_ge(sig("beta_ready"), bp + 1)
                V.tensor_tensor(cols[:, BSUF], cols[:, BSUF], cols[:, BETA], ALU.mult).then_inc(sig("cols_ready"), 1)
                dve.wait_ge(sig("cols_ready"), bp * 2 + 2)
                dve.wait_ge(sig("g_ready"), bp + 1)

            def decay_rhs(J, kh):
                dve.wait_ge(sig("decay_beta"), J * 2 + 1)
                V.tensor_scalar(cg[:], cols[:, 0:2, :, bass.ds(kh * PV, PV)]
                                if not isinstance(kh, int) else cols[:, 0:2, :, kh * PV:kh * PV + PV], 1.0, None,
                                ALU.mult).then_inc(sig("cg_ready"), 1)
                dve.wait_ge(sig("cg_ready"), J + 1)
                dve.wait_ge(sig("decay_ps"), J * 2 + 1)
                gc = cg[:, 1].rearrange("p t v -> p (t v)")
                for g in range(BG):
                    V.tensor_tensor(units(g_le, g), le[:].unsqueeze(1).broadcast_to([P, GU, P]),
                                    gc[:, GU * g:GU * g + GU].unsqueeze(2).broadcast_to([P, GU, P]),
                                    ALU.mult).then_inc(sig("g_le_ready"), 1)

            def conv(J, i):
                src = bank_p[i % 2][:].rearrange("p (g t) -> p g t", g=BG)
                dve.wait_ge(sig("tap_last"), J * 4 + i + 1)
                for s in range(1, TAPS):
                    if s > 1:
                        dve.wait_ge(sig("conv_step"), J * 12 + 3 * i + s - 1 + 1)
                    V.scalar_tensor_tensor(cc[:, i, :, s:T], src[:, :, 0:T - s], wconv[:, i, 3 - s:4 - s],
                                           cc[:, i, :, s:T], ALU.mult, ALU.add).then_inc(sig("conv_step"), 1)

            def z_gate(j, i):
                dve.wait_ge(sig("z_tanh"), j * 2 + i + 1)
                V.scalar_tensor_tensor(zg[:, 2 * i:2 * i + 2].rearrange("p t v d -> p (t v d)"),
                                       zth[:, 2 * i:2 * i + 2].rearrange("p t d -> p (t d)"), 1.0, bank_p[i][:],
                                       ALU.add, ALU.mult).then_inc(sig("z_gate"), 1)

            def head(j, J, kh):
                dve.wait_ge(sig("qs_ready"), j * 4 + 1)
                dve.wait_ge(sig("us_ready"), j * 2 + 1)
                V.tensor_scalar(ck[:].rearrange("p k t v -> p (k t) v"),
                              (cols[:, :, :, bass.ds(kh * PV, PV)] if not isinstance(kh, int)
                               else cols[:, :, :, kh * PV:kh * PV + PV]).rearrange("p k t v -> p (k t) v"),
                              1.0, None, ALU.mult).then_inc(sig("ck_ready"), 1)
                dve.wait_ge(sig("ss_ps"), j + 1 + 1)
                dve.wait_ge(sig("rn_ready"), j + 1)
                V.tensor_scalar(n2[:], bank_b[0][:, 0:2 * TL], EPS_K2, None, ALU.max).then_inc(sig("ss_max"), 1)
                dve.wait_ge(sig("kt_ps"), j + 1 + 1)
                dve.wait_ge(sig("rn_ready"), j + 1 + 1)
                dve.wait_ge(sig("s_ps"), j * 2 + 1)
                V.tensor_tensor(kn[:], grid(bank_a[0][:]), rn[:, 0:TL].unsqueeze(2).broadcast_to([P, TL, P]),
                                ALU.mult).then_inc(sig("kn_ready"), 1)
                dve.wait_ge(sig("decay_beta"), j * 2 + 2 + 1)
                for g in range(BG):
                    dve.wait_ge(sig("kk_ps"), j + 1)
                    dve.wait_ge(sig("ahi_ready"), j * 2 + 1)
                    V.tensor_tensor(at[:, GU * g:GU * g + GU].rearrange("p (t v) s -> p t v s", v=PV),
                                    units(e_b, g)[:, :, 0:P].rearrange("p (t v) s -> p t v s", v=PV),
                                    grid(bank_a[0][:])[:, CH * g:CH * g + CH].unsqueeze(2).broadcast_to([P, CH, PV, P]),
                                    ALU.mult).then_inc(sig("a_ready"), 1)
                for g in range(BG):
                    dve.wait_ge(sig("ahi_ready"), j * 2 + g + 1 + 1)
                    V.tensor_tensor(units(f_hi, g), ident16[:].unsqueeze(1).broadcast_to([P, GU, P]), units(a_hi, g),
                                    ALU.subtract).then_inc(sig("f_ready"), 1)
                for g in range(BG):
                    dve.wait_ge(sig("qk_ps"), j + 1)
                    dve.wait_ge(sig("o1_ps"), j * 2 + 1)
                    V.tensor_tensor(pt[:, GU * g:GU * g + GU].rearrange("p (t v) s -> p t v s", v=PV),
                                    units(e_b, g)[:, :, 1:P + 1].rearrange("p (t v) s -> p t v s", v=PV),
                                    grid(bank_b[0][:])[:, CH * g:CH * g + CH].unsqueeze(2).broadcast_to([P, CH, PV, P]),
                                    ALU.mult).then_inc(sig("pt_ready"), 1)
                for g in range(BG):
                    dve.wait_ge(sig("f_ready"), j * 2 + g + 1 + 1)
                    dve.wait_ge(sig("t_ps"), j * 2 + 1)
                    V.tensor_tensor(units(invT, g), maskT1[:].unsqueeze(1).broadcast_to([P, GU, P]), units(f_hi, g),
                                    ALU.mult).then_inc(sig("xt1_ready"), 1)
                    dve.wait_ge(sig("f_ps"), j * 2 + g + 1)
                    V.tensor_tensor(units(inv, g), grid(bank_a[g][:]), mask[:, 0, :].unsqueeze(1).broadcast_to([P, GU, P]),
                                    ALU.mult).then_inc(sig("x1_ready"), 1)
                if J is not None:
                    decay_rhs(J, kh + 1)
                for g in range(BG):
                    dve.wait_ge(sig("a_ready"), j * 2 + g + 1 + 1)
                    V.tensor_tensor(units(a_lo, g), units(at, g), units(a_hi, g), ALU.subtract).then_inc(sig("alo_ready"), 1)
                for l in range(6):
                    for g in range(BG):
                        c0 = j * 12 + 2 * l + g
                        dve.wait_ge(sig("y_ps"), c0 + 1)
                        V.tensor_tensor(units(ym, g), grid(bank_a[g][:]),
                                        mask[:, l + 1, :].unsqueeze(1).broadcast_to([P, GU, P]),
                                        ALU.mult).then_inc(sig("ym_ready"), 1)
                    if J is not None and l < 4:
                        conv(J, l)
                    if l >= 4:
                        z_gate(j, l - 4)
                dve.wait_ge(sig("wo_dma"), j * 16 + 16)
                dve.wait_ge(sig("y_sum"), j + 1)
                V.tensor_scalar(wo_n[:], wo_sb[:], nw_sb[:, 0:1], 0.5 * P ** 0.5, ALU.mult, ALU.mult).then_inc(sig("wo_ready"), 1)
                for g in range(BG):
                    dve.wait_ge(sig("h_ps"), j * 2 + g + 1 + 1)
                    V.tensor_tensor(units(ym, g), twoI[:].unsqueeze(1).broadcast_to([P, GU, P]), grid(bank_a[g][:]),
                                    ALU.subtract).then_inc(sig("h_ready"), 1)
                for g in range(BG):
                    dve.wait_ge(sig("u0_ready"), j * 2 + g + 1)
                    V.tensor_tensor(us[:, g], u0[:, g],
                                    ck[:, BSUF, CH * g].unsqueeze(2).broadcast_to([P, PV, P]),
                                    ALU.mult).then_inc(sig("us_ready"), 1)
                for g in range(BG):
                    dve.wait_ge(sig("qs_ps"), j * 2 + g + 1 + 1)
                    for p_ in range(PV):
                        V.scalar_tensor_tensor(rr[:, g, p_], bank_b[g][:, p_ * P:p_ * P + P],
                                               ck[:, NEGP, CH * g + 1, p_:p_ + 1], v[:, CH * g + 1, p_],
                                               ALU.mult, ALU.add).then_inc(sig("r_ready"), 1)
                for g in range(BG):
                    dve.wait_ge(sig("o1_ps"), j * 2 + g + 1 + 1)
                    dve.wait_ge(sig("qs_ready"), j * 4 + 2 * g + 2 + 1)
                    dve.wait_ge(sig("osq_ready"), j * 2 + 1)
                    V.tensor_tensor(o[:, CH * g + 1].rearrange("p v d -> p (v d)"), bank_a[g][:, 0:256],
                                    qs[:, g].rearrange("p v d -> p (v d)"), ALU.add).then_inc(sig("o1_ready"), 1)
                for g in range(BG):
                    dve.wait_ge(sig("osq_ready"), j * 2 + g + 1 + 1)
                    dve.wait_ge(sig("osc_ready"), j * 5 + 1)
                    V.tensor_reduce(oss[:, CH * g:CH * g + CH].rearrange("p t v -> p (t v)"), units(osq, g), AXX,
                                    ALU.add).then_inc(sig("oss_ready"), 1)
                dve.wait_ge(sig("osc_ready"), j * 5 + 5 + 1)
                dve.wait_ge(sig("z_gate"), j * 2 + 2 + 1)
                dve.wait_ge(sig("o1_ready"), j * 2 + 2 + 1)
                for t in range(TL):
                    for p_ in range(PV):
                        V.scalar_tensor_tensor(go[:, t, p_], o[:, t, p_], osc[:, 3, t, p_:p_ + 1], zg[:, t, p_],
                                               ALU.mult, ALU.mult).then_inc(sig("go_ready"), 1)

            def residual(bp):
                for g in range(BG):
                    gx = gates[:, bass.ds(bp * BG + g, 1), 0].rearrange("p a c -> p (a c)")
                    for c_ in range(CH):
                        t = CH * g + c_
                        if t == 0:
                            dve.wait_ge(sig("y_sum"), bp * NK + NK + 1)
                            dve.wait_ge(sig("yo_ready"), bp * TL + 1)
                        V.tensor_tensor(x2[:, t], bank_y[g][:, c_ * C:c_ * C + C], gx, ALU.mult).then_inc(sig("x2_mul"), 1)
                for t in range(TL):
                    dve.wait_ge(sig("x2_mul"), bp * TL + t + 1)
                    V.tensor_tensor(x2[:, t], x2[:, t], xs[:, t], ALU.add).then_inc(sig("x2_ready"), 1)

            def ffn(bp):
                for t in range(TL):
                    n_ = bp * TL + t
                    for hf in range(2):
                        dve.wait_ge(sig("f_tanh"), n_ * 2 + hf + 1)
                        fs = f_th[:, hf * 512:hf * 512 + 512]
                        V.scalar_tensor_tensor(f_a[:, hf * 512:hf * 512 + 512], fs, 1.0, bank[2 + hf][:], ALU.add,
                                               ALU.mult).then_inc(sig("f_silu"), 1)
                    for hf in range(2):
                        dve.wait_ge(sig("f_silu"), n_ * 2 + hf + 1 + 1)
                        V.tensor_tensor(f_h[:, hf * 512:hf * 512 + 512], f_a[:, hf * 512:hf * 512 + 512],
                                        bank[4 + hf][:], ALU.mult).then_inc(sig("f_h_ready"), 1)
                    dve.wait_ge(sig("f_h_ready"), n_ * 2 + 2 + 1)
                    V.scalar_tensor_tensor(f_a, f_h, -1.0, f_h, ALU.mult, ALU.max).then_inc(sig("f_abs"), 1)
                    dve.wait_ge(sig("f_abs"), n_ + 1)
                    a4 = f_a.rearrange("p (n f) -> p n f", f=4)
                    V.tensor_tensor(f_c1[:], a4[:, :, 0:3], a4[:, :, 1:4], ALU.is_ge).then_inc(sig("f_cmp"), 1)
                    V.tensor_tensor(f_c2[:], a4[:, :, 0:2], a4[:, :, 2:4], ALU.is_ge).then_inc(sig("f_cmp"), 1)
                    V.tensor_tensor(f_c3[:], a4[:, :, 0], a4[:, :, 3], ALU.is_ge).then_inc(sig("f_cmp"), 1)
                    dve.wait_ge(sig("f_cmp"), n_ * 3 + 3)
                    c01, c12, c23 = (f_c1[:, :, i] for i in range(3))
                    c02, c13 = (f_c2[:, :, i] for i in range(2))
                    c03 = f_c3[:]
                    w = f_w
                    V.tensor_tensor(w[:, 0, 0], c01, c02, ALU.add).then_inc(sig("f_part"), 1)
                    V.tensor_tensor(w[:, 0, 1], c12, c13, ALU.add).then_inc(sig("f_part"), 1)
                    V.tensor_tensor(w[:, 0, 2], c23, c02, ALU.subtract).then_inc(sig("f_part"), 1)
                    V.tensor_tensor(w[:, 0, 3], c03, c13, ALU.add).then_inc(sig("f_part"), 1)
                    dve.wait_ge(sig("f_part"), n_ * 4 + 4)
                    V.tensor_tensor(w[:, 1, 0], w[:, 0, 0], c03, ALU.add).then_inc(sig("f_wins"), 1)
                    V.tensor_tensor(w[:, 1, 1], w[:, 0, 1], c01, ALU.subtract).then_inc(sig("f_wins"), 1)
                    V.tensor_tensor(w[:, 1, 2], w[:, 0, 2], c12, ALU.subtract).then_inc(sig("f_wins"), 1)
                    V.tensor_tensor(w[:, 1, 3], w[:, 0, 3], c23, ALU.add).then_inc(sig("f_wins"), 1)
                    dve.wait_ge(sig("f_wins"), n_ * 4 + 4)
                    dve.wait_ge(sig("f_sT_ps"), n_ * 2 + 1)
                    h4 = f_h.rearrange("p (n f) -> p n f", f=4)
                    s4 = f_s.rearrange("p (n f) -> p n f", f=4)
                    for i, (op, thr) in enumerate(((ALU.is_ge, 2.0), (ALU.is_ge, 1.0), (ALU.is_ge, 0.0), (ALU.is_le, 1.0))):
                        V.scalar_tensor_tensor(s4[:, :, i], w[:, 1, i], thr, h4[:, :, i], op,
                                               ALU.mult).then_inc(sig("f_s_ready"), 1)
                    dve.wait_ge(sig("down_ps"), n_ + 1 + 1)
                    dve.wait_ge(sig("out_dma"), n_ * 16 + 1)
                    gx = gates[:, bass.ds(bp * BG + t // CH, 1), 1].rearrange("p a c -> p (a c)")
                    V.tensor_tensor(yo[:], bank[0][:, 0:C], gx, ALU.mult).then_inc(sig("yo_mul"), 1)
                    dve.wait_ge(sig("yo_mul"), n_ + 1 + 1)
                    V.tensor_tensor(yo[:], yo[:], x2[:, t], ALU.add).then_inc(sig("yo_ready"), 1)

            with dve.Fori(0, NB) as bp:
                layernorm(bp * 2, xs, bp, None)
                beta_decay(bp)
                decay_rhs(bp * NK, 0)
                for i in range(4):
                    conv(bp * NK, i)
                with dve.Fori(0, NK - 1) as kh:
                    head(bp * NK + kh, bp * NK + kh + 1, kh)
                head(bp * NK + (NK - 1), None, NK - 1)
                residual(bp)
                layernorm(bp * 2 + 1, x2, bp, bp * TL + TL)
                ffn(bp)


_OUT = (B, T, C)


def kernel(**inputs):
    import numpy as np
    import concourse.bacc as bacc
    from concourse.bass_utils import run_bass_kernel_spmd

    a = {k.replace("L0_", ""): np.asarray(v) for k, v in inputs.items()}
    qd = NK * P

    def rows128(w):
        return np.ascontiguousarray(w.reshape(-1, P, w.shape[1]).transpose(1, 0, 2))

    wq = a["attn_W_qkv"]
    heads = []
    for h in range(NK):
        q, k = wq[h * P:(h + 1) * P], wq[qd + h * P:qd + (h + 1) * P]
        vv = wq[2 * qd + h * PV * P:2 * qd + (h + 1) * PV * P]
        cw = a["attn_conv_w"]
        cws = [cw[qd + h * P:qd + (h + 1) * P], cw[h * P:(h + 1) * P],
               cw[2 * qd + h * PV * P:2 * qd + h * PV * P + P], cw[2 * qd + h * PV * P + P:2 * qd + (h + 1) * PV * P]]
        w = rows128(np.concatenate([k, q, vv], 0).T).reshape(P, -1)
        heads.append(np.concatenate([w, np.stack(cws, 1).reshape(P, -1)], 1))
    arrays = {
        "x": a["attn_x"].reshape(B * T, C),
        "wqkv": np.stack(heads),
        "wz": np.stack([rows128(a["attn_W_z"][h * PV * P:(h + 1) * PV * P].T) for h in range(NK)]),
        "wout": np.ascontiguousarray(a["attn_W_out"].T.reshape(NK, PV, P, C).transpose(0, 2, 1, 3)),
        "nw": a["attn_norm_w"].reshape(P, 1),
        "wba": rows128(np.concatenate([a["attn_W_b"], a["attn_W_a"]], 0).T),
        "dtb": a["attn_dt_bias"].reshape(1, NV),
        "alog": a["attn_A_log"].reshape(1, NV),
        "wgate": rows128(a["ffn_w_gate"]),
        "wup": rows128(a["ffn_w_up"]),
        "wdown": rows128(a["ffn_w_down"]),
        "cT": rows128(a["c"].T),
        "wmod": rows128(a["wmod"]),
    }
    arrays = {f"in_{k}": np.ascontiguousarray(v) for k, v in arrays.items()}
    nc = bacc.Bacc("TRN2", target_bir_lowering=False, num_devices=1)
    args = [nc.dram_tensor(k, v.shape, mybir.dt.from_np(v.dtype), kind="ExternalInput").ap() for k, v in arrays.items()]
    args.append(nc.dram_tensor("out_0", (B * T, C), F32, kind="ExternalOutput").ap())
    adaln_deltanet_ffn(nc, *args)
    r = run_bass_kernel_spmd(nc, [arrays], core_ids=[0])
    return r.results[0]["out_0"].reshape(_OUT)
```

```python
from contextlib import ExitStack

import concourse.bass as bass
from concourse import mybir

ALU = mybir.AluOpType
ACT = mybir.ActivationFunctionType
AXX = mybir.AxisListType.X
F32 = mybir.dt.float32
F16 = mybir.dt.float16

P = 128
HP = P // 2
B, T, C = 8, 256, 256
NK, PV = 16, 2
NV = NK * PV
TAPS = 4
FF = 1024
CK = C // P
BG = 2
NB = B // BG
TL = BG * T // P
CH = T // P
TOK = BG * T
U = TL * PV
GU = CH * PV
QKV_BLK = 4
LEVELS = (2, 4, 8, 16, 32, 64)
NEG = -30000.0
EPS_LN, EPS_RMS, EPS_K2 = 1e-5, 1e-6, 1e-24
GUARD = 0.25
BETA, GLOG, EG, NEGP, BSUF, KINDS = 0, 1, 2, 3, 4, 5


def adaln_deltanet_ffn(nc, x, wqkv, wz, wout, nw, wba, dtb, alog, wgate, wup, wdown, cT, wmod, out):
    with ExitStack() as ctx:
        def sb(name, shape, dt=F32):
            return ctx.enter_context(nc.sbuf_tensor(name, shape, dt))

        def sem(name):
            return ctx.enter_context(nc.semaphore(name))

        bank = [ctx.enter_context(nc.psum_tensor(f"bank{i}", [P, 512], F32)) for i in range(8)]
        bank_y = bank[0:2]
        bank_p = bank[2:4]
        bank_a = (bank[4], bank[6])
        bank_b = (bank[5], bank[7])

        ident = sb("ident", [P, P])
        ident16 = sb("ident16", [P, P], F16)
        twoI = sb("twoI", [P, P])
        le = sb("le", [P, P])
        lt = sb("lt", [P, P])
        gt = sb("gt", [P, P])
        neg16 = sb("neg16", [P, P], F16)
        ones = sb("ones", [P, P])
        zero16 = sb("zero16", [P, 512], F16)
        mhalf = sb("mhalf", [P, 16])
        eps = sb("eps", [P, 2, 8])
        blockrows = sb("blockrows", [P, 6, P], F16)
        same = sb("same", [P, 8, P], F16)
        mask = sb("mask", [P, 7, P], F16)
        maskT1 = sb("maskT1", [P, P], F16)
        wg_sb = sb("wg_sb", [P, CK, FF])
        wu_sb = sb("wu_sb", [P, CK, FF])
        wd_sb = sb("wd_sb", [P, FF // P, C])
        wba_sb = sb("wba_sb", [P, CK, 2 * NV])
        wmod_sb = sb("wmod_sb", [P, CK, 6 * C])
        nw_sb = sb("nw_sb", [P, 1])
        rows = sb("rows", [1, 2 * NV])
        dtb_b = sb("dtb_b", [P, NV])
        expA = sb("expA", [P, NV])
        cT_sb = sb("cT_sb", [P, CK, B])
        c_th = sb("c_th", [P, CK, B])
        silu_c = sb("silu_c", [P, CK, B])
        silu_cb = sb("silu_cb", [P, CK, B, P])
        g_le = silu_cb[:, 0]
        e_raw = silu_cb[:, 1]
        modT = sb("modT", [P, CK * 6, B])
        gates = sb("gates", [P, B, 2, C])
        xs = sb("xs", [P, TL, C])
        x2 = sb("x2", [P, TL, C])
        stats = sb("stats", [P, TL, 6])
        mv = sb("mv", [P, TL, 2])
        ve = sb("ve", [P, TL])
        rstd = sb("rstd", [P, TL])
        xn = sb("xn", [P, TL, C])
        modc = sb("modc", [P, CK * 6, BG])
        hT = sb("hT", [P, CK, TOK])
        ba = sb("ba", [P, TL, 2 * NV])
        ba_t = sb("ba_t", [P, 4, TL, NV])
        cols = sb("cols", [P, KINDS, TL, NV])
        NQ = QKV_BLK * P
        wq_sb = sb("wq_sb", [P, CK * NQ + QKV_BLK * TAPS])
        wz_sb = sb("wz_sb", [P, CK, PV * P])
        wo_sb = sb("wo_sb", [P, PV, C])
        wo_n = sb("wo_n", [P, PV, C])
        wconv = wq_sb[:, CK * NQ:].rearrange("p (b j) -> p b j", j=TAPS)
        cg = sb("cg", [P, BG, 2, CH, PV])
        e_b = sb("e_b", [P, U, P + 1])
        cc = sb("cc", [P, QKV_BLK, BG, T])
        sq = sb("sq", [P, BG, 2, T])
        ck = sb("ck", [P, BG, KINDS, CH, PV])
        n2 = sb("n2", [P, BG, 2, CH])
        rn = sb("rn", [P, BG, 2, CH])
        rq = sb("rq", [P, BG, CH])
        kn = sb("kn", [P, BG, CH, P])
        knT = sb("knT", [P, BG, T])
        qT = sb("qT", [P, BG, T])
        v = sb("v", [P, TL, PV, P])
        at = sb("at", [P, U, P])
        pt = sb("pt", [P, U, P])
        a_hi = sb("a_hi", [P, U, P], F16)
        a_lo = sb("a_lo", [P, U, P], F16)
        f_hi = sb("f_hi", [P, U, P], F16)
        inv = sb("inv", [P, U, P], F16)
        invT = sb("invT", [P, U, P], F16)
        ym = sb("ym", [P, U, P], F16)
        yl = sb("yl", [P, len(LEVELS), GU, P], F16)
        tt = sb("tt", [P, U, P])
        u0 = sb("u0", [P, BG, PV, P])
        us = sb("us", [P, BG, PV, P])
        st = sb("st", [P, BG, PV * P])
        rr = sb("rr", [P, BG, PV, P])
        u1 = sb("u1", [P, BG, PV, P])
        qs = sb("qs", [P, BG, PV, P])
        o = sb("o", [P, TL, PV, P])
        oss = sb("oss", [P, BG, CH, PV])
        osc = sb("osc", [P, BG, 4, CH, PV])
        zth = sb("zth", [P, TL, PV * P])
        zg = sb("zg", [P, TL, PV, P])
        go = sb("go", [P, TL, PV, P])
        goT = sb("goT", [P, U, P])
        osq = goT
        g_sign = zth[:, 0:2].rearrange("p t d -> p (t d)")
        g_abs = zth[:, 2:4].rearrange("p t d -> p (t d)")
        g_sb = go[:, 0:2].rearrange("p t v d -> p (t v d)")
        f_th = at[:].rearrange("p u s -> p (u s)")
        f_h = tt[:].rearrange("p u s -> p (u s)")
        f_a = pt[:].rearrange("p u s -> p (u s)")
        f_s = go[:].rearrange("p t v d -> p (t v d)")
        f_sT = v[:].rearrange("p t v d -> p (t v) d")
        f_c1 = sb("f_c1", [P, FF // 4, 3], F16)
        f_c2 = sb("f_c2", [P, FF // 4, 2], F16)
        f_c3 = sb("f_c3", [P, FF // 4], F16)
        f_w = sb("f_w", [P, 2, 4, FF // 4], F16)
        yo = sb("yo", [P, C])

        S = {}

        FREE = ("down_ps", "f_h_ready", "f_sT_ps", "f_sT_ready", "f_silu", "hT_ready",
                "out_dma", "wo_ready", "x2_ready", "xnT_ps", "yo_mul", "yo_ready")
        FREE_G = ("a_ready", "alo_ready", "begin_ps", "ck_ready", "conv_step", "decay_beta",
                "decay_ps", "f_ready", "goT_ps", "goT_ready", "go_ready", "kn_ready",
                "o1_ready", "osc_ready", "osq_ready", "pt_ready", "q_copied", "qs_ready",
                "r_ready", "rn_ready", "solve_ps", "sq_ready", "ss_ps", "us_ready",
                "y_sum", "z_gate", "z_ps")

        def sig(name):
            if name not in S:
                S[name] = sem(name)
            return S[name]

        x_t = x.rearrange("(n t p) c -> n p t c", p=P, t=TL)
        out_t = out.rearrange("(n t p) c -> n t p c", p=P, t=TL)

        def units(tensor, g):
            return tensor[:, GU * g:GU * g + GU, :]

        def grid(ap):
            return ap.rearrange("p (u s) -> p u s", s=P)

        H_PS, T_PS, U0_PS, O0_PS, S_PS, QS_PS, U1_PS, O1_PS = range(1, 9)
        SOLVE_PS = 8
        KT_PS, VT_PS, KNT_PS, KQ_PS, F_PS = range(1, 6)
        BEGIN_PS = 5
        XT1_READY, X1_READY = range(1, 3)
        FIRST_READY = 2
        CG_READY, G_LE_DONE = range(1, 3)
        G_LE_STEPS = 2

        def sg(name, g):
            return sig(f"{name}_{g}")

        block = ctx.enter_context(nc.Block())

        @block.sync
        def _(sp):
            sp.dma_start(cT_sb[:], cT).then_inc(sig("setup_dma"), 16)
            sp.dma_start(wmod_sb[:], wmod).then_inc(sig("setup_dma"), 16)
            sp.dma_start(rows[0:1, 0:NV], dtb).then_inc(sig("setup_dma"), 16)
            sp.dma_start(rows[0:1, NV:2 * NV], alog).then_inc(sig("setup_dma"), 16)
            sp.dma_start(nw_sb[:], nw).then_inc(sig("setup_dma"), 16)
            sp.dma_start(wba_sb[:], wba).then_inc(sig("setup_dma"), 16)
            with sp.Fori(0, NB) as bp:
                sp.wait_ge(sig("x2_ready"), bp * TL + 1)
                sp.dma_start(xs[:], x_t[bass.ds(bp, 1)].rearrange("a p t c -> p (a t) c")).then_inc(sig("x_dma"), 16)

                def load_qkv(j, kh):
                    sp.wait_ge(sg("conv_step", 1), j * 12 + 1)
                    src = wqkv[kh] if isinstance(kh, int) else wqkv[bass.ds(kh, 1)].rearrange("a p n -> p (a n)")
                    sp.dma_start(wq_sb[:], src).then_inc(sig("wq_dma"), 16)

                def load_zo(j, kh):
                    sp.wait_ge(sg("z_ps", 1), j + 1)
                    s1 = wz[kh] if isinstance(kh, int) else wz[bass.ds(kh, 1)].rearrange("a p k n -> p (a k) n")
                    sp.dma_start(wz_sb[:], s1).then_inc(sig("wz_dma"), 16)
                    sp.wait_ge(sig("wo_ready"), j + 1)
                    s2 = wout[kh] if isinstance(kh, int) else wout[bass.ds(kh, 1)].rearrange("a p k n -> p (a k) n")
                    sp.dma_start(wo_sb[:], s2).then_inc(sig("wo_dma"), 16)

                load_qkv(bp * NK, 0)
                with sp.Fori(0, NK - 1) as kh:
                    load_qkv(bp * NK + kh + 1, kh + 1)
                    load_zo(bp * NK + kh, kh)
                load_zo(bp * NK + (NK - 1), NK - 1)

        def left(ap, l):
            return ap.rearrange("p (b h s) -> p b h s", h=2, s=LEVELS[l])[:, :, 0, :]

        def right(ap, l):
            return ap.rearrange("p (b h s) -> p b h s", h=2, s=LEVELS[l])[:, :, 1, :]

        def lefts(ap, l):
            return ap.rearrange("p u (b h s) -> p u b h s", h=2, s=LEVELS[l])[:, :, :, 0, :]

        def rights(ap, l):
            return ap.rearrange("p u (b h s) -> p u b h s", h=2, s=LEVELS[l])[:, :, :, 1, :]

        def halves(bk, l):
            return bk[:, 0:GU * HP].rearrange("p (u b s) -> p u b s", u=GU, s=LEVELS[l])

        SLOTS = 12

        def schedule(eng, bp, start, half, finish):
            start(bp * NK)
            half(0, bp * NK, 0, True, False)
            half(1, bp * NK, 0, True, False)
            with eng.Fori(1, NK - 1) as kh:
                half(0, bp * NK + kh, kh, False, False)
                half(1, bp * NK + kh, kh, False, False)
            half(0, bp * NK + (NK - 1), NK - 1, False, True)
            half(1, bp * NK + (NK - 1), NK - 1, False, True)
            finish(bp * NK + (NK - 1))

        @block.gpsimd
        def _(pool):
            gp = nc.gpsimd
            for name in FREE:
                pool.sem_inc(sig(name), 1)
            for name in FREE_G:
                for g in range(BG):
                    pool.sem_inc(sg(name, g), 1)
            cst = sig("pool_const")
            n = [0]

            def done(ins):
                n[0] += 1
                ins.then_inc(cst, 1)
                pool.wait_ge(cst, n[0])

            done(gp.memset(ones[:], 1.0))
            gp.memset(mhalf[:], -0.5).then_inc(cst, 1)
            gp.memset(eps[:, 0], EPS_LN).then_inc(cst, 1)
            gp.memset(eps[:, 1], P * EPS_RMS).then_inc(cst, 1)
            gp.memset(twoI[:], 2.0).then_inc(cst, 1)
            gp.memset(zero16[:], 0.0).then_inc(cst, 1)
            gp.memset(e_b[:], 0.0).then_inc(cst, 1)
            gp.memset(blockrows[:], 1.0).then_inc(cst, 1)
            n[0] += 7
            pool.wait_ge(cst, n[0])
            gp.affine_select(out=ident[:], in_=ones[:], compare_op=ALU.is_equal, fill=0.0, base=0,
                             pattern=[[-1, P]], channel_multiplier=1).then_inc(cst, 1)
            gp.affine_select(out=ident16[:], in_=ones[:], compare_op=ALU.is_equal, fill=0.0, base=0,
                             pattern=[[-1, P]], channel_multiplier=1).then_inc(cst, 1)
            gp.affine_select(out=twoI[:], in_=twoI[:], compare_op=ALU.is_equal, fill=0.0, base=0,
                             pattern=[[-1, P]], channel_multiplier=1).then_inc(cst, 1)
            gp.affine_select(out=le[:], in_=ones[:], compare_op=ALU.is_ge, fill=0.0, base=0,
                             pattern=[[1, P]], channel_multiplier=-1).then_inc(cst, 1)
            gp.affine_select(out=lt[:], in_=ones[:], compare_op=ALU.is_gt, fill=0.0, base=0,
                             pattern=[[1, P]], channel_multiplier=-1).then_inc(cst, 1)
            gp.affine_select(out=gt[:], in_=ones[:], compare_op=ALU.is_gt, fill=0.0, base=0,
                             pattern=[[-1, P]], channel_multiplier=1).then_inc(cst, 1)
            gp.affine_select(out=neg16[:], in_=zero16[:, 0:P], compare_op=ALU.is_ge, fill=NEG, base=0,
                             pattern=[[1, P]], channel_multiplier=-1).then_inc(cst, 1)
            n[0] += 7
            pool.wait_ge(cst, n[0])
            for i, size in enumerate(LEVELS):
                done(gp.affine_select(out=blockrows[:, i, :], in_=blockrows[:, i, :], compare_op=ALU.is_ge, fill=0.0,
                                      base=0, pattern=[[1, P]], channel_multiplier=-size))
                ins = gp.affine_select(out=blockrows[:, i, :], in_=blockrows[:, i, :], compare_op=ALU.is_ge, fill=0.0,
                                       base=size - 1, pattern=[[-1, P]], channel_multiplier=size)
                ins.then_inc(sig("blockrows_ready"), 1)
            pool.wait_ge(sig("blockrows_ready"), len(LEVELS))
            gp.tensor_copy(same[:, 0, :], ident16[:]).then_inc(sig("same_ends"), 1)
            gp.tensor_copy(same[:, 7, :], ones[:]).then_inc(sig("same_ends"), 1)
            pool.wait_ge(sig("mask_diff"), 7)
            for i in range(7):
                gp.affine_select(out=mask[:, i, :], in_=mask[:, i, :], compare_op=ALU.is_ge, fill=0.0, base=0,
                                 pattern=[[-1, P]], channel_multiplier=1).then_inc(sig("mask_low"), 1)
            gp.affine_select(out=maskT1[:], in_=same[:, 1, :], compare_op=ALU.is_ge, fill=0.0, base=0,
                             pattern=[[1, P]], channel_multiplier=-1).then_inc(sig("mask_low"), 1)

            def layernorm_rstd(n):
                pool.wait_ge(sig("ln_aggr"), n * TL + TL)
                gp.tensor_tensor(ve[:], mv[:, :, 1], eps[:, 0, 0:TL], ALU.add).then_inc(sig("ln_eps"), 1)
                pool.wait_ge(sig("ln_eps"), n + 1)
                gp.tensor_tensor(rstd[:], ve[:], mhalf[:, 0:TL], ALU.pow).then_inc(sig("ln_rstd"), 1)

            def decays(g, J):
                pool.wait_ge(sg("decay_exp", g), J + 1)
                pool.wait_ge(sg("a_ready", g), J + 1)
                pool.wait_ge(sg("pt_ready", g), J + 1)
                gp.tensor_tensor(units(e_b, g)[:, :, 1:P + 1], units(e_raw, g),
                                 cg[:, g, 0].rearrange("p t v -> p (t v)").unsqueeze(2)
                                 .broadcast_to([P, GU, P]), ALU.mult).then_inc(sg("decay_beta", g), 1)

            def decay_rhs(g, J):
                pool.wait_ge(sg("decay_ps", g), J + 1)
                pool.wait_ge(sg("g_le_ready", g), J * G_LE_STEPS + CG_READY)
                gp.tensor_tensor(units(g_le, g), le[:].unsqueeze(1).broadcast_to([P, GU, P]),
                                 cg[:, g, 1].rearrange("p t v -> p (t v)").unsqueeze(2).broadcast_to([P, GU, P]),
                                 ALU.mult).then_inc(sg("g_le_ready", g), 1)

            def low_half(g, J):
                pool.wait_ge(sg("solve_ps", g), J * SOLVE_PS + 1)
                pool.wait_ge(sg("ahi_ready", g), J + 1)
                gp.tensor_tensor(units(a_lo, g), units(at, g), units(a_hi, g), ALU.subtract).then_inc(sg("alo_ready", g), 1)

            def squares(g, J):
                pool.wait_ge(sg("conv_step", g), J * 12 + 6 + 1)
                pool.wait_ge(sg("ss_ps", g), J + 1)
                kq = cc[:, 0:2, g]
                gp.tensor_tensor(sq[:, g], kq, kq, ALU.mult).then_inc(sg("sq_ready", g), 1)

            def keep_rq(g, j):
                pool.wait_ge(sg("rn_ready", g), j + 1 + 1)
                pool.wait_ge(sg("osc_ready", g), j * 6 + 1)
                gp.tensor_tensor(rq[:, g], rn[:, g, 1], ones[:, 0:2], ALU.mult).then_inc(sg("osc_ready", g), 1)

            def norms(g, J, kept):
                pool.wait_ge(sg("osc_ready", g), kept + 1)
                pool.wait_ge(sg("ss_max", g), J + 1)
                pool.wait_ge(sg("kn_ready", g), J + 1)
                gp.tensor_tensor(rn[:, g], n2[:, g], mhalf[:, 0:4].rearrange("p (b t) -> p b t", b=2),
                                 ALU.pow).then_inc(sg("rn_ready", g), 1)

            def output_scale(g, j):
                pool.wait_ge(sg("osc_ready", g), j * 6 + 1 + 1)
                pool.wait_ge(sg("oss_ready", g), j + 1)
                pool.wait_ge(sg("go_ready", g), j * 4 + 1)
                qn = rq[:, g].unsqueeze(2).broadcast_to([P, CH, PV])
                ow = osc[:, g]
                gp.tensor_tensor(ow[:, 0], oss[:, g], qn, ALU.mult).then_inc(sg("osc_ready", g), 1)
                pool.wait_ge(sg("osc_ready", g), j * 6 + 2 + 1)
                gp.tensor_tensor(ow[:, 1], ow[:, 0], qn, ALU.mult).then_inc(sg("osc_ready", g), 1)
                pool.wait_ge(sg("osc_ready", g), j * 6 + 3 + 1)
                gp.tensor_tensor(ow[:, 2], ow[:, 1], eps[:, 1, 0:GU].rearrange("p (t v) -> p t v", v=PV),
                                 ALU.add).then_inc(sg("osc_ready", g), 1)
                pool.wait_ge(sg("osc_ready", g), j * 6 + 4 + 1)
                gp.tensor_tensor(ow[:, 0], ow[:, 2], mhalf[:, 0:GU].rearrange("p (t v) -> p t v", v=PV),
                                 ALU.pow).then_inc(sg("osc_ready", g), 1)
                pool.wait_ge(sg("osc_ready", g), j * 6 + 5 + 1)
                gp.tensor_tensor(ow[:, 3], ow[:, 0], qn, ALU.mult).then_inc(sg("osc_ready", g), 1)

            def start(j):
                decay_rhs(0, j)
                decay_rhs(1, j)
                decays(0, j)
                squares(0, j)
                norms(0, j, j * 6)
                low_half(0, j)
                decays(1, j)
                squares(1, j)

            def half(h, j, kh, first, last):
                g, js = 1 - h, j - 1 + h
                if h == 1 or not first:
                    keep_rq(g, js)
                    if h == 0 or not last:
                        norms(g, js + 1, js * 6 + 1)
                else:
                    norms(g, js + 1, (js + 1) * 6)
                if not last:
                    decay_rhs(h, j + 1)
                    squares(h, j + 1)
                if h == 1 or not first:
                    output_scale(g, js)
                if not last:
                    decays(h, j + 1)
                if h == 0 or not last:
                    low_half(g, js + 1)

            def finish(j):
                keep_rq(1, j)
                output_scale(1, j)

            with pool.Fori(0, NB) as bp:
                layernorm_rstd(bp * 2)
                schedule(pool, bp, start, half, finish)
                layernorm_rstd(bp * 2 + 1)

        @block.tensor
        def _(pe):
            mm = nc.tensor.matmul

            def m(o_, l_, r_, start=True, stop=True):
                return mm(o_, l_, r_, start=start, stop=stop, skip_group_check=True)

            pe.wait_ge(sig("blockrows_ready"), len(LEVELS))
            for i in range(len(LEVELS)):
                ins = m(bank[i // 4][:, P * (i % 4):P * (i % 4) + P], blockrows[:, i, :], blockrows[:, i, :])
            ins.then_inc(sig("same_ps"), 1)
            pe.wait_ge(sig("setup_dma"), 96)
            m(bank[2][:, 0:2 * NV], ones[0:1, :], rows[:]).then_inc(sig("rows_ps"), 1)
            pe.wait_ge(sig("silu_c"), 3)
            for i in range(6):
                for k in range(CK):
                    for kk in range(CK):
                        ins = m(bank[3][:, (k * 6 + i) * B:(k * 6 + i + 1) * B],
                                wmod_sb[:, kk, i * C + k * P:i * C + k * P + P], silu_c[:, kk, :],
                                start=(kk == 0), stop=(kk == CK - 1))
            ins.then_inc(sig("mod_ps"), 1)
            for b in range(B):
                if b >= 2:
                    pe.wait_ge(sig("gates_ready"), 2 * (b - 1))
                for h, i in enumerate((2, 5)):
                    for kk in range(CK):
                        ins = m(bank[4 + b % 2][:, h * C:h * C + C], silu_cb[:, kk, b, :],
                                wmod_sb[:, kk, i * C:i * C + C], start=(kk == 0), stop=(kk == CK - 1))
                ins.then_inc(sig("gates_ps"), 1)

            def transpose_h(n):
                pe.wait_ge(sig("xn_ready"), n * TL + TL)
                for k in range(CK):
                    for t in range(TL):
                        ins = nc.tensor.transpose(bank_p[k][:, t * P:t * P + P], xn[:, t, k * P:k * P + P], ident[:])
                    ins.then_inc(sig("xnT_ps"), 1)

            def beta_decay(bp):
                pe.wait_ge(sig("hT_ready"), bp * 8 + 4 + 1)
                for t in range(TL):
                    for k in range(CK):
                        ins = m(bank[4][:, t * 2 * NV:(t + 1) * 2 * NV], hT[:, k, t * P:t * P + P], wba_sb[:, k, :],
                                start=(k == 0), stop=(k == CK - 1))
                ins.then_inc(sig("ba_ps"), 1)
                pe.wait_ge(sig("g_ready"), bp + 1)
                gl = cols[:, GLOG].rearrange("p t h -> p (t h)")
                m(bank[5][:, 0:P], le[:], gl)
                m(bank[5][:, P:2 * P], lt[:], gl)
                m(bank[5][:, 2 * P:3 * P], gt[:], gl).then_inc(sig("cum_ps"), 1)
                for g in range(BG):
                    ins = m(bank_y[g][:], zero16[:, 0:P], zero16[:])

            def decay_product(g, J):
                pe.wait_ge(sg("g_le_ready", g), J * G_LE_STEPS + G_LE_DONE)
                m(bank_p[1][:], gt[:], units(g_le, g).rearrange("p u s -> p (u s)"), stop=False)
                m(grid(bank_p[1][:]), ident16[:], neg16[:].unsqueeze(1).broadcast_to([P, GU, P]),
                  start=False).then_inc(sg("decay_ps", g), 1)

            def project(i, g, J):
                if i == 0:
                    pe.wait_ge(sig("wq_dma"), J * 16 + 16)
                elif i >= 2:
                    pe.wait_ge(sg("conv_step", g), J * 12 + 3 * (i - 1) + 1)
                for c in range(CK):
                    ins = m(bank_p[1 - i % 2][:, 0:T], wq_sb[:, c * NQ + i * P:c * NQ + i * P + P],
                            hT[:, c, g * T:g * T + T], start=(c == 0), stop=(c == CK - 1))
                ins.then_inc(sg("proj_ps", g), 1)

            def sum_squares(g, J):
                pe.wait_ge(sg("conv_step", g), J * 12 + 12 + 1)
                pe.wait_ge(sg("sq_ready", g), J + 1 + 1)
                for b in range(2):
                    for c in range(CH):
                        ins = m(bank_p[0][:, b * CH + c:b * CH + c + 1], sq[:, g, b, c * P:c * P + P], ones[:, 0:1])
                ins.then_inc(sg("ss_ps", g), 1)

            def z_rows(c, g, j):
                if c == 0:
                    pe.wait_ge(sig("wz_dma"), j * 16 + 16)
                t = CH * g + c
                for k in range(CK):
                    ins = m(bank_p[1][:, c * 256:c * 256 + 256], hT[:, k, t * P:t * P + P], wz_sb[:, k, :],
                            start=(k == 0), stop=(k == CK - 1))
                if c == CH - 1:
                    ins.then_inc(sg("z_ps", g), 1)

            def turn_output(g, j, bk):
                pe.wait_ge(sg("go_ready", g), j * 4 + 4 + 1)
                for i in range(GU):
                    ins = nc.tensor.transpose(bk[:, i * P:i * P + P], go[:, CH * g + i // PV, i % PV, :], ident[:])
                ins.then_inc(sg("goT_ps", g), 1)

            def sum_output(c, g, j):
                if c == 0:
                    pe.wait_ge(sig("wo_ready"), j + 1 + 1)
                    pe.wait_ge(sg("goT_ready", g), j + 1 + 1)
                for p_ in range(PV):
                    ins = m(bank_y[g][:, c * C:c * C + C], goT[:, GU * g + c * PV + p_, :], wo_n[:, p_, :],
                            start=False, stop=False)
                if c == CH - 1:
                    ins.then_inc(sg("y_sum", g), 1)

            def level(s, g, j):
                l = s // 2
                bA, bB = bank_a[g], bank_b[g]
                if s % 2 == 0:
                    if l == 0:
                        pe.wait_ge(sg("first_ready", g), j * FIRST_READY + X1_READY)
                    else:
                        pe.wait_ge(sg("x_ready", g), j * 6 + l)
                    for i in range(GU):
                        ins = m(bA[:, i * HP:i * HP + HP], units(f_hi, g)[:, i, :], left(units(inv, g)[:, i, :], l))
                    ins.then_inc(sg("y_ps", g), 1)
                else:
                    if l == 0:
                        pe.wait_ge(sg("first_ready", g), j * FIRST_READY + XT1_READY)
                        pe.wait_ge(sg("pt_ready", g), j + 1 + 1)
                    else:
                        pe.wait_ge(sg("xt_ready", g), j * 6 + l)
                    pe.wait_ge(sg("ym_ready", g), j * 6 + l + 1)
                    for i in range(GU):
                        ins = m(bA[:, i * HP:i * HP + HP], units(invT, g)[:, i, :], left(yl[:, l, i, :], l))
                    ins.then_inc(sg("level_ps", g), 1)
                    for i in range(GU):
                        ins = m(bB[:, i * HP:i * HP + HP], yl[:, l, i, :], right(units(invT, g)[:, i, :], l))
                    ins.then_inc(sg("level_ps", g), 1)

            def solve(s, g, j):
                bA, bB = bank_a[g], bank_b[g]
                if s == 0:
                    pe.wait_ge(sg("x_ready", g), j * 6 + 6)
                    pe.wait_ge(sg("alo_ready", g), j + 1 + 1)
                    for i in range(GU):
                        o_, xi = bA[:, i * P:i * P + P], units(inv, g)[:, i, :]
                        m(o_, units(a_hi, g)[:, i, :], xi, stop=False)
                        m(o_, units(a_lo, g)[:, i, :], xi, start=False, stop=False)
                        ins = m(o_, ident16[:], xi, start=False)
                    ins.then_inc(sg("solve_ps", g), 1)
                elif s == 1:
                    pe.wait_ge(sg("xt_ready", g), j * 6 + 6)
                    pe.wait_ge(sg("h_ready", g), j + 1)
                    for i in range(GU):
                        ins = m(bB[:, i * P:i * P + P], units(ym, g)[:, i, :], units(invT, g)[:, i, :])
                    ins.then_inc(sg("solve_ps", g), 1)
                elif s == 2:
                    pe.wait_ge(sg("t_ready", g), j + 1)
                    for p_ in range(PV):
                        ins = m(bA[:, p_ * P:p_ * P + P], tt[:, GU * g + p_, :], v[:, CH * g, p_, :])
                    ins.then_inc(sg("solve_ps", g), 1)
                elif s == 3:
                    pe.wait_ge(sg("u0_ready", g), j + 1)
                    for p_ in range(PV):
                        ins = m(bA[:, 256 + p_ * P:256 + p_ * P + P], pt[:, GU * g + p_, :], u0[:, g, p_, :])
                    ins.then_inc(sg("solve_ps", g), 1)
                    pe.wait_ge(sg("us_ready", g), j + 1 + 1)
                    m(bB[:, 0:256], kn[:, g, 0], us[:, g].rearrange("p v d -> p (v d)")).then_inc(sg("solve_ps", g), 1)
                elif s == 4:
                    pe.wait_ge(sg("s_ready", g), j + 1)
                    m(bB[:, 0:256], knT[:, g, P:2 * P], st[:, g])
                    m(bB[:, 256:512], qT[:, g, P:2 * P], st[:, g]).then_inc(sg("solve_ps", g), 1)
                elif s == 5:
                    pe.wait_ge(sg("o0_ready", g), j + 1)
                    pe.wait_ge(sg("r_ready", g), j * 2 + 2 + 1)
                    for p_ in range(PV):
                        ins = m(bA[:, p_ * P:p_ * P + P], tt[:, GU * g + PV + p_, :], rr[:, g, p_, :])
                    ins.then_inc(sg("solve_ps", g), 1)
                elif s == 6:
                    pe.wait_ge(sg("u1_ready", g), j + 1)
                    for p_ in range(PV):
                        ins = m(bA[:, 256 + p_ * P:256 + p_ * P + P], pt[:, GU * g + PV + p_, :], u1[:, g, p_, :])
                    ins.then_inc(sg("solve_ps", g), 1)

            def begin(s, g, j):
                bA, bB = bank_a[g], bank_b[g]
                if s == 7:
                    pe.wait_ge(sg("conv_step", g), j * 12 + 12 + 1)
                    pe.wait_ge(sg("qs_ready", g), j * 2 + 1)
                    for c in range(CH):
                        ins = nc.tensor.transpose(bB[:, c * P:c * P + P], cc[:, 0, g, c * P:c * P + P], ident[:])
                    ins.then_inc(sg("begin_ps", g), 1)
                    pe.wait_ge(sg("o1_ready", g), j + 1)
                    for c in range(CH):
                        for p_ in range(PV):
                            n_ = c * PV + p_
                            ins = nc.tensor.transpose(bA[:, n_ * P:n_ * P + P], cc[:, 2 + p_, g, c * P:c * P + P], ident[:])
                    ins.then_inc(sg("begin_ps", g), 1)
                elif s == 8:
                    pe.wait_ge(sg("kn_ready", g), j + 1 + 1)
                    for c in range(CH):
                        ins = nc.tensor.transpose(bB[:, 256 + c * P:256 + c * P + P], kn[:, g, c], ident[:])
                    ins.then_inc(sg("begin_ps", g), 1)
                elif s == 9:
                    pe.wait_ge(sg("knT_ready", g), j + 1)
                    for c in range(CH):
                        k_ = knT[:, g, c * P:c * P + P]
                        m(bB[:, c * P:c * P + P], k_, k_)
                    pe.wait_ge(sg("q_copied", g), j + 1 + 1)
                    for c in range(CH):
                        ins = m(bB[:, 256 + c * P:256 + c * P + P], knT[:, g, c * P:c * P + P], qT[:, g, c * P:c * P + P])
                    ins.then_inc(sg("begin_ps", g), 1)
                elif s == 10:
                    pe.wait_ge(sg("v_ready", g), j + 1)
                    pe.wait_ge(sg("f_ready", g), j + 1 + 1)
                    for i in range(GU):
                        ins = m(bA[:, i * P:i * P + P], units(f_hi, g)[:, i, :], ident16[:])
                    ins.then_inc(sg("begin_ps", g), 1)

            def prepare(g, j):
                decay_product(g, j)
                pe.wait_ge(sg("decay_exp", g), j + 1)
                for i in range(QKV_BLK):
                    if i == 1 and g == 1:
                        pe.wait_ge(sg("ss_max", 0), j + 1)
                    project(i, g, j)
                sum_squares(g, j)

            def start(j):
                prepare(0, j)
                for s in range(7, 11):
                    begin(s, 0, j)
                prepare(1, j)

            def half(h, j, kh, first, last):
                g, js = 1 - h, j - 1 + h
                for s in range(SLOTS):
                    level(s, h, j)
                    if h == 1 or not first:
                        solve(s, g, js)
                    if h == 0 or not last:
                        begin(s, g, js + 1)
                    if s == 1:
                        if h == 0 and first:
                            pe.wait_ge(sg("conv_step", 1), j * 12 + 12 + 1)
                        else:
                            pe.wait_ge(sg("z_gate", g), js + 1 + 1)
                        if not last:
                            project(0, h, j + 1)
                    if s == 2 and not first:
                        if h == 1 and last:
                            pe.wait_ge(sg("goT_ready", 0), j + 1)
                        else:
                            pe.wait_ge(sg("ss_max", g), js + 2)
                        turn_output(h, j - 1, bank_p[0])
                    if s == 4 and not last:
                        if first:
                            pe.wait_ge(sg("ss_max", g), js + 2)
                        else:
                            pe.wait_ge(sg("goT_ready", h), j + 1)
                        project(1, h, j + 1)
                    if s == 5 and not last:
                        project(2, h, j + 1)
                    if s == 6 and not first:
                        sum_output(0, h, j - 1)
                    if s == 7 and not last:
                        project(3, h, j + 1)
                    if s == 8 and not first:
                        sum_output(1, h, j - 1)
                    if s == 9 and not last:
                        pe.wait_ge(sg("conv_step", h), (j + 1) * 12 + 9 + 1)
                        decay_product(h, j + 1)
                    if s == 10:
                        if not last:
                            sum_squares(h, j + 1)
                            pe.wait_ge(sg("decay_exp", h), j + 2)
                        z_rows(0, h, j)
                    if s == 11:
                        z_rows(1, h, j)

            def finish(j):
                for s in range(SLOTS):
                    solve(s, 1, j)
                    if s == 2:
                        pe.wait_ge(sg("goT_ready", 1), j + 1)
                        turn_output(0, j, bank_p[0])
                    if s == 4:
                        sum_output(0, 0, j)
                        sum_output(1, 0, j)
                pe.wait_ge(sg("goT_ready", 0), j + 1 + 1)
                turn_output(1, j, bank_p[0])
                sum_output(0, 1, j)
                sum_output(1, 1, j)

            def gate_up(bp, t):
                n_ = bp * TL + t
                pe.wait_ge(sig("f_h_ready"), n_ * 2 + 1)
                for w_, bk in ((wg_sb, (bank[2], bank[3])), (wu_sb, (bank[4], bank[5]))):
                    for hf in range(2):
                        for k in range(CK):
                            ins = m(bk[hf][:], hT[:, k, t * P:t * P + P], w_[:, k, hf * 512:hf * 512 + 512],
                                    start=(k == 0), stop=(k == CK - 1))
                ins.then_inc(sig("gu_ps"), 1)

            def down(bp, t):
                n_ = bp * TL + t
                pe.wait_ge(sig("f_s_ready"), n_ * 4 + 4)
                pe.wait_ge(sig("f_sT_ready"), n_ * 2 + 1)
                for hf in range(2):
                    for i in range(4):
                        c_ = (hf * 4 + i) * P
                        ins = nc.tensor.transpose(bank[6 + hf][:, i * P:i * P + P], f_s[:, c_:c_ + P], ident[:])
                    ins.then_inc(sig("f_sT_ps"), 1)
                pe.wait_ge(sig("f_sT_ready"), n_ * 2 + 2 + 1)
                pe.wait_ge(sig("x2_ready"), bp * TL + TL + 1)
                pe.wait_ge(sig("yo_mul"), n_ + 1)
                for i in range(FF // P):
                    ins = m(bank[0][:, 0:C], f_sT[:, i, :], wd_sb[:, i, :], start=(i == 0), stop=(i == FF // P - 1))
                ins.then_inc(sig("down_ps"), 1)

            pe.wait_ge(sig("gates_ready"), 2 * B)
            pe.wait_ge(sig("rows_ready"), 2)
            pe.wait_ge(sig("modT_ready"), 1)
            pe.wait_ge(sig("same_ready"), len(LEVELS))
            pe.wait_ge(sig("ffn_w_dma"), 48)
            with pe.Fori(0, NB) as bp:
                pe.wait_ge(sig("f_h_ready"), bp * TL * 2 + 1)
                transpose_h(bp * 2)
                pe.wait_ge(sig("yo_mul"), bp * TL + 1)
                beta_decay(bp)
                schedule(pe, bp, start, half, finish)
                transpose_h(bp * 2 + 1)
                pe.wait_ge(sig("hT_ready"), bp * 8 + 8 + 1)
                gate_up(bp, 0)
                for t in range(TL):
                    if t + 1 < TL:
                        gate_up(bp, t + 1)
                    down(bp, t)

        @block.scalar
        def _(act):
            A = nc.scalar.activation

            act.dma_start(wg_sb[:], wgate).then_inc(sig("ffn_w_dma"), 16)
            act.dma_start(wu_sb[:], wup).then_inc(sig("ffn_w_dma"), 16)
            act.dma_start(wd_sb[:], wdown).then_inc(sig("ffn_w_dma"), 16)
            act.wait_ge(sig("setup_dma"), 96)
            A(c_th[:], cT_sb[:], ACT.Tanh, scale=0.5).then_inc(sig("c_tanh"), 1)
            act.wait_ge(sig("rows_ps"), 1)
            A(expA[:], bank[2][:, NV:2 * NV], ACT.Exp).then_inc(sig("rows_ready"), 1)
            A(dtb_b[:], bank[2][:, 0:NV], ACT.Copy).then_inc(sig("rows_ready"), 1)

            def h_rows(n, which):
                act.wait_ge(sig("modc_ready"), n + 1)
                for k in range(CK):
                    act.wait_ge(sig("xnT_ps"), n * 2 + k + 1 + 1)
                    for g in range(BG):
                        A(hT[:, k, g * T:g * T + T], bank_p[k][:, g * T:g * T + T], ACT.Identity,
                          scale=modc[:, k * 6 + which + 1, g:g + 1],
                          bias=modc[:, k * 6 + which, g:g + 1]).then_inc(sig("hT_ready"), 1)

            def beta_decay(bp):
                act.wait_ge(sig("ba_neg"), bp * 2 + 2)
                A(ba_t[:, 0], ba_t[:, 1], ACT.Exp).then_inc(sig("ba_exp"), 1)
                A(ba_t[:, 2], ba[:, :, 0:NV], ACT.Exp, scale=-1.0).then_inc(sig("ba_exp"), 1)
                act.wait_ge(sig("ba_exp"), bp * 2 + 1)
                A(ba_t[:, 1], ba_t[:, 0], ACT.Ln, bias=1.0).then_inc(sig("ba_ln"), 1)
                act.wait_ge(sig("cum_ps"), bp + 1)
                act.wait_ge(sg("ck_ready", 1), bp * NK + 1)
                cum = bank[5][:, 0:3 * P].rearrange("p (k t h) -> p k t h", k=3, t=TL)
                A(cols[:, EG:EG + 3], cum, ACT.Exp).then_inc(sig("cum_exp"), 1)

            def decay_exp(g, J):
                act.wait_ge(sg("decay_ps", g), J + 1 + 1)
                act.wait_ge(sg("decay_beta", g), J + 1)
                A(units(e_raw, g), grid(bank_p[1][:]), ACT.Exp).then_inc(sg("decay_exp", g), 1)

            def last_tap(i, g, J):
                act.wait_ge(sg("proj_ps", g), J * 4 + i + 1)
                if i == 0:
                    act.wait_ge(sg("begin_ps", g), J * BEGIN_PS + 1)
                    act.wait_ge(sg("sq_ready", g), J + 1)
                elif i == 1:
                    act.wait_ge(sg("q_copied", g), J + 1)
                else:
                    act.wait_ge(sg("begin_ps", g), J * BEGIN_PS + 1)
                A(cc[:, i, g], bank_p[1 - i % 2][:, 0:T], ACT.Copy, scale=wconv[:, i, 3:4]).then_inc(sg("tap_last", g), 1)

            def z_tanh(g, j):
                act.wait_ge(sg("z_ps", g), j + 1 + 1)
                act.wait_ge(sg("z_gate", g), j + 1)
                A(zth[:, CH * g:CH * g + CH].rearrange("p t d -> p (t d)"), bank_p[1][:], ACT.Tanh,
                  scale=0.5).then_inc(sg("z_tanh", g), 1)

            def output_turned(g, j, bk):
                act.wait_ge(sg("goT_ps", g), j + 1 + 1)
                act.wait_ge(sg("oss_ready", g), j + 1)
                A(units(goT, g), grid(bk[:]), ACT.Copy).then_inc(sg("goT_ready", g), 1)

            def level(s, g, j):
                l = s // 2
                if s % 2:
                    act.wait_ge(sg("level_ps", g), j * 12 + 2 * l + 1)
                    A(lefts(units(inv, g), l), halves(bank_a[g], l), ACT.Copy).then_inc(sg("x_ready", g), 1)
                    act.wait_ge(sg("level_ps", g), j * 12 + 2 * l + 2)
                    A(rights(units(invT, g), l), halves(bank_b[g], l), ACT.Copy).then_inc(sg("xt_ready", g), 1)

            def flat(ap):
                return ap.rearrange("p v d -> p (v d)")

            def solve(s, g, j):
                bA, bB = bank_a[g], bank_b[g]
                if s == 1:
                    act.wait_ge(sg("solve_ps", g), j * SOLVE_PS + T_PS + 1)
                    A(units(tt, g), grid(bB[:]), ACT.Copy).then_inc(sg("t_ready", g), 1)
                elif s == 2:
                    act.wait_ge(sg("us_ready", g), j + 1)
                    act.wait_ge(sg("solve_ps", g), j * SOLVE_PS + U0_PS + 1)
                    A(flat(u0[:, g]), bA[:, 0:256], ACT.Copy).then_inc(sg("u0_ready", g), 1)
                elif s == 3:
                    act.wait_ge(sg("solve_ps", g), j * SOLVE_PS + S_PS + 1)
                    A(st[:, g], bB[:, 0:256], ACT.Copy).then_inc(sg("s_ready", g), 1)
                    act.wait_ge(sg("go_ready", g), j * 4 + 1)
                    act.wait_ge(sg("solve_ps", g), j * SOLVE_PS + O0_PS + 1)
                    A(flat(o[:, CH * g]), bA[:, 256:512], ACT.Copy).then_inc(sg("o0_ready", g), 1)
                elif s == 4:
                    act.wait_ge(sg("o1_ready", g), j + 1)
                    act.wait_ge(sg("r_ready", g), j * 2 + 2 + 1)
                    for p_ in range(PV):
                        A(qs[:, g, p_], bB[:, 256 + p_ * P:256 + p_ * P + P], ACT.Copy,
                          scale=ck[:, g, EG, 1, p_:p_ + 1]).then_inc(sg("qs_ready", g), 1)
                elif s == 5:
                    act.wait_ge(sg("solve_ps", g), j * SOLVE_PS + U1_PS + 1)
                    A(flat(u1[:, g]), bA[:, 0:256], ACT.Copy).then_inc(sg("u1_ready", g), 1)
                elif s == 6:
                    act.wait_ge(sg("o0_ready", g), j + 1)
                    act.wait_ge(sg("y_sum", g), j + 1)
                    act.wait_ge(sg("o1_ready", g), j + 1 + 1)
                    A(units(osq, g), o[:, CH * g:CH * g + CH].rearrange("p t v d -> p (t v) d"),
                      ACT.Square).then_inc(sg("osq_ready", g), 1)

            def begin(s, g, j):
                bA, bB = bank_a[g], bank_b[g]
                if s == 7:
                    act.wait_ge(sg("begin_ps", g), j * BEGIN_PS + VT_PS + 1)
                    act.wait_ge(sg("solve_ps", g), j * SOLVE_PS + 1)
                    act.wait_ge(sg("r_ready", g), j * 2 + 1)
                    A(v[:, CH * g:CH * g + CH].rearrange("p t v d -> p (t v d)"), bA[:], ACT.Copy).then_inc(sg("v_ready", g), 1)
                    act.wait_ge(sg("solve_ps", g), j * SOLVE_PS + 1)
                    act.wait_ge(sg("conv_step", g), j * 12 + 12 + 1)
                    A(qT[:, g], cc[:, 1, g], ACT.Copy).then_inc(sg("q_copied", g), 1)
                elif s == 8:
                    act.wait_ge(sg("solve_ps", g), j * SOLVE_PS + 1)
                    act.wait_ge(sg("begin_ps", g), j * BEGIN_PS + KNT_PS + 1)
                    A(knT[:, g], bB[:, 256:512], ACT.Copy).then_inc(sg("knT_ready", g), 1)
                elif s == 9:
                    act.wait_ge(sg("solve_ps", g), j * SOLVE_PS + 1)
                    act.wait_ge(sg("f_ready", g), j + 1)
                    act.wait_ge(sg("alo_ready", g), j + 1)
                    act.wait_ge(sg("a_ready", g), j + 1 + 1)
                    A(units(a_hi, g), units(at, g), ACT.Copy).then_inc(sg("ahi_ready", g), 1)

            def prepare(g, j):
                decay_exp(g, j)
                for i in range(QKV_BLK):
                    last_tap(i, g, j)

            def start(j):
                prepare(0, j)
                for s in range(7, 11):
                    begin(s, 0, j)
                prepare(1, j)

            def half(h, j, kh, first, last):
                g, js = 1 - h, j - 1 + h
                for s in range(SLOTS):
                    level(s, h, j)
                    if h == 1 or not first:
                        if s == 0:
                            z_tanh(g, js)
                        solve(s, g, js)
                    if h == 0 or not last:
                        begin(s, g, js + 1)
                    if s == 3 and not first:
                        output_turned(h, j - 1, bank_p[0])
                    if not last:
                        if s in (1, 4, 5, 7):
                            last_tap((1, 4, 5, 7).index(s), h, j + 1)
                        if s == 9:
                            decay_exp(h, j + 1)

            def finish(j):
                for s in range(SLOTS):
                    if s == 0:
                        z_tanh(1, j)
                    solve(s, 1, j)
                    if s == 3:
                        output_turned(0, j, bank_p[0])
                output_turned(1, j, bank_p[0])

            def ffn(bp):
                for t in range(TL):
                    n_ = bp * TL + t
                    act.wait_ge(sig("gu_ps"), n_ + 1)
                    act.wait_ge(sig("f_silu"), n_ * 2 + 1)
                    for hf in range(2):
                        A(f_th[:, hf * 512:hf * 512 + 512], bank[2 + hf][:], ACT.Tanh,
                          scale=0.5).then_inc(sig("f_tanh"), 1)
                    act.wait_ge(sig("down_ps"), n_ + 1)
                    for hf in range(2):
                        act.wait_ge(sig("f_sT_ps"), n_ * 2 + hf + 1 + 1)
                        A(f_sT[:, 4 * hf:4 * hf + 4], grid(bank[6 + hf][:]), ACT.Copy).then_inc(sig("f_sT_ready"), 1)
                    act.wait_ge(sig("yo_ready"), n_ + 1 + 1)
                    act.dma_start(out_t[bass.ds(bp, 1)].rearrange("a t p c -> p (a t) c")[:, t, :],
                                  yo[:]).then_inc(sig("out_dma"), 16)

            with act.Fori(0, NB) as bp:
                h_rows(bp * 2, 0)
                beta_decay(bp)
                schedule(act, bp, start, half, finish)
                h_rows(bp * 2 + 1, 3)
                ffn(bp)
            act.wait_ge(sig("out_dma"), NB * TL * 16 + 1)

        @block.vector
        def _(dve):
            V = nc.vector

            dve.wait_ge(sig("same_ps"), 1)
            dve.wait_ge(sig("same_ends"), 2)
            for i in range(len(LEVELS)):
                V.tensor_copy(same[:, i + 1, :], bank[i // 4][:, P * (i % 4):P * (i % 4) + P]).then_inc(sig("same_ready"), 1)
            dve.wait_ge(sig("same_ready"), len(LEVELS))
            for i in range(7):
                V.tensor_tensor(mask[:, i, :], same[:, i + 1, :], same[:, i, :], ALU.subtract).then_inc(sig("mask_diff"), 1)
            dve.wait_ge(sig("mask_low"), 8)
            for i in range(7):
                V.tensor_tensor(mask[:, i, :], mask[:, i, :], ident16[:], ALU.add).then_inc(sig("mask_ready"), 1)
            dve.wait_ge(sig("c_tanh"), 1)
            V.tensor_scalar(c_th[:], c_th[:], 1.0, 0.5, ALU.add, ALU.mult).then_inc(sig("silu_c"), 1)
            dve.wait_ge(sig("silu_c"), 1)
            V.tensor_tensor(silu_c[:], c_th[:], cT_sb[:], ALU.mult).then_inc(sig("silu_c"), 1)
            dve.wait_ge(sig("silu_c"), 2)
            V.tensor_copy(silu_cb[:].rearrange("p k b t -> p (k b) t"),
                          silu_c[:].rearrange("p k b -> p (k b)").unsqueeze(2).broadcast_to([P, CK * B, P])).then_inc(sig("silu_c"), 1)
            dve.wait_ge(sig("mod_ps"), 1)
            V.tensor_copy(modT[:], bank[3][:, 0:CK * 6 * B].rearrange("p (m b) -> p m b", b=B)).then_inc(sig("modT_ready"), 1)
            dve.wait_ge(sig("modT_ready"), 1)
            for k in range(CK):
                for i in (1, 4):
                    r = modT[:, k * 6 + i, :]
                    V.tensor_scalar(r, r, 1.0, None, ALU.add).then_inc(sig("modT_ready"), 1)
            for b in range(B):
                dve.wait_ge(sig("gates_ps"), b + 1)
                gp_ = bank[4 + b % 2][:]
                if b >= 1:
                    dve.wait_ge(sig("gates_ready"), 2 * b)
                V.tensor_copy(g_sb, gp_).then_inc(sig("gates_parts"), 1)
                V.tensor_scalar(g_sign, gp_, 0.0, 2.0, ALU.is_ge, ALU.mult).then_inc(sig("gates_parts"), 1)
                dve.wait_ge(sig("gates_parts"), 4 * b + 2)
                V.scalar_tensor_tensor(g_abs, g_sb, -1.0, g_sb, ALU.mult, ALU.max).then_inc(sig("gates_parts"), 1)
                V.tensor_scalar(g_sign, g_sign, -1.0, None, ALU.add).then_inc(sig("gates_parts"), 1)
                dve.wait_ge(sig("gates_parts"), 4 * b + 4)
                V.scalar_tensor_tensor(gates[:, b].rearrange("p h c -> p (h c)"), g_abs, GUARD, g_sign,
                                       ALU.max, ALU.mult).then_inc(sig("gates_ready"), 1)
                dve.wait_ge(sig("gates_ready"), 2 * b + 1)
                V.tensor_scalar(gates[:, b, 1], gates[:, b, 1], 0.5, None, ALU.mult).then_inc(sig("gates_ready"), 1)
            dve.wait_ge(sig("gates_ready"), 2 * B)
            dve.wait_ge(sig("mask_ready"), 7)
            dve.wait_ge(sig("modT_ready"), 5)
            for i in range(GU):
                V.tensor_copy(yl[:, :, i], ident16[:].unsqueeze(1).broadcast_to([P, len(LEVELS), P])).then_inc(sig("yl_ready"), 1)

            def layernorm(n, src, bp, x2_count):
                if x2_count is None:
                    dve.wait_ge(sig("x_dma"), bp * 16 + 16)
                else:
                    dve.wait_ge(sig("x2_ready"), x2_count + 1)
                for t in range(TL):
                    V.bn_stats(stats[:, t, :], src[:, t, :]).then_inc(sig("ln_stats"), 1)
                dve.wait_ge(sig("ln_stats"), n * TL + TL)
                dve.wait_ge(sig("hT_ready"), n * 4 + 1)
                V.tensor_scalar(modc[:], modT[:, :, bass.ds(bp * BG, BG)], 1.0, None,
                                ALU.mult).then_inc(sig("modc_ready"), 1)
                for t in range(TL):
                    V.bn_aggr(mv[:, t, :], stats[:, t, :]).then_inc(sig("ln_aggr"), 1)
                dve.wait_ge(sig("ln_rstd"), n + 1)
                dve.wait_ge(sig("xnT_ps"), n * 2 + 1)
                for t in range(TL):
                    V.tensor_scalar(xn[:, t, :], src[:, t, :], mv[:, t, 0:1], rstd[:, t:t + 1], ALU.subtract,
                                    ALU.mult).then_inc(sig("xn_ready"), 1)

            def beta_decay(bp):
                dve.wait_ge(sig("ba_ps"), bp + 1)
                V.tensor_copy(ba[:], bank[4][:, 0:TL * 2 * NV].rearrange("p (t h) -> p t h", t=TL)).then_inc(sig("ba_ready"), 1)
                dve.wait_ge(sig("ba_ready"), bp * 2 + 1)
                av = ba[:, :, NV:2 * NV]
                V.tensor_tensor(av, av, dtb_b[:].unsqueeze(1).broadcast_to([P, TL, NV]), ALU.add).then_inc(sig("ba_ready"), 1)
                dve.wait_ge(sig("ba_ready"), bp * 2 + 2)
                V.scalar_tensor_tensor(ba_t[:, 1], av, -1.0, av, ALU.mult, ALU.min).then_inc(sig("ba_neg"), 1)
                V.tensor_scalar(ba_t[:, 3], av, 0.0, None, ALU.max).then_inc(sig("ba_neg"), 1)
                dve.wait_ge(sig("ba_exp"), bp * 2 + 2)
                V.tensor_scalar(ba_t[:, 2], ba_t[:, 2], 1.0, None, ALU.add).then_inc(sig("ba_one"), 1)
                dve.wait_ge(sig("ba_one"), bp + 1)
                V.reciprocal(cols[:, BETA], ba_t[:, 2]).then_inc(sig("beta_ready"), 1)
                dve.wait_ge(sig("ba_neg"), bp * 2 + 2)
                dve.wait_ge(sig("ba_ln"), bp + 1)
                V.tensor_tensor(ba_t[:, 3], ba_t[:, 3], ba_t[:, 1], ALU.add).then_inc(sig("dt_ready"), 1)
                dve.wait_ge(sig("dt_ready"), bp + 1)
                V.scalar_tensor_tensor(cols[:, GLOG], ba_t[:, 3], -1.0,
                                       expA[:].unsqueeze(1).broadcast_to([P, TL, NV]), ALU.mult,
                                       ALU.mult).then_inc(sig("g_ready"), 1)
                dve.wait_ge(sig("cum_exp"), bp + 1)
                V.tensor_scalar(cols[:, NEGP], cols[:, NEGP], -1.0, None, ALU.mult).then_inc(sig("cols_ready"), 1)
                dve.wait_ge(sig("beta_ready"), bp + 1)
                V.tensor_tensor(cols[:, BSUF], cols[:, BSUF], cols[:, BETA], ALU.mult).then_inc(sig("cols_ready"), 1)
                dve.wait_ge(sig("cols_ready"), bp * 2 + 2)
                dve.wait_ge(sig("g_ready"), bp + 1)

            def head_cols(g, kh, kinds):
                h0 = kh * PV
                hs = slice(h0, h0 + PV) if isinstance(kh, int) else bass.ds(h0, PV)
                return cols[:, 0:kinds, CH * g:CH * g + CH, hs]

            def decay_rhs(g, J, kh):
                dve.wait_ge(sg("decay_beta", g), J + 1)
                V.tensor_scalar(cg[:, g], head_cols(g, kh, 2), 1.0, None, ALU.mult).then_inc(sg("g_le_ready", g), 1)

            def convolution(i, g, J):
                dve.wait_ge(sg("tap_last", g), J * 4 + i + 1)
                for s in range(1, TAPS):
                    if s > 1:
                        dve.wait_ge(sg("conv_step", g), J * 12 + 3 * i + s - 1 + 1)
                    V.scalar_tensor_tensor(cc[:, i, g, s:T], bank_p[1 - i % 2][:, 0:T - s], wconv[:, i, 3 - s:4 - s],
                                           cc[:, i, g, s:T], ALU.mult, ALU.add).then_inc(sg("conv_step", g), 1)

            def sum_squares(g, J):
                dve.wait_ge(sg("ss_ps", g), J + 1 + 1)
                dve.wait_ge(sg("rn_ready", g), J + 1)
                V.tensor_scalar(n2[:, g], bank_p[0][:, 0:2 * CH].rearrange("p (b t) -> p b t", b=2), EPS_K2, None,
                                ALU.max).then_inc(sg("ss_max", g), 1)

            def z_gate(g, j):
                dve.wait_ge(sg("go_ready", g), j * 4 + 1)
                dve.wait_ge(sg("z_tanh", g), j + 1)
                V.scalar_tensor_tensor(zg[:, CH * g:CH * g + CH].rearrange("p t v d -> p (t v d)"),
                                       zth[:, CH * g:CH * g + CH].rearrange("p t d -> p (t d)"), 1.0, bank_p[1][:],
                                       ALU.add, ALU.mult).then_inc(sg("z_gate", g), 1)

            def level(s, g, j):
                l = s // 2
                if s % 2 == 0:
                    dve.wait_ge(sg("y_ps", g), j * 6 + l + 1)
                    n_ = LEVELS[l]
                    V.tensor_tensor(lefts(yl[:, l], l), halves(bank_a[g], l),
                                    left(mask[:, l + 1, :], l).unsqueeze(1).broadcast_to([P, GU, HP // n_, n_]),
                                    ALU.mult).then_inc(sg("ym_ready", g), 1)

            def pairs(ap):
                return ap.rearrange("p (t v) s -> p t v s", v=PV)

            def chunks(ap):
                return ap.rearrange("p (t s) -> p t s", s=P).unsqueeze(2).broadcast_to([P, CH, PV, P])

            def solve(s, g, j, kh):
                bA, bB = bank_a[g], bank_b[g]
                if s == 0:
                    dve.wait_ge(sg("us_ready", g), j + 1)
                    dve.wait_ge(sg("qs_ready", g), j * 2 + 1)
                    V.tensor_scalar(ck[:, g], head_cols(g, kh, KINDS), 1.0, None, ALU.mult).then_inc(sg("ck_ready", g), 1)
                    dve.wait_ge(sg("solve_ps", g), j * SOLVE_PS + H_PS + 1)
                    V.tensor_tensor(units(ym, g), twoI[:].unsqueeze(1).broadcast_to([P, GU, P]), grid(bA[:]),
                                    ALU.subtract).then_inc(sg("h_ready", g), 1)
                elif s == 2:
                    dve.wait_ge(sg("solve_ps", g), j * SOLVE_PS + 1)
                    dve.wait_ge(sg("ck_ready", g), j + 1 + 1)
                    dve.wait_ge(sg("u0_ready", g), j + 1)
                    V.tensor_tensor(us[:, g], u0[:, g], ck[:, g, BSUF, 0].unsqueeze(2).broadcast_to([P, PV, P]),
                                    ALU.mult).then_inc(sg("us_ready", g), 1)
                elif s == 4:
                    dve.wait_ge(sg("solve_ps", g), j * SOLVE_PS + QS_PS + 1)
                    for p_ in range(PV):
                        V.scalar_tensor_tensor(rr[:, g, p_], bB[:, p_ * P:p_ * P + P], ck[:, g, NEGP, 1, p_:p_ + 1],
                                               v[:, CH * g + 1, p_], ALU.mult, ALU.add).then_inc(sg("r_ready", g), 1)
                elif s == 6:
                    dve.wait_ge(sg("osq_ready", g), j + 1)
                    dve.wait_ge(sg("qs_ready", g), j * 2 + 2 + 1)
                    dve.wait_ge(sg("solve_ps", g), j * SOLVE_PS + O1_PS + 1)
                    V.tensor_tensor(o[:, CH * g + 1].rearrange("p v d -> p (v d)"), bA[:, 256:512],
                                    qs[:, g].rearrange("p v d -> p (v d)"), ALU.add).then_inc(sg("o1_ready", g), 1)
                elif s == 7:
                    dve.wait_ge(sg("osc_ready", g), j * 6 + 1)
                    dve.wait_ge(sg("osq_ready", g), j + 1 + 1)
                    V.tensor_reduce(oss[:, g].rearrange("p t v -> p (t v)"), units(osq, g), AXX,
                                    ALU.add).then_inc(sg("oss_ready", g), 1)
                elif s == 11:
                    dve.wait_ge(sg("goT_ps", g), j + 1)
                    dve.wait_ge(sg("o0_ready", g), j + 1)
                    dve.wait_ge(sg("o1_ready", g), j + 1 + 1)
                    dve.wait_ge(sg("z_gate", g), j + 1 + 1)
                    dve.wait_ge(sg("osc_ready", g), j * 6 + 6 + 1)
                    for c in range(CH):
                        for p_ in range(PV):
                            t = CH * g + c
                            V.scalar_tensor_tensor(go[:, t, p_], o[:, t, p_], osc[:, g, 3, c, p_:p_ + 1], zg[:, t, p_],
                                                   ALU.mult, ALU.mult).then_inc(sg("go_ready", g), 1)

            def begin(s, g, j):
                bA, bB = bank_a[g], bank_b[g]
                if s == 7:
                    dve.wait_ge(sg("solve_ps", g), j * SOLVE_PS + 1)
                    dve.wait_ge(sg("rn_ready", g), j + 1 + 1)
                    dve.wait_ge(sg("begin_ps", g), j * BEGIN_PS + KT_PS + 1)
                    V.tensor_tensor(kn[:, g], bB[:, 0:256].rearrange("p (t d) -> p t d", d=P),
                                    rn[:, g, 0].unsqueeze(2).broadcast_to([P, CH, P]), ALU.mult).then_inc(sg("kn_ready", g), 1)
                elif s == 9:
                    dve.wait_ge(sg("decay_beta", g), j + 1 + 1)
                    dve.wait_ge(sg("alo_ready", g), j + 1)
                    dve.wait_ge(sg("begin_ps", g), j * BEGIN_PS + KQ_PS + 1)
                    V.tensor_tensor(pairs(units(at, g)), pairs(units(e_b, g)[:, :, 0:P]), chunks(bB[:, 0:256]),
                                    ALU.mult).then_inc(sg("a_ready", g), 1)
                    dve.wait_ge(sg("solve_ps", g), j * SOLVE_PS + 1)
                    V.tensor_tensor(pairs(units(pt, g)), pairs(units(e_b, g)[:, :, 1:P + 1]), chunks(bB[:, 256:512]),
                                    ALU.mult).then_inc(sg("pt_ready", g), 1)
                    dve.wait_ge(sg("ahi_ready", g), j + 1)
                    V.tensor_tensor(units(f_hi, g), ident16[:].unsqueeze(1).broadcast_to([P, GU, P]), units(a_hi, g),
                                    ALU.subtract).then_inc(sg("f_ready", g), 1)
                    dve.wait_ge(sg("solve_ps", g), j * SOLVE_PS + 1)
                    dve.wait_ge(sg("f_ready", g), j + 1 + 1)
                    V.tensor_tensor(units(invT, g), maskT1[:].unsqueeze(1).broadcast_to([P, GU, P]), units(f_hi, g),
                                    ALU.mult).then_inc(sg("first_ready", g), 1)
                elif s == 10:
                    dve.wait_ge(sg("begin_ps", g), j * BEGIN_PS + F_PS + 1)
                    V.tensor_tensor(units(inv, g), grid(bA[:]), mask[:, 0, :].unsqueeze(1).broadcast_to([P, GU, P]),
                                    ALU.mult).then_inc(sg("first_ready", g), 1)

            def out_weights(j):
                dve.wait_ge(sig("wo_dma"), j * 16 + 16)
                dve.wait_ge(sg("y_sum", 1), j + 1)
                V.tensor_scalar(wo_n[:], wo_sb[:], nw_sb[:, 0:1], 0.5 * P ** 0.5, ALU.mult, ALU.mult).then_inc(sig("wo_ready"), 1)

            def start(j):
                decay_rhs(0, j, 0)
                decay_rhs(1, j, 0)
                for i in range(QKV_BLK):
                    convolution(i, 0, j)
                sum_squares(0, j)
                for s in range(7, 11):
                    begin(s, 0, j)
                for i in range(QKV_BLK):
                    convolution(i, 1, j)
                sum_squares(1, j)

            def half(h, j, kh, first, last):
                g, js = 1 - h, j - 1 + h
                for s in range(SLOTS):
                    level(s, h, j)
                    if h == 1 or not first:
                        solve(s, g, js, kh - 1 + h)
                        if s == 1:
                            z_gate(g, js)
                    if h == 0 or not last:
                        begin(s, g, js + 1)
                    if not last:
                        if s == 2:
                            decay_rhs(h, j + 1, kh + 1)
                        if s in (3, 5, 7, 8):
                            convolution((3, 5, 7, 8).index(s), h, j + 1)
                        if s == 11:
                            sum_squares(h, j + 1)
                    if h == 1 and s == 11:
                        out_weights(j)

            def finish(j):
                for s in range(SLOTS):
                    solve(s, 1, j, NK - 1)
                    if s == 1:
                        z_gate(1, j)

            def residual(bp):
                for g in range(BG):
                    gx = gates[:, bass.ds(bp * BG + g, 1), 0].rearrange("p a c -> p (a c)")
                    for c_ in range(CH):
                        t = CH * g + c_
                        if t == 0:
                            dve.wait_ge(sg("y_sum", 0), bp * NK + NK + 1)
                            dve.wait_ge(sg("y_sum", 1), bp * NK + NK + 1)
                            dve.wait_ge(sig("yo_ready"), bp * TL + 1)
                        V.tensor_tensor(x2[:, t], bank_y[g][:, c_ * C:c_ * C + C], gx, ALU.mult).then_inc(sig("x2_mul"), 1)
                for t in range(TL):
                    dve.wait_ge(sig("x2_mul"), bp * TL + t + 1)
                    V.tensor_tensor(x2[:, t], x2[:, t], xs[:, t], ALU.add).then_inc(sig("x2_ready"), 1)

            def ffn(bp):
                for t in range(TL):
                    n_ = bp * TL + t
                    for hf in range(2):
                        dve.wait_ge(sig("f_tanh"), n_ * 2 + hf + 1)
                        fs = f_th[:, hf * 512:hf * 512 + 512]
                        V.scalar_tensor_tensor(f_a[:, hf * 512:hf * 512 + 512], fs, 1.0, bank[2 + hf][:], ALU.add,
                                               ALU.mult).then_inc(sig("f_silu"), 1)
                    for hf in range(2):
                        dve.wait_ge(sig("f_silu"), n_ * 2 + hf + 1 + 1)
                        V.tensor_tensor(f_h[:, hf * 512:hf * 512 + 512], f_a[:, hf * 512:hf * 512 + 512],
                                        bank[4 + hf][:], ALU.mult).then_inc(sig("f_h_ready"), 1)
                    dve.wait_ge(sig("f_h_ready"), n_ * 2 + 2 + 1)
                    V.scalar_tensor_tensor(f_a, f_h, -1.0, f_h, ALU.mult, ALU.max).then_inc(sig("f_rank"), 1)
                    dve.wait_ge(sig("f_rank"), n_ * 12 + 1)
                    a4 = f_a.rearrange("p (n f) -> p n f", f=4)
                    V.tensor_tensor(f_c1[:], a4[:, :, 0:3], a4[:, :, 1:4], ALU.is_ge).then_inc(sig("f_rank"), 1)
                    V.tensor_tensor(f_c2[:], a4[:, :, 0:2], a4[:, :, 2:4], ALU.is_ge).then_inc(sig("f_rank"), 1)
                    V.tensor_tensor(f_c3[:], a4[:, :, 0], a4[:, :, 3], ALU.is_ge).then_inc(sig("f_rank"), 1)
                    dve.wait_ge(sig("f_rank"), n_ * 12 + 4)
                    c01, c12, c23 = (f_c1[:, :, i] for i in range(3))
                    c02, c13 = (f_c2[:, :, i] for i in range(2))
                    c03 = f_c3[:]
                    w = f_w
                    V.tensor_tensor(w[:, 0, 0], c01, c02, ALU.add).then_inc(sig("f_rank"), 1)
                    V.tensor_tensor(w[:, 0, 1], c12, c13, ALU.add).then_inc(sig("f_rank"), 1)
                    V.tensor_tensor(w[:, 0, 2], c23, c02, ALU.subtract).then_inc(sig("f_rank"), 1)
                    V.tensor_tensor(w[:, 0, 3], c03, c13, ALU.add).then_inc(sig("f_rank"), 1)
                    dve.wait_ge(sig("f_rank"), n_ * 12 + 8)
                    V.tensor_tensor(w[:, 1, 0], w[:, 0, 0], c03, ALU.add).then_inc(sig("f_rank"), 1)
                    V.tensor_tensor(w[:, 1, 1], w[:, 0, 1], c01, ALU.subtract).then_inc(sig("f_rank"), 1)
                    V.tensor_tensor(w[:, 1, 2], w[:, 0, 2], c12, ALU.subtract).then_inc(sig("f_rank"), 1)
                    V.tensor_tensor(w[:, 1, 3], w[:, 0, 3], c23, ALU.add).then_inc(sig("f_rank"), 1)
                    dve.wait_ge(sig("f_rank"), n_ * 12 + 12)
                    dve.wait_ge(sig("f_sT_ps"), n_ * 2 + 1)
                    h4 = f_h.rearrange("p (n f) -> p n f", f=4)
                    s4 = f_s.rearrange("p (n f) -> p n f", f=4)
                    for i, (op, thr) in enumerate(((ALU.is_ge, 2.0), (ALU.is_ge, 1.0), (ALU.is_ge, 0.0), (ALU.is_le, 1.0))):
                        V.scalar_tensor_tensor(s4[:, :, i], w[:, 1, i], thr, h4[:, :, i], op,
                                               ALU.mult).then_inc(sig("f_s_ready"), 1)
                    dve.wait_ge(sig("down_ps"), n_ + 1 + 1)
                    dve.wait_ge(sig("out_dma"), n_ * 16 + 1)
                    gx = gates[:, bass.ds(bp * BG + t // CH, 1), 1].rearrange("p a c -> p (a c)")
                    V.tensor_tensor(yo[:], bank[0][:, 0:C], gx, ALU.mult).then_inc(sig("yo_mul"), 1)
                    dve.wait_ge(sig("yo_mul"), n_ + 1 + 1)
                    V.tensor_tensor(yo[:], yo[:], x2[:, t], ALU.add).then_inc(sig("yo_ready"), 1)

            with dve.Fori(0, NB) as bp:
                layernorm(bp * 2, xs, bp, None)
                beta_decay(bp)
                schedule(dve, bp, start, half, finish)
                residual(bp)
                layernorm(bp * 2 + 1, x2, bp, bp * TL + TL)
                ffn(bp)


_OUT = (B, T, C)


def kernel(**inputs):
    import numpy as np
    import concourse.bacc as bacc
    from concourse.bass_utils import run_bass_kernel_spmd

    a = {k.replace("L0_", ""): np.asarray(v) for k, v in inputs.items()}
    qd = NK * P

    def rows128(w):
        return np.ascontiguousarray(w.reshape(-1, P, w.shape[1]).transpose(1, 0, 2))

    wq = a["attn_W_qkv"]
    heads = []
    for h in range(NK):
        q, k = wq[h * P:(h + 1) * P], wq[qd + h * P:qd + (h + 1) * P]
        vv = wq[2 * qd + h * PV * P:2 * qd + (h + 1) * PV * P]
        cw = a["attn_conv_w"]
        cws = [cw[qd + h * P:qd + (h + 1) * P], cw[h * P:(h + 1) * P],
               cw[2 * qd + h * PV * P:2 * qd + h * PV * P + P], cw[2 * qd + h * PV * P + P:2 * qd + (h + 1) * PV * P]]
        w = rows128(np.concatenate([k, q, vv], 0).T).reshape(P, -1)
        heads.append(np.concatenate([w, np.stack(cws, 1).reshape(P, -1)], 1))
    arrays = {
        "x": a["attn_x"].reshape(B * T, C),
        "wqkv": np.stack(heads),
        "wz": np.stack([rows128(a["attn_W_z"][h * PV * P:(h + 1) * PV * P].T) for h in range(NK)]),
        "wout": np.ascontiguousarray(a["attn_W_out"].T.reshape(NK, PV, P, C).transpose(0, 2, 1, 3)),
        "nw": a["attn_norm_w"].reshape(P, 1),
        "wba": rows128(np.concatenate([a["attn_W_b"], a["attn_W_a"]], 0).T),
        "dtb": a["attn_dt_bias"].reshape(1, NV),
        "alog": a["attn_A_log"].reshape(1, NV),
        "wgate": rows128(a["ffn_w_gate"]),
        "wup": rows128(a["ffn_w_up"]),
        "wdown": rows128(a["ffn_w_down"]),
        "cT": rows128(a["c"].T),
        "wmod": rows128(a["wmod"]),
    }
    arrays = {f"in_{k}": np.ascontiguousarray(v) for k, v in arrays.items()}
    nc = bacc.Bacc("TRN2", target_bir_lowering=False, num_devices=1)
    args = [nc.dram_tensor(k, v.shape, mybir.dt.from_np(v.dtype), kind="ExternalInput").ap() for k, v in arrays.items()]
    args.append(nc.dram_tensor("out_0", (B * T, C), F32, kind="ExternalOutput").ap())
    adaln_deltanet_ffn(nc, *args)
    r = run_bass_kernel_spmd(nc, [arrays], core_ids=[0])
    return r.results[0]["out_0"].reshape(_OUT)
```

```python
from contextlib import ExitStack

import concourse.bass as bass
from concourse import mybir

ALU = mybir.AluOpType
ACT = mybir.ActivationFunctionType
AXX = mybir.AxisListType.X
F32 = mybir.dt.float32
F16 = mybir.dt.float16

P = 128
HP = P // 2
B, T, C = 8, 256, 256
NK, PV = 16, 2
NV = NK * PV
TAPS = 4
FF = 1024
CK = C // P
BG = 2
NB = B // BG
TL = BG * T // P
CH = T // P
TOK = BG * T
U = TL * PV
GU = CH * PV
QKV_BLK = 4
LEVELS = (2, 4, 8, 16, 32, 64)
NEG = -30000.0
EPS_LN, EPS_RMS, EPS_K2 = 1e-5, 1e-6, 1e-24
GUARD = 0.25
W_SCALE, Z_SCALE, O_SCALE = 64.0, 8.0, 8.0
BETA, GLOG, EG, NEGP, BSUF, KINDS = 0, 1, 2, 3, 4, 5


def adaln_deltanet_ffn(nc, x, wqkv, wz, wout, nw, wba, dtb, alog, wgate, wup, wdown, cT, wmod, out):
    with ExitStack() as ctx:
        def sb(name, shape, dt=F32):
            return ctx.enter_context(nc.sbuf_tensor(name, shape, dt))

        def sem(name):
            return ctx.enter_context(nc.semaphore(name))

        bank = [ctx.enter_context(nc.psum_tensor(f"bank{i}", [P, 512], F32)) for i in range(8)]
        bank_y = bank[0:2]
        bank_p = bank[2:4]
        bank_a = (bank[4], bank[6])
        bank_b = (bank[5], bank[7])

        ident = sb("ident", [P, P])
        ident16 = sb("ident16", [P, P], F16)
        twoI = sb("twoI", [P, P])
        le = sb("le", [P, P])
        lt = sb("lt", [P, P])
        gt = sb("gt", [P, P])
        neg16 = sb("neg16", [P, P], F16)
        ones = sb("ones", [P, P])
        zero16 = sb("zero16", [P, 512], F16)
        mhalf = sb("mhalf", [P, 16])
        eps = sb("eps", [P, 2, 8])
        blockrows = sb("blockrows", [P, 6, P], F16)
        same = sb("same", [P, 8, P], F16)
        mask = sb("mask", [P, 7, P], F16)
        maskT1 = sb("maskT1", [P, P], F16)
        wg_sb = sb("wg_sb", [P, CK, FF])
        wu_sb = sb("wu_sb", [P, CK, FF])
        wd_sb = sb("wd_sb", [P, FF // P, C])
        wba_sb = sb("wba_sb", [P, CK, 2 * NV])
        wmod_sb = sb("wmod_sb", [P, CK, 6 * C])
        nw_sb = sb("nw_sb", [P, 1])
        rows = sb("rows", [1, 2 * NV])
        dtb_b = sb("dtb_b", [P, NV])
        expA = sb("expA", [P, NV])
        cT_sb = sb("cT_sb", [P, CK, B])
        c_th = sb("c_th", [P, CK, B])
        silu_c = sb("silu_c", [P, CK, B])
        silu_cb = sb("silu_cb", [P, CK, B, P])
        g_le = silu_cb[:, 0]
        e_raw = silu_cb[:, 1]
        modT = sb("modT", [P, CK * 6, B])
        gates = sb("gates", [P, B, 2, C])
        xs = sb("xs", [P, TL, C])
        x2 = sb("x2", [P, TL, C])
        stats = sb("stats", [P, TL, 6])
        mv = sb("mv", [P, TL, 2])
        ve = sb("ve", [P, TL])
        rstd = sb("rstd", [P, TL])
        xn = sb("xn", [P, TL, C])
        modc = sb("modc", [P, CK * 6, BG])
        hT = sb("hT", [P, CK, TOK])
        ba = sb("ba", [P, TL, 2 * NV])
        ba_t = sb("ba_t", [P, 4, TL, NV])
        cols = sb("cols", [P, KINDS, TL, NV])
        NQ = QKV_BLK * P
        wq_sb = sb("wq_sb", [P, CK * NQ + QKV_BLK * TAPS])
        wz_sb = sb("wz_sb", [P, CK, PV * P])
        wo_sb = sb("wo_sb", [P, PV, C])
        wo_n = sb("wo_n", [P, PV, C])
        wq16 = sb("wq16", [P, 2, CK * NQ], F16)
        wz16 = sb("wz16", [P, 2, CK, PV * P], F16)
        wo16 = sb("wo16", [P, 2, PV, C], F16)
        h16 = sb("h16", [P, 2, CK, TOK], F16)
        wc = sb("wc", [P, QKV_BLK, TAPS])
        wconv = wq_sb[:, CK * NQ:].rearrange("p (b j) -> p b j", j=TAPS)
        cg = sb("cg", [P, BG, 2, CH, PV])
        e_b = sb("e_b", [P, U, P + 1])
        setup_cols = wmod_sb[:].rearrange("p k n -> p (k n)")
        cc = setup_cols[:, 0:QKV_BLK * TOK].rearrange("p (i g t) -> p i g t", i=QKV_BLK, g=BG)
        sq = setup_cols[:, QKV_BLK * TOK:(QKV_BLK + 2) * TOK].rearrange("p (g b t) -> p g b t", g=BG, b=2)
        ck = sb("ck", [P, BG, KINDS, CH, PV])
        n2 = sb("n2", [P, BG, 2, CH])
        rn = sb("rn", [P, BG, 2, CH])
        rq = sb("rq", [P, BG, CH])
        kn = sb("kn", [P, BG, CH, P])
        knT = sb("knT", [P, BG, T])
        qT = sb("qT", [P, BG, T])
        v = sb("v", [P, TL, PV, P])
        at = sb("at", [P, U, P])
        pt = sb("pt", [P, U, P])
        a_hi = sb("a_hi", [P, U, P], F16)
        a_lo = sb("a_lo", [P, U, P], F16)
        f_hi = sb("f_hi", [P, U, P], F16)
        inv = sb("inv", [P, U, P], F16)
        invT = sb("invT", [P, U, P], F16)
        ym = sb("ym", [P, U, P], F16)
        yl = sb("yl", [P, len(LEVELS), GU, P], F16)
        tt = sb("tt", [P, U, P])
        u0 = sb("u0", [P, BG, PV, P])
        us = sb("us", [P, BG, PV, P])
        st = sb("st", [P, BG, PV * P])
        rr = sb("rr", [P, BG, PV, P])
        u1 = sb("u1", [P, BG, PV, P])
        qs = sb("qs", [P, BG, PV, P])
        o = sb("o", [P, TL, PV, P])
        oss = sb("oss", [P, BG, CH, PV])
        osc = sb("osc", [P, BG, 4, CH, PV])
        zth = sb("zth", [P, TL, PV * P])
        zg = sb("zg", [P, TL, PV, P])
        go = sb("go", [P, TL, PV, P])
        goT16 = sb("goT16", [P, 2, U, P], F16)
        osq = xn[:].rearrange("p t (u s) -> p (t u) s", s=P)
        g_sign = zth[:, 0:2].rearrange("p t d -> p (t d)")
        g_abs = zth[:, 2:4].rearrange("p t d -> p (t d)")
        g_sb = go[:, 0:2].rearrange("p t v d -> p (t v d)")
        h_ffn = zg[:].rearrange("p t v d -> p (t v d)").rearrange("p (k t) -> p k t", k=CK)
        f_th = at[:].rearrange("p u s -> p (u s)")
        f_h = tt[:].rearrange("p u s -> p (u s)")
        f_a = pt[:].rearrange("p u s -> p (u s)")
        f_s = go[:].rearrange("p t v d -> p (t v d)")
        f_sT = v[:].rearrange("p t v d -> p (t v) d")
        f_c1 = sb("f_c1", [P, 3, FF // 4], F16)
        f_c2 = sb("f_c2", [P, 2, FF // 4], F16)
        f_c3 = sb("f_c3", [P, FF // 4], F16)
        f_w = sb("f_w", [P, 2, 4, FF // 4], F16)
        yo = sb("yo", [P, C])

        S = {}

        OPEN = 1
        FREE = ("down_ps", "f_h_ready", "f_sT_ps", "f_sT_ready", "f_s_ready", "f_silu",
                "hT_ready", "out_dma", "wo_ready", "wq_split", "wz_split", "x2_ready",
                "xnT_ps", "yo_mul", "yo_ready")
        FREE_G = ("a_ready", "alo_ready", "begin_ps", "ck_ready", "conv_step", "decay_beta",
                "decay_ps", "f_ready", "goT_ps", "goT_ready", "go_ready", "kn_ready",
                "o1_ready", "osc_ready", "osq_ready", "oss_ready", "proj_ps", "pt_ready",
                "q_copied", "qs_ready", "r_ready", "rn_ready", "solve_ps", "sq_ready",
                "ss_ps", "us_ready", "y_sum", "z_gate", "z_ps")

        def sig(name):
            if name not in S:
                S[name] = sem(name)
            return S[name]

        x_t = x.rearrange("(n t p) c -> n p t c", p=P, t=TL)
        out_t = out.rearrange("(n t p) c -> n t p c", p=P, t=TL)

        def units(tensor, g):
            return tensor[:, GU * g:GU * g + GU, :]

        def grid(ap):
            return ap.rearrange("p (u s) -> p u s", s=P)

        H_PS, T_PS, U0_PS, S_PS, O0_PS, QS_PS, U1_PS, O1_PS = range(1, 9)
        SOLVE_PS = 8
        KT_PS, VT_PS, KNT_PS, KQ_PS, F_PS = range(1, 6)
        BEGIN_PS = 5
        CG_READY, G_LE_DONE = range(1, 3)
        G_LE_STEPS = 2

        def sg(name, g):
            return sig(f"{name}_{g}")

        block = ctx.enter_context(nc.Block())

        @block.sync
        def _(sp):
            sp.dma_start(cT_sb[:], cT).then_inc(sig("setup_dma"), 16)
            sp.dma_start(wmod_sb[:], wmod).then_inc(sig("setup_dma"), 16)
            sp.dma_start(rows[0:1, 0:NV], dtb).then_inc(sig("setup_dma"), 16)
            sp.dma_start(rows[0:1, NV:2 * NV], alog).then_inc(sig("setup_dma"), 16)
            sp.dma_start(nw_sb[:], nw).then_inc(sig("setup_dma"), 16)
            sp.dma_start(wba_sb[:], wba).then_inc(sig("setup_dma"), 16)
            with sp.Fori(0, NB) as bp:
                sp.wait_ge(sig("x2_ready"), bp * TL + OPEN)
                sp.dma_start(xs[:], x_t[bass.ds(bp, 1)].rearrange("a p t c -> p (a t) c")).then_inc(sig("x_dma"), 16)

                def load_qkv(j, kh):
                    sp.wait_ge(sig("wq_split"), j * 3 + OPEN)
                    src = wqkv[kh] if isinstance(kh, int) else wqkv[bass.ds(kh, 1)].rearrange("a p n -> p (a n)")
                    sp.dma_start(wq_sb[:], src).then_inc(sig("wq_dma"), 16)

                def load_zo(j, kh):
                    sp.wait_ge(sig("wz_split"), j * 2 + OPEN)
                    s1 = wz[kh] if isinstance(kh, int) else wz[bass.ds(kh, 1)].rearrange("a p k n -> p (a k) n")
                    sp.dma_start(wz_sb[:], s1).then_inc(sig("wz_dma"), 16)
                    sp.wait_ge(sig("wo_ready"), j * 3 + OPEN)
                    s2 = wout[kh] if isinstance(kh, int) else wout[bass.ds(kh, 1)].rearrange("a p k n -> p (a k) n")
                    sp.dma_start(wo_sb[:], s2).then_inc(sig("wo_dma"), 16)

                load_qkv(bp * NK, 0)
                with sp.Fori(0, NK - 1) as kh:
                    load_qkv(bp * NK + kh + 1, kh + 1)
                    load_zo(bp * NK + kh, kh)
                load_zo(bp * NK + (NK - 1), NK - 1)

        def left(ap, l):
            return ap.rearrange("p (b h s) -> p b h s", h=2, s=LEVELS[l])[:, :, 0, :]

        def right(ap, l):
            return ap.rearrange("p (b h s) -> p b h s", h=2, s=LEVELS[l])[:, :, 1, :]

        def lefts(ap, l):
            return ap.rearrange("p u (b h s) -> p u b h s", h=2, s=LEVELS[l])[:, :, :, 0, :]

        def rights(ap, l):
            return ap.rearrange("p u (b h s) -> p u b h s", h=2, s=LEVELS[l])[:, :, :, 1, :]

        def halves(bk, l):
            return bk[:, 0:GU * HP].rearrange("p (u b s) -> p u b s", u=GU, s=LEVELS[l])

        SLOTS = 12
        PE_AT = {"project_0": 5, "turn": 3, "project_1": 8, "project_2": 11, "y_0": 13,
                 "project_3": 14, "y_1": 16, "decays": 19, "sum_squares": 20, "z_0": 21, "z_1": 23}
        ACT_AT = {"z_tanh": 0, "tap_0": 5, "turned": 4, "tap_1": 7, "tap_2": 12,
                  "tap_3": 14, "decays": 19, "wo_high": 7, "wq_high": 1, "wz_high": 12}
        DVE_AT = {"z_gate": 1, "decay_cols": 5, "conv_0": 7, "conv_1": 11, "conv_2": 13,
                  "conv_3": 17, "sum_squares": 23, "wq_low": 1, "wz_low": 17, "turned": 5}

        def schedule(eng, bp, start, half, finish):
            start(bp * NK, bp)
            half(0, bp * NK, 0, True, False)
            half(1, bp * NK, 0, True, False)
            with eng.Fori(1, NK - 1) as kh:
                half(0, bp * NK + kh, kh, False, False)
                half(1, bp * NK + kh, kh, False, False)
            half(0, bp * NK + (NK - 1), NK - 1, False, True)
            half(1, bp * NK + (NK - 1), NK - 1, False, True)
            finish(bp * NK + (NK - 1))

        start_banks = (bank_p, (bank_a[1], bank_b[1]))

        @block.gpsimd
        def _(pool):
            gp = nc.gpsimd
            for name in FREE:
                pool.sem_inc(sig(name), OPEN)
            for name in FREE_G:
                for g in range(BG):
                    pool.sem_inc(sg(name, g), OPEN)
            cst = sig("pool_const")
            n = [0]

            def done(ins):
                n[0] += 1
                ins.then_inc(cst, 1)
                pool.wait_ge(cst, n[0])

            done(gp.memset(ones[:], 1.0))
            gp.memset(mhalf[:], -0.5).then_inc(cst, 1)
            gp.memset(eps[:, 0], EPS_LN).then_inc(cst, 1)
            gp.memset(eps[:, 1], P * EPS_RMS).then_inc(cst, 1)
            gp.memset(twoI[:], 2.0).then_inc(cst, 1)
            gp.memset(zero16[:], 0.0).then_inc(cst, 1)
            gp.memset(e_b[:], 0.0).then_inc(cst, 1)
            gp.memset(blockrows[:], 1.0).then_inc(cst, 1)
            n[0] += 7
            pool.wait_ge(cst, n[0])
            gp.affine_select(out=ident[:], in_=ones[:], compare_op=ALU.is_equal, fill=0.0, base=0,
                             pattern=[[-1, P]], channel_multiplier=1).then_inc(cst, 1)
            gp.affine_select(out=ident16[:], in_=ones[:], compare_op=ALU.is_equal, fill=0.0, base=0,
                             pattern=[[-1, P]], channel_multiplier=1).then_inc(cst, 1)
            gp.affine_select(out=twoI[:], in_=twoI[:], compare_op=ALU.is_equal, fill=0.0, base=0,
                             pattern=[[-1, P]], channel_multiplier=1).then_inc(cst, 1)
            gp.affine_select(out=le[:], in_=ones[:], compare_op=ALU.is_ge, fill=0.0, base=0,
                             pattern=[[1, P]], channel_multiplier=-1).then_inc(cst, 1)
            gp.affine_select(out=lt[:], in_=ones[:], compare_op=ALU.is_gt, fill=0.0, base=0,
                             pattern=[[1, P]], channel_multiplier=-1).then_inc(cst, 1)
            gp.affine_select(out=gt[:], in_=ones[:], compare_op=ALU.is_gt, fill=0.0, base=0,
                             pattern=[[-1, P]], channel_multiplier=1).then_inc(cst, 1)
            gp.affine_select(out=neg16[:], in_=zero16[:, 0:P], compare_op=ALU.is_ge, fill=NEG, base=0,
                             pattern=[[1, P]], channel_multiplier=-1).then_inc(cst, 1)
            n[0] += 7
            pool.wait_ge(cst, n[0])
            for i, size in enumerate(LEVELS):
                done(gp.affine_select(out=blockrows[:, i, :], in_=blockrows[:, i, :], compare_op=ALU.is_ge, fill=0.0,
                                      base=0, pattern=[[1, P]], channel_multiplier=-size))
                ins = gp.affine_select(out=blockrows[:, i, :], in_=blockrows[:, i, :], compare_op=ALU.is_ge, fill=0.0,
                                       base=size - 1, pattern=[[-1, P]], channel_multiplier=size)
                ins.then_inc(sig("blockrows_ready"), 1)
            pool.wait_ge(sig("blockrows_ready"), len(LEVELS))
            gp.tensor_copy(same[:, 0, :], ident16[:]).then_inc(sig("same_ends"), 1)
            gp.tensor_copy(same[:, 7, :], ones[:]).then_inc(sig("same_ends"), 1)
            pool.wait_ge(sig("mask_steps"), 7)
            for i in range(7):
                gp.affine_select(out=mask[:, i, :], in_=mask[:, i, :], compare_op=ALU.is_ge, fill=0.0, base=0,
                                 pattern=[[-1, P]], channel_multiplier=1).then_inc(sig("mask_steps"), 1)
            gp.affine_select(out=maskT1[:], in_=same[:, 1, :], compare_op=ALU.is_ge, fill=0.0, base=0,
                             pattern=[[1, P]], channel_multiplier=-1).then_inc(sig("mask_steps"), 1)

            def layernorm_rstd(n):
                pool.wait_ge(sig("ln_aggr"), n * TL + TL)
                gp.tensor_tensor(ve[:], mv[:, :, 1], eps[:, 0, 0:TL], ALU.add).then_inc(sig("ln_eps"), 1)
                pool.wait_ge(sig("ln_eps"), n + 1)
                gp.tensor_tensor(rstd[:], ve[:], mhalf[:, 0:TL], ALU.pow).then_inc(sig("ln_rstd"), 1)

            def decays(g, J):
                pool.wait_ge(sg("decay_exp", g), J + 1)
                pool.wait_ge(sg("a_ready", g), J + OPEN)
                pool.wait_ge(sg("pt_ready", g), J + OPEN)
                gp.tensor_tensor(units(e_b, g)[:, :, 1:P + 1], units(e_raw, g),
                                 cg[:, g, 0].rearrange("p t v -> p (t v)").unsqueeze(2)
                                 .broadcast_to([P, GU, P]), ALU.mult).then_inc(sg("decay_beta", g), 1)

            def decay_rhs(g, J):
                pool.wait_ge(sg("decay_ps", g), J + OPEN)
                pool.wait_ge(sg("g_le_ready", g), J * G_LE_STEPS + CG_READY)
                gp.tensor_tensor(units(g_le, g), le[:].unsqueeze(1).broadcast_to([P, GU, P]),
                                 cg[:, g, 1].rearrange("p t v -> p (t v)").unsqueeze(2).broadcast_to([P, GU, P]),
                                 ALU.mult).then_inc(sg("g_le_ready", g), 1)

            def wo_low(j):
                pool.wait_ge(sig("wo_ready"), j * 3 + 2 + OPEN)
                gp.tensor_tensor(wo16[:, 1], wo_n[:], wo16[:, 0], ALU.subtract).then_inc(sig("wo_ready"), 1)

            def first_inverse(g, j):
                pool.wait_ge(sg("solve_ps", g), j * SOLVE_PS + OPEN)
                pool.wait_ge(sg("f_ready", g), j * 2 + 1 + OPEN)
                gp.tensor_tensor(units(invT, g), maskT1[:].unsqueeze(1).broadcast_to([P, GU, P]), units(f_hi, g),
                                 ALU.mult).then_inc(sg("f_ready", g), 1)

            def low_half(g, J):
                pool.wait_ge(sg("solve_ps", g), J * SOLVE_PS + OPEN)
                pool.wait_ge(sg("ahi_ready", g), J + 1)
                gp.tensor_tensor(units(a_lo, g), units(at, g), units(a_hi, g), ALU.subtract).then_inc(sg("alo_ready", g), 1)
                pool.wait_ge(sg("alo_ready", g), J * 2 + 1 + OPEN)
                pool.wait_ge(sg("f_ready", g), J * 2 + 1 + OPEN)
                gp.tensor_tensor(units(a_hi, g), units(a_hi, g), ident16[:].unsqueeze(1).broadcast_to([P, GU, P]),
                                 ALU.add).then_inc(sg("alo_ready", g), 1)

            def squares(g, J):
                pool.wait_ge(sg("conv_step", g), J * 12 + 6 + OPEN)
                pool.wait_ge(sg("ss_ps", g), J + OPEN)
                kq = cc[:, 0:2, g]
                gp.tensor_tensor(sq[:, g], kq, kq, ALU.mult).then_inc(sg("sq_ready", g), 1)

            def keep_rq(g, j):
                pool.wait_ge(sg("rn_ready", g), j + 1 + OPEN)
                pool.wait_ge(sg("osc_ready", g), j * 6 + OPEN)
                gp.tensor_tensor(rq[:, g], rn[:, g, 1], ones[:, 0:2], ALU.mult).then_inc(sg("osc_ready", g), 1)

            def norms(g, J, kept):
                pool.wait_ge(sg("osc_ready", g), kept + OPEN)
                pool.wait_ge(sg("ss_max", g), J + 1)
                pool.wait_ge(sg("kn_ready", g), J * 2 + OPEN)
                gp.tensor_tensor(rn[:, g], n2[:, g], mhalf[:, 0:4].rearrange("p (b t) -> p b t", b=2),
                                 ALU.pow).then_inc(sg("rn_ready", g), 1)

            def gate_output(g, j):
                pool.wait_ge(sg("o0_ready", g), j + 1)
                pool.wait_ge(sg("o1_ready", g), j + 1 + OPEN)
                pool.wait_ge(sg("z_gate", g), j * 2 + 1 + OPEN)
                zo = zg[:, CH * g:CH * g + CH].rearrange("p t v d -> p (t v) d")
                gp.tensor_tensor(zo, o[:, CH * g:CH * g + CH].rearrange("p t v d -> p (t v) d"), zo,
                                 ALU.mult).then_inc(sg("z_gate", g), 1)

            def output_scale(g, j):
                pool.wait_ge(sg("osc_ready", g), j * 6 + 1 + OPEN)
                pool.wait_ge(sg("oss_ready", g), j + 1 + OPEN)
                pool.wait_ge(sg("go_ready", g), j * 4 + OPEN)
                qn = rq[:, g].unsqueeze(2).broadcast_to([P, CH, PV])
                ow = osc[:, g]
                gp.tensor_tensor(ow[:, 0], oss[:, g], qn, ALU.mult).then_inc(sg("osc_ready", g), 1)
                pool.wait_ge(sg("osc_ready", g), j * 6 + 2 + OPEN)
                gp.tensor_tensor(ow[:, 1], ow[:, 0], qn, ALU.mult).then_inc(sg("osc_ready", g), 1)
                pool.wait_ge(sg("osc_ready", g), j * 6 + 3 + OPEN)
                gp.tensor_tensor(ow[:, 2], ow[:, 1], eps[:, 1, 0:GU].rearrange("p (t v) -> p t v", v=PV),
                                 ALU.add).then_inc(sg("osc_ready", g), 1)
                pool.wait_ge(sg("osc_ready", g), j * 6 + 4 + OPEN)
                gp.tensor_tensor(ow[:, 0], ow[:, 2], mhalf[:, 0:GU].rearrange("p (t v) -> p t v", v=PV),
                                 ALU.pow).then_inc(sg("osc_ready", g), 1)
                pool.wait_ge(sg("osc_ready", g), j * 6 + 5 + OPEN)
                gp.tensor_tensor(ow[:, 3], ow[:, 0], qn, ALU.mult).then_inc(sg("osc_ready", g), 1)

            def start(j, bp):
                decay_rhs(0, j)
                decay_rhs(1, j)
                decays(0, j)
                decays(1, j)
                squares(0, j)
                norms(0, j, j * 6)
                squares(1, j)
                first_inverse(0, j)
                low_half(0, j)

            def half(h, j, kh, first, last):
                g, js = 1 - h, j - 1 + h
                if h == 0 and not first:
                    wo_low(j - 1)
                if h == 1 or not first:
                    keep_rq(g, js)
                    if h == 0 or not last:
                        norms(g, js + 1, js * 6 + 1)
                else:
                    norms(g, js + 1, (js + 1) * 6)
                if not last:
                    decay_rhs(h, j + 1)
                    squares(h, j + 1)
                if h == 1 or not first:
                    gate_output(g, js)
                    output_scale(g, js)
                if not last:
                    decays(h, j + 1)
                if h == 0 or not last:
                    first_inverse(g, js + 1)
                    low_half(g, js + 1)

            def finish(j):
                wo_low(j)
                keep_rq(1, j)
                gate_output(1, j)
                output_scale(1, j)

            def whole_block(bp, last):
                schedule(pool, bp, start, half, finish)
                layernorm_rstd(bp * 2 + 1)
                if not last:
                    layernorm_rstd(bp * 2 + 2)

            layernorm_rstd(0)
            with pool.Fori(0, NB - 1) as bp:
                whole_block(bp, False)
            whole_block(NB - 1, True)

        @block.tensor
        def _(pe):
            mm = nc.tensor.matmul

            def m(o_, l_, r_, start=True, stop=True):
                return mm(o_, l_, r_, start=start, stop=stop, skip_group_check=True)

            pe.wait_ge(sig("blockrows_ready"), len(LEVELS))
            for i in range(len(LEVELS)):
                ins = m(bank[i // 4][:, P * (i % 4):P * (i % 4) + P], blockrows[:, i, :], blockrows[:, i, :])
            ins.then_inc(sig("same_ps"), 1)
            pe.wait_ge(sig("setup_dma"), 96)
            m(bank[2][:, 0:2 * NV], ones[0:1, :], rows[:]).then_inc(sig("rows_ps"), 1)
            pe.wait_ge(sig("silu_c"), 4)
            for i in range(6):
                for k in range(CK):
                    for kk in range(CK):
                        ins = m(bank[3][:, (k * 6 + i) * B:(k * 6 + i + 1) * B],
                                wmod_sb[:, kk, i * C + k * P:i * C + k * P + P], silu_c[:, kk, :],
                                start=(kk == 0), stop=(kk == CK - 1))
            ins.then_inc(sig("mod_ps"), 1)
            for b in range(B):
                if b >= 2:
                    pe.wait_ge(sig("gates_ready"), 2 * (b - 1))
                for h, i in enumerate((2, 5)):
                    for kk in range(CK):
                        ins = m(bank[4 + b % 2][:, h * C:h * C + C], silu_cb[:, kk, b, :],
                                wmod_sb[:, kk, i * C:i * C + C], start=(kk == 0), stop=(kk == CK - 1))
                ins.then_inc(sig("gates_ps"), 1)

            def transpose_norm(k, n):
                if k == 0:
                    pe.wait_ge(sig("xn_ready"), n * TL + TL)
                else:
                    pe.wait_ge(sig("hT_ready"), n * 4 + 2 + OPEN)
                for t in range(TL):
                    ins = nc.tensor.transpose(bank[1][:, t * P:t * P + P], xn[:, t, k * P:k * P + P], ident[:])
                ins.then_inc(sig("xnT_ps"), 1)

            def beta_product(bp):
                pe.wait_ge(sig("hT_ready"), bp * 8 + 4 + OPEN)
                for t in range(TL):
                    for k in range(CK):
                        ins = m(bank[1][:, t * 2 * NV:(t + 1) * 2 * NV], hT[:, k, t * P:t * P + P], wba_sb[:, k, :],
                                start=(k == 0), stop=(k == CK - 1))
                ins.then_inc(sig("ba_ps"), 1)

            def cumulate(bp):
                pe.wait_ge(sig("g_ready"), bp + 1)
                gl = cols[:, GLOG].rearrange("p t h -> p (t h)")
                m(bank[1][:, 0:P], le[:], gl)
                m(bank[1][:, P:2 * P], lt[:], gl)
                m(bank[1][:, 2 * P:3 * P], gt[:], gl).then_inc(sig("cum_ps"), 1)

            def open_y(bp):
                pe.wait_ge(sig("f_h_ready"), bp * TL * 2 + OPEN)
                pe.wait_ge(sig("yo_mul"), bp * TL + OPEN)
                pe.wait_ge(sig("cum_exp"), bp + 1)
                for g in range(BG):
                    m(bank_y[g][:], zero16[:, 0:P], zero16[:])

            def split_product(out_, left_, right_, start=True, stop=True):
                steps = [(l_, r_, a, b) for l_, r_ in zip(left_, right_) for a, b in ((0, 0), (0, 1), (1, 0))]
                for n_, (l_, r_, a, b) in enumerate(steps):
                    ins = m(out_, l_[:, a, :], r_[:, b, :], start=start and n_ == 0,
                            stop=stop and n_ == len(steps) - 1)
                return ins

            def decay_product(g, J, banks=bank_p):
                pe.wait_ge(sg("g_le_ready", g), J * G_LE_STEPS + G_LE_DONE)
                m(banks[1][:], gt[:], units(g_le, g).rearrange("p u s -> p (u s)"), stop=False)
                m(grid(banks[1][:]), ident16[:], neg16[:].unsqueeze(1).broadcast_to([P, GU, P]),
                  start=False).then_inc(sg("decay_ps", g), 1)

            def project(i, g, J, banks=bank_p):
                if i == 0:
                    pe.wait_ge(sig("wq_split"), J * 3 + 3 + OPEN)
                elif i >= 2:
                    pe.wait_ge(sg("conv_step", g), J * 12 + 3 * (i - 1) + OPEN)
                ins = split_product(banks[1 - i % 2][:, 0:T],
                                    [wq16[:, :, c * NQ + i * P:c * NQ + i * P + P] for c in range(CK)],
                                    [h16[:, :, c, g * T:g * T + T] for c in range(CK)])
                ins.then_inc(sg("proj_ps", g), 1)

            def sum_squares(g, J, banks=bank_p):
                pe.wait_ge(sg("conv_step", g), J * 12 + 12 + OPEN)
                pe.wait_ge(sg("sq_ready", g), J + 1 + OPEN)
                for b in range(2):
                    for c in range(CH):
                        ins = m(banks[0][:, b * CH + c:b * CH + c + 1], sq[:, g, b, c * P:c * P + P], ones[:, 0:1])
                ins.then_inc(sg("ss_ps", g), 1)

            def z_rows(c, g, j):
                if c == 0:
                    pe.wait_ge(sig("wz_split"), j * 2 + 2 + OPEN)
                t = CH * g + c
                ins = split_product(bank_p[1][:, c * 256:c * 256 + 256],
                                    [h16[:, :, k, t * P:t * P + P] for k in range(CK)],
                                    [wz16[:, :, k, :] for k in range(CK)])
                if c == CH - 1:
                    ins.then_inc(sg("z_ps", g), 1)

            def turn_output(g, j, bk):
                pe.wait_ge(sg("go_ready", g), j * 4 + 4 + OPEN)
                for i in range(GU):
                    ins = nc.tensor.transpose(bk[:, i * P:i * P + P], go[:, CH * g + i // PV, i % PV, :], ident[:])
                ins.then_inc(sg("goT_ps", g), 1)

            def sum_output(c, g, j):
                if c == 0:
                    pe.wait_ge(sig("wo_ready"), j * 3 + 3 + OPEN)
                    pe.wait_ge(sg("goT_ready", g), j * 2 + 2 + OPEN)
                ins = split_product(bank_y[g][:, c * C:c * C + C],
                                    [goT16[:, :, GU * g + c * PV + p_, :] for p_ in range(PV)],
                                    [wo16[:, :, p_, :] for p_ in range(PV)], start=False, stop=False)
                if c == CH - 1:
                    ins.then_inc(sg("y_sum", g), 1)

            def level(s, g, j):
                l = s // 2
                bA, bB = bank_a[g], bank_b[g]
                if s % 2 == 0:
                    if l == 0:
                        pe.wait_ge(sg("x1_ready", g), j + 1)
                    else:
                        pe.wait_ge(sg("x_ready", g), j * 6 + l)
                    for i in range(GU):
                        ins = m(bA[:, i * HP:i * HP + HP], units(f_hi, g)[:, i, :], left(units(inv, g)[:, i, :], l))
                    ins.then_inc(sg("y_ps", g), 1)
                else:
                    if l == 0:
                        pe.wait_ge(sg("f_ready", g), j * 2 + 2 + OPEN)
                        pe.wait_ge(sg("pt_ready", g), j + 1 + OPEN)
                    else:
                        pe.wait_ge(sg("xt_ready", g), j * 6 + l)
                    pe.wait_ge(sg("ym_ready", g), j * 6 + l + 1)
                    for i in range(GU):
                        ins = m(bA[:, i * HP:i * HP + HP], units(invT, g)[:, i, :], left(yl[:, l, i, :], l))
                    ins.then_inc(sg("level_ps", g), 1)
                    for i in range(GU):
                        ins = m(bB[:, i * HP:i * HP + HP], yl[:, l, i, :], right(units(invT, g)[:, i, :], l))
                    ins.then_inc(sg("level_ps", g), 1)

            def solve(s, g, j):
                bA, bB = bank_a[g], bank_b[g]
                if s == 0:
                    pe.wait_ge(sg("x_ready", g), j * 6 + 6)
                    pe.wait_ge(sg("alo_ready", g), j * 2 + 2 + OPEN)
                    for i in range(GU):
                        o_, xi = bA[:, i * P:i * P + P], units(inv, g)[:, i, :]
                        m(o_, units(a_hi, g)[:, i, :], xi, stop=False)
                        ins = m(o_, units(a_lo, g)[:, i, :], xi, start=False)
                    ins.then_inc(sg("solve_ps", g), 1)
                elif s == 1:
                    pe.wait_ge(sg("xt_ready", g), j * 6 + 6)
                    pe.wait_ge(sg("h_ready", g), j + 1)
                    for i in range(GU):
                        ins = m(bB[:, i * P:i * P + P], units(ym, g)[:, i, :], units(invT, g)[:, i, :])
                    ins.then_inc(sg("solve_ps", g), 1)
                elif s == 2:
                    pe.wait_ge(sg("t_ready", g), j + 1)
                    for p_ in range(PV):
                        ins = m(bA[:, p_ * P:p_ * P + P], tt[:, GU * g + p_, :], v[:, CH * g, p_, :])
                    ins.then_inc(sg("solve_ps", g), 1)
                elif s == 3:
                    pe.wait_ge(sg("us_ready", g), j * 2 + 2 + OPEN)
                    m(bB[:, 0:256], kn[:, g, 0], us[:, g].rearrange("p v d -> p (v d)")).then_inc(sg("solve_ps", g), 1)
                    pe.wait_ge(sg("u0_ready", g), j + 1)
                    for p_ in range(PV):
                        ins = m(bA[:, 256 + p_ * P:256 + p_ * P + P], pt[:, GU * g + p_, :], u0[:, g, p_, :])
                    ins.then_inc(sg("solve_ps", g), 1)
                elif s == 4:
                    pe.wait_ge(sg("s_ready", g), j + 1)
                    m(bB[:, 0:256], knT[:, g, P:2 * P], st[:, g])
                    m(bB[:, 256:512], qT[:, g, P:2 * P], st[:, g]).then_inc(sg("solve_ps", g), 1)
                elif s == 5:
                    pe.wait_ge(sg("o0_ready", g), j + 1)
                    pe.wait_ge(sg("r_ready", g), j * 2 + 2 + OPEN)
                    for p_ in range(PV):
                        ins = m(bA[:, p_ * P:p_ * P + P], tt[:, GU * g + PV + p_, :], rr[:, g, p_, :])
                    ins.then_inc(sg("solve_ps", g), 1)
                elif s == 6:
                    pe.wait_ge(sg("u1_ready", g), j + 1)
                    for p_ in range(PV):
                        ins = m(bA[:, 256 + p_ * P:256 + p_ * P + P], pt[:, GU * g + PV + p_, :], u1[:, g, p_, :])
                    ins.then_inc(sg("solve_ps", g), 1)

            def begin(s, g, j):
                bA, bB = bank_a[g], bank_b[g]
                if s == 7:
                    pe.wait_ge(sg("conv_step", g), j * 12 + 12 + OPEN)
                    pe.wait_ge(sg("qs_ready", g), j * 2 + OPEN)
                    for c in range(CH):
                        ins = nc.tensor.transpose(bB[:, c * P:c * P + P], cc[:, 0, g, c * P:c * P + P], ident[:])
                    ins.then_inc(sg("begin_ps", g), 1)
                    pe.wait_ge(sg("o1_ready", g), j + OPEN)
                    for c in range(CH):
                        for p_ in range(PV):
                            n_ = c * PV + p_
                            ins = nc.tensor.transpose(bA[:, n_ * P:n_ * P + P], cc[:, 2 + p_, g, c * P:c * P + P], ident[:])
                    ins.then_inc(sg("begin_ps", g), 1)
                elif s == 8:
                    pe.wait_ge(sg("kn_ready", g), j * 2 + 2 + OPEN)
                    for c in range(CH):
                        ins = nc.tensor.transpose(bB[:, 256 + c * P:256 + c * P + P], kn[:, g, c], ident[:])
                    ins.then_inc(sg("begin_ps", g), 1)
                elif s == 9:
                    pe.wait_ge(sg("knT_ready", g), j + 1)
                    for c in range(CH):
                        k_ = knT[:, g, c * P:c * P + P]
                        m(bB[:, c * P:c * P + P], k_, k_)
                    pe.wait_ge(sg("q_copied", g), j + 1 + OPEN)
                    for c in range(CH):
                        ins = m(bB[:, 256 + c * P:256 + c * P + P], knT[:, g, c * P:c * P + P], qT[:, g, c * P:c * P + P])
                    ins.then_inc(sg("begin_ps", g), 1)
                elif s == 10:
                    pe.wait_ge(sg("v_ready", g), j + 1)
                    pe.wait_ge(sg("f_ready", g), j * 2 + 1 + OPEN)
                    for i in range(GU):
                        ins = m(bA[:, i * P:i * P + P], units(f_hi, g)[:, i, :], ident16[:])
                    ins.then_inc(sg("begin_ps", g), 1)

            def before_start(bp):
                pe.wait_ge(sig("f_h_ready"), bp * TL * 2 + OPEN)
                decay_product(0, bp * NK)
                pe.wait_ge(sig("h_split"), bp * 2 + 2)
                pe.wait_ge(sg("decay_exp", 0), bp * NK + 1)
                for i in range(2):
                    project(i, 0, bp * NK)

            def start(j, bp):
                decay_product(1, j, start_banks[1])
                project(2, 0, j)
                project(3, 0, j)
                pe.wait_ge(sg("decay_exp", 1), j + 1)
                for i in range(2):
                    project(i, 1, j, start_banks[1])
                sum_squares(0, j)
                begin(7, 0, j)
                project(2, 1, j, start_banks[1])
                begin(8, 0, j)
                begin(9, 0, j)
                project(3, 1, j, start_banks[1])
                begin(10, 0, j)
                sum_squares(1, j, start_banks[1])
                pe.wait_ge(sg("ss_max", 1), j + 1)

            def half(h, j, kh, first, last):
                g, js = 1 - h, j - 1 + h

                def beside(n):
                    if n == PE_AT["project_0"]:
                        if h == 0 and first:
                            pe.wait_ge(sg("conv_step", 1), j * 12 + 12 + OPEN)
                        else:
                            pe.wait_ge(sg("z_gate", g), js * 2 + 1 + OPEN)
                        if not last:
                            project(0, h, j + 1)
                    if n == PE_AT["turn"] and not first:
                        if h == 1 and last:
                            pe.wait_ge(sg("goT_ready", 0), j * 2 + OPEN)
                        else:
                            pe.wait_ge(sg("ss_max", g), js + 2)
                        turn_output(h, j - 1, bank_p[0])
                    if n == PE_AT["project_1"] and not last:
                        if first:
                            pe.wait_ge(sg("ss_max", g), js + 2)
                        else:
                            pe.wait_ge(sg("goT_ready", h), j * 2 + OPEN)
                        project(1, h, j + 1)
                    if n == PE_AT["project_2"] and not last:
                        project(2, h, j + 1)
                    if n == PE_AT["y_0"] and not first:
                        sum_output(0, h, j - 1)
                    if n == PE_AT["project_3"] and not last:
                        project(3, h, j + 1)
                    if n == PE_AT["y_1"] and not first:
                        sum_output(1, h, j - 1)
                    if n == PE_AT["decays"] and not last:
                        pe.wait_ge(sg("conv_step", h), (j + 1) * 12 + 9 + OPEN)
                        decay_product(h, j + 1)
                    if n == PE_AT["sum_squares"] and not last:
                        sum_squares(h, j + 1)
                    if n == PE_AT["z_0"]:
                        if not last:
                            pe.wait_ge(sg("decay_exp", h), j + 2)
                        z_rows(0, h, j)
                    if n == PE_AT["z_1"]:
                        z_rows(1, h, j)

                for s in range(SLOTS):
                    level(s, h, j)
                    beside(2 * s)
                    if h == 1 or not first:
                        solve(s, g, js)
                    if h == 0 or not last:
                        begin(s, g, js + 1)
                    beside(2 * s + 1)

            def finish(j):
                for s in range(SLOTS):
                    solve(s, 1, j)
                    if s == 2:
                        pe.wait_ge(sg("goT_ready", 1), j * 2 + OPEN)
                        turn_output(0, j, bank_p[0])
                    if s == 6:
                        sum_output(0, 0, j)
                        sum_output(1, 0, j)
                pe.wait_ge(sg("goT_ready", 0), j * 2 + 2 + OPEN)
                turn_output(1, j, bank_p[0])
                sum_output(0, 1, j)
                sum_output(1, 1, j)

            def gate_up(bp, t):
                n_ = bp * TL + t
                pe.wait_ge(sig("f_h_ready"), n_ * 2 + OPEN)
                for w_, bk in ((wg_sb, (bank[2], bank[3])), (wu_sb, (bank[4], bank[5]))):
                    for hf in range(2):
                        for k in range(CK):
                            ins = m(bk[hf][:], h_ffn[:, k, t * P:t * P + P], w_[:, k, hf * 512:hf * 512 + 512],
                                    start=(k == 0), stop=(k == CK - 1))
                ins.then_inc(sig("gu_ps"), 1)

            def down(bp, t):
                n_ = bp * TL + t
                pe.wait_ge(sig("f_s_ready"), n_ * 4 + 4 + OPEN)
                pe.wait_ge(sig("f_sT_ready"), n_ * 2 + OPEN)
                for hf in range(2):
                    for i in range(4):
                        c_ = (hf * 4 + i) * P
                        ins = nc.tensor.transpose(bank[6 + hf][:, i * P:i * P + P], f_s[:, c_:c_ + P], ident[:])
                    ins.then_inc(sig("f_sT_ps"), 1)
                pe.wait_ge(sig("f_sT_ready"), n_ * 2 + 2 + OPEN)
                pe.wait_ge(sig("x2_ready"), bp * TL + TL + OPEN)
                pe.wait_ge(sig("yo_mul"), n_ + OPEN)
                for i in range(FF // P):
                    ins = m(bank[0][:, 0:C], f_sT[:, i, :], wd_sb[:, i, :], start=(i == 0), stop=(i == FF // P - 1))
                ins.then_inc(sig("down_ps"), 1)

            pe.wait_ge(sig("gates_ready"), 2 * B)
            pe.wait_ge(sig("rows_ready"), 2)
            pe.wait_ge(sig("modT_ready"), 1)
            pe.wait_ge(sig("same_ready"), len(LEVELS))
            pe.wait_ge(sig("ffn_w_dma"), 48)

            def whole_block(bp, last):
                open_y(bp)
                schedule(pe, bp, start, half, finish)
                transpose_norm(0, bp * 2 + 1)
                transpose_norm(1, bp * 2 + 1)
                pe.wait_ge(sig("hT_ready"), bp * 8 + 8 + OPEN)
                gate_up(bp, 0)
                for t in range(TL):
                    if t + 1 < TL:
                        gate_up(bp, t + 1)
                    if not last and t == 0:
                        transpose_norm(0, bp * 2 + 2)
                    if not last and t == 1:
                        beta_product(bp + 1)
                    if not last and t == 2:
                        cumulate(bp + 1)
                    if not last and t == 3:
                        before_start(bp + 1)
                    down(bp, t)
                    if not last and t == 0:
                        transpose_norm(1, bp * 2 + 2)

            transpose_norm(0, 0)
            transpose_norm(1, 0)
            beta_product(0)
            cumulate(0)
            before_start(0)
            with pe.Fori(0, NB - 1) as bp:
                whole_block(bp, False)
            whole_block(NB - 1, True)

        @block.scalar
        def _(act):
            A = nc.scalar.activation

            act.dma_start(wg_sb[:], wgate).then_inc(sig("ffn_w_dma"), 16)
            act.dma_start(wu_sb[:], wup).then_inc(sig("ffn_w_dma"), 16)
            act.dma_start(wd_sb[:], wdown).then_inc(sig("ffn_w_dma"), 16)
            act.wait_ge(sig("setup_dma"), 96)
            A(c_th[:], cT_sb[:], ACT.Tanh, scale=0.5).then_inc(sig("silu_c"), 1)
            act.wait_ge(sig("rows_ps"), 1)
            A(expA[:], bank[2][:, NV:2 * NV], ACT.Exp).then_inc(sig("rows_ready"), 1)
            A(dtb_b[:], bank[2][:, 0:NV], ACT.Copy).then_inc(sig("rows_ready"), 1)

            def h_half(k, n, dst, which):
                act.wait_ge(sig("modc_ready"), n + 1)
                act.wait_ge(sig("xnT_ps"), n * 2 + k + 1 + OPEN)
                for g in range(BG):
                    A(dst[:, k, g * T:g * T + T], bank[1][:, g * T:g * T + T], ACT.Identity,
                      scale=modc[:, k * 6 + which + 1, g:g + 1],
                      bias=modc[:, k * 6 + which, g:g + 1]).then_inc(sig("hT_ready"), 1)

            def h_high(bp):
                act.wait_ge(sig("hT_ready"), bp * 8 + 4 + OPEN)
                act.wait_ge(sg("z_ps", 1), bp * NK + OPEN)
                A(h16[:, 0], hT[:], ACT.Copy).then_inc(sig("h_split"), 1)

            def beta_exp(bp):
                act.wait_ge(sig("ba_neg"), bp * 2 + 2)
                A(ba_t[:, 0], ba_t[:, 1], ACT.Exp).then_inc(sig("ba_exp"), 1)
                A(ba_t[:, 2], ba[:, :, 0:NV], ACT.Exp, scale=-1.0).then_inc(sig("ba_exp"), 1)
                act.wait_ge(sig("ba_exp"), bp * 2 + 1)
                A(ba_t[:, 1], ba_t[:, 0], ACT.Ln, bias=1.0).then_inc(sig("ba_ln"), 1)

            def cumulated_exp(bp):
                act.wait_ge(sig("cum_ps"), bp + 1)
                act.wait_ge(sg("ck_ready", 1), bp * NK + OPEN)
                cum = bank[1][:, 0:3 * P].rearrange("p (k t h) -> p k t h", k=3, t=TL)
                A(cols[:, EG:EG + 3], cum, ACT.Exp).then_inc(sig("cum_exp"), 1)

            def wq_high(J):
                act.wait_ge(sig("wq_dma"), J * 16 + 16)
                act.wait_ge(sg("proj_ps", 1), J * 4 + OPEN)
                A(wq16[:, 0], wq_sb[:, 0:CK * NQ], ACT.Copy, scale=W_SCALE).then_inc(sig("wq_split"), 1)

            def wz_high(j):
                act.wait_ge(sig("wz_dma"), j * 16 + 16)
                act.wait_ge(sg("z_ps", 1), j + OPEN)
                A(wz16[:, 0], wz_sb[:], ACT.Copy, scale=Z_SCALE).then_inc(sig("wz_split"), 1)

            def wo_high(j):
                act.wait_ge(sig("wo_ready"), j * 3 + 1 + OPEN)
                act.wait_ge(sg("y_sum", 1), j + OPEN)
                A(wo16[:, 0], wo_n[:], ACT.Copy).then_inc(sig("wo_ready"), 1)

            def decay_exp(g, J, banks=bank_p):
                act.wait_ge(sg("decay_ps", g), J + 1 + OPEN)
                act.wait_ge(sg("decay_beta", g), J + OPEN)
                A(units(e_raw, g), grid(banks[1][:]), ACT.Exp).then_inc(sg("decay_exp", g), 1)

            def last_tap(i, g, J, banks=bank_p):
                act.wait_ge(sg("proj_ps", g), J * 4 + i + 1 + OPEN)
                if i == 0:
                    act.wait_ge(sg("begin_ps", g), J * BEGIN_PS + OPEN)
                    act.wait_ge(sg("sq_ready", g), J + OPEN)
                elif i == 1:
                    act.wait_ge(sg("q_copied", g), J + OPEN)
                else:
                    act.wait_ge(sg("begin_ps", g), J * BEGIN_PS + OPEN)
                A(cc[:, i, g], banks[1 - i % 2][:, 0:T], ACT.Copy, scale=wc[:, i, 3:4]).then_inc(sg("tap_last", g), 1)

            def z_tanh(g, j):
                act.wait_ge(sg("z_ps", g), j + 1 + OPEN)
                act.wait_ge(sg("z_gate", g), j * 2 + OPEN)
                A(zth[:, CH * g:CH * g + CH].rearrange("p t d -> p (t d)"), bank_p[1][:], ACT.Tanh,
                  scale=0.5 / Z_SCALE).then_inc(sg("z_tanh", g), 1)

            def output_turned(g, j, bk):
                act.wait_ge(sg("goT_ps", g), j + 1 + OPEN)
                act.wait_ge(sg("y_sum", g), j + OPEN)
                A(units(goT16[:, 0], g), grid(bk[:]), ACT.Copy).then_inc(sg("goT_ready", g), 1)

            def level(s, g, j):
                l = s // 2
                if s % 2:
                    act.wait_ge(sg("level_ps", g), j * 12 + 2 * l + 1)
                    A(lefts(units(inv, g), l), halves(bank_a[g], l), ACT.Copy).then_inc(sg("x_ready", g), 1)
                    act.wait_ge(sg("level_ps", g), j * 12 + 2 * l + 2)
                    A(rights(units(invT, g), l), halves(bank_b[g], l), ACT.Copy).then_inc(sg("xt_ready", g), 1)

            def flat(ap):
                return ap.rearrange("p v d -> p (v d)")

            def solve(s, g, j):
                bA, bB = bank_a[g], bank_b[g]
                if s == 1:
                    act.wait_ge(sg("solve_ps", g), j * SOLVE_PS + T_PS + OPEN)
                    A(units(tt, g), grid(bB[:]), ACT.Copy).then_inc(sg("t_ready", g), 1)
                elif s == 2:
                    act.wait_ge(sg("ck_ready", g), j + 1 + OPEN)
                    act.wait_ge(sg("solve_ps", g), j * SOLVE_PS + U0_PS + OPEN)
                    for p_ in range(PV):
                        A(us[:, g, p_], bA[:, p_ * P:p_ * P + P], ACT.Copy,
                          scale=ck[:, g, BSUF, 0, p_:p_ + 1]).then_inc(sg("us_ready", g), 1)
                    A(flat(u0[:, g]), bA[:, 0:256], ACT.Copy).then_inc(sg("u0_ready", g), 1)
                elif s == 3:
                    act.wait_ge(sg("solve_ps", g), j * SOLVE_PS + S_PS + OPEN)
                    A(st[:, g], bB[:, 0:256], ACT.Copy).then_inc(sg("s_ready", g), 1)
                    act.wait_ge(sg("go_ready", g), j * 4 + OPEN)
                    act.wait_ge(sg("solve_ps", g), j * SOLVE_PS + O0_PS + OPEN)
                    A(flat(o[:, CH * g]), bA[:, 256:512], ACT.Copy).then_inc(sg("o0_ready", g), 1)
                elif s == 4:
                    act.wait_ge(sg("o1_ready", g), j + OPEN)
                    act.wait_ge(sg("r_ready", g), j * 2 + 2 + OPEN)
                    for p_ in range(PV):
                        A(qs[:, g, p_], bB[:, 256 + p_ * P:256 + p_ * P + P], ACT.Copy,
                          scale=ck[:, g, EG, 1, p_:p_ + 1]).then_inc(sg("qs_ready", g), 1)
                elif s == 5:
                    act.wait_ge(sg("solve_ps", g), j * SOLVE_PS + U1_PS + OPEN)
                    A(flat(u1[:, g]), bA[:, 0:256], ACT.Copy).then_inc(sg("u1_ready", g), 1)
                elif s == 6:
                    act.wait_ge(sg("o0_ready", g), j + 1)
                    act.wait_ge(sg("oss_ready", g), j + OPEN)
                    act.wait_ge(sg("o1_ready", g), j + 1 + OPEN)
                    A(units(osq, g), o[:, CH * g:CH * g + CH].rearrange("p t v d -> p (t v) d"),
                      ACT.Square).then_inc(sg("osq_ready", g), 1)
                elif s == 10:
                    act.wait_ge(sg("goT_ps", g), j + OPEN)
                    act.wait_ge(sg("z_gate", g), j * 2 + 2 + OPEN)
                    act.wait_ge(sg("osc_ready", g), j * 6 + 6 + OPEN)
                    for c in range(CH):
                        for p_ in range(PV):
                            t = CH * g + c
                            A(go[:, t, p_], zg[:, t, p_], ACT.Copy,
                              scale=osc[:, g, 3, c, p_:p_ + 1]).then_inc(sg("go_ready", g), 1)

            def begin(s, g, j):
                bA, bB = bank_a[g], bank_b[g]
                if s == 7:
                    act.wait_ge(sg("solve_ps", g), j * SOLVE_PS + OPEN)
                    act.wait_ge(sg("rn_ready", g), j + 1 + OPEN)
                    act.wait_ge(sg("begin_ps", g), j * BEGIN_PS + KT_PS + OPEN)
                    for c in range(CH):
                        A(kn[:, g, c], bB[:, c * P:c * P + P], ACT.Copy,
                          scale=rn[:, g, 0, c:c + 1]).then_inc(sg("kn_ready", g), 1)
                elif s == 8:
                    act.wait_ge(sg("solve_ps", g), j * SOLVE_PS + OPEN)
                    act.wait_ge(sg("begin_ps", g), j * BEGIN_PS + KNT_PS + OPEN)
                    A(knT[:, g], bB[:, 256:512], ACT.Copy).then_inc(sg("knT_ready", g), 1)
                    act.wait_ge(sg("solve_ps", g), j * SOLVE_PS + OPEN)
                    act.wait_ge(sg("conv_step", g), j * 12 + 12 + OPEN)
                    A(qT[:, g], cc[:, 1, g], ACT.Copy).then_inc(sg("q_copied", g), 1)
                    act.wait_ge(sg("begin_ps", g), j * BEGIN_PS + VT_PS + OPEN)
                    act.wait_ge(sg("solve_ps", g), j * SOLVE_PS + OPEN)
                    act.wait_ge(sg("r_ready", g), j * 2 + OPEN)
                    A(v[:, CH * g:CH * g + CH].rearrange("p t v d -> p (t v d)"), bA[:], ACT.Copy).then_inc(sg("v_ready", g), 1)
                elif s == 9:
                    act.wait_ge(sg("solve_ps", g), j * SOLVE_PS + OPEN)
                    act.wait_ge(sg("f_ready", g), j * 2 + OPEN)
                    act.wait_ge(sg("alo_ready", g), j * 2 + OPEN)
                    act.wait_ge(sg("a_ready", g), j + 1 + OPEN)
                    A(units(a_hi, g), units(at, g), ACT.Copy).then_inc(sg("ahi_ready", g), 1)

            def before_start(j):
                decay_exp(0, j)
                for i in range(2):
                    last_tap(i, 0, j)

            def start(j, bp):
                decay_exp(1, j, start_banks[1])
                for i in range(2, QKV_BLK):
                    last_tap(i, 0, j)
                for i in range(2):
                    last_tap(i, 1, j, start_banks[1])
                begin(7, 0, j)
                last_tap(2, 1, j, start_banks[1])
                begin(8, 0, j)
                begin(9, 0, j)
                last_tap(3, 1, j, start_banks[1])
                begin(10, 0, j)

            def half(h, j, kh, first, last):
                g, js = 1 - h, j - 1 + h

                def beside(n):
                    if n == ACT_AT["z_tanh"] and (h == 1 or not first):
                        z_tanh(g, js)
                    if n == ACT_AT["wo_high"] and h == 0 and not first:
                        wo_high(j - 1)
                    if n == ACT_AT["wq_high"] and h == 0 and not last:
                        wq_high(j + 1)
                    if n == ACT_AT["wz_high"] and h == 0:
                        wz_high(j)
                    if n == ACT_AT["turned"] and not first:
                        output_turned(h, j - 1, bank_p[0])
                    for i in range(QKV_BLK):
                        if n == ACT_AT[f"tap_{i}"] and not last:
                            last_tap(i, h, j + 1)
                    if n == ACT_AT["decays"] and not last:
                        decay_exp(h, j + 1)

                for s in range(SLOTS):
                    level(s, h, j)
                    beside(2 * s)
                    if h == 1 or not first:
                        solve(s, g, js)
                    if h == 0 or not last:
                        begin(s, g, js + 1)
                    beside(2 * s + 1)

            def finish(j):
                for s in range(SLOTS):
                    solve(s, 1, j)
                    if s == 1:
                        z_tanh(1, j)
                    if s == 2:
                        wo_high(j)
                    if s == 3:
                        output_turned(0, j, bank_p[0])
                output_turned(1, j, bank_p[0])

            def gate_tanh(bp, t):
                n_ = bp * TL + t
                act.wait_ge(sig("gu_ps"), n_ + 1)
                act.wait_ge(sig("f_silu"), n_ * 2 + OPEN)
                for hf in range(2):
                    A(f_th[:, hf * 512:hf * 512 + 512], bank[2 + hf][:], ACT.Tanh,
                      scale=0.5).then_inc(sig("f_tanh"), 1)

            def whole_block(bp, last):
                schedule(act, bp, start, half, finish)
                for k in range(CK):
                    h_half(k, bp * 2 + 1, h_ffn, 3)
                gate_tanh(bp, 0)
                for t in range(TL):
                    n_ = bp * TL + t
                    if not last and t == 0:
                        h_half(0, bp * 2 + 2, hT, 0)
                    if not last and t == 2:
                        cumulated_exp(bp + 1)
                    if not last and t == 3:
                        before_start(bp * NK + NK)
                    act.wait_ge(sig("down_ps"), n_ + OPEN)
                    for hf in range(2):
                        act.wait_ge(sig("f_sT_ps"), n_ * 2 + hf + 1 + OPEN)
                        A(f_sT[:, 4 * hf:4 * hf + 4], grid(bank[6 + hf][:]), ACT.Copy).then_inc(sig("f_sT_ready"), 1)
                    if t + 1 < TL:
                        gate_tanh(bp, t + 1)
                    if not last and t == 0:
                        h_half(1, bp * 2 + 2, hT, 0)
                    if not last and t == 1:
                        beta_exp(bp + 1)
                    act.wait_ge(sig("yo_ready"), n_ + 1 + OPEN)
                    act.dma_start(out_t[bass.ds(bp, 1)].rearrange("a t p c -> p (a t) c")[:, t, :],
                                  yo[:]).then_inc(sig("out_dma"), 16)
                    if not last and t == 2:
                        h_high(bp + 1)
                        wq_high(bp * NK + NK)

            for k in range(CK):
                h_half(k, 0, hT, 0)
            h_high(0)
            beta_exp(0)
            cumulated_exp(0)
            wq_high(0)
            before_start(0)
            with act.Fori(0, NB - 1) as bp:
                whole_block(bp, False)
            whole_block(NB - 1, True)
            act.wait_ge(sig("out_dma"), NB * TL * 16 + OPEN)

        @block.vector
        def _(dve):
            V = nc.vector

            dve.wait_ge(sig("same_ps"), 1)
            dve.wait_ge(sig("same_ends"), 2)
            for i in range(len(LEVELS)):
                V.tensor_copy(same[:, i + 1, :], bank[i // 4][:, P * (i % 4):P * (i % 4) + P]).then_inc(sig("same_ready"), 1)
            dve.wait_ge(sig("same_ready"), len(LEVELS))
            for i in range(7):
                V.tensor_tensor(mask[:, i, :], same[:, i + 1, :], same[:, i, :], ALU.subtract).then_inc(sig("mask_steps"), 1)
            dve.wait_ge(sig("mask_steps"), 15)
            for i in range(7):
                V.tensor_tensor(mask[:, i, :], mask[:, i, :], ident16[:], ALU.add).then_inc(sig("mask_steps"), 1)
            dve.wait_ge(sig("silu_c"), 1)
            V.tensor_scalar(c_th[:], c_th[:], 1.0, 0.5, ALU.add, ALU.mult).then_inc(sig("silu_c"), 1)
            dve.wait_ge(sig("silu_c"), 2)
            V.tensor_tensor(silu_c[:], c_th[:], cT_sb[:], ALU.mult).then_inc(sig("silu_c"), 1)
            dve.wait_ge(sig("silu_c"), 3)
            V.tensor_copy(silu_cb[:].rearrange("p k b t -> p (k b) t"),
                          silu_c[:].rearrange("p k b -> p (k b)").unsqueeze(2).broadcast_to([P, CK * B, P])).then_inc(sig("silu_c"), 1)
            dve.wait_ge(sig("mod_ps"), 1)
            V.tensor_copy(modT[:], bank[3][:, 0:CK * 6 * B].rearrange("p (m b) -> p m b", b=B)).then_inc(sig("modT_ready"), 1)
            dve.wait_ge(sig("modT_ready"), 1)
            for k in range(CK):
                for i in (1, 4):
                    r = modT[:, k * 6 + i, :]
                    V.tensor_scalar(r, r, 1.0, None, ALU.add).then_inc(sig("modT_ready"), 1)
            for b in range(B):
                dve.wait_ge(sig("gates_ps"), b + 1)
                gp_ = bank[4 + b % 2][:]
                if b >= 1:
                    dve.wait_ge(sig("gates_ready"), 2 * b)
                V.tensor_copy(g_sb, gp_).then_inc(sig("gates_parts"), 1)
                V.tensor_scalar(g_sign, gp_, 0.0, 2.0, ALU.is_ge, ALU.mult).then_inc(sig("gates_parts"), 1)
                dve.wait_ge(sig("gates_parts"), 4 * b + 2)
                V.scalar_tensor_tensor(g_abs, g_sb, -1.0, g_sb, ALU.mult, ALU.max).then_inc(sig("gates_parts"), 1)
                V.tensor_scalar(g_sign, g_sign, -1.0, None, ALU.add).then_inc(sig("gates_parts"), 1)
                dve.wait_ge(sig("gates_parts"), 4 * b + 4)
                V.scalar_tensor_tensor(gates[:, b].rearrange("p h c -> p (h c)"), g_abs, GUARD, g_sign,
                                       ALU.max, ALU.mult).then_inc(sig("gates_ready"), 1)
                dve.wait_ge(sig("gates_ready"), 2 * b + 1)
                V.tensor_scalar(gates[:, b, 1], gates[:, b, 1], 0.5, None, ALU.mult).then_inc(sig("gates_ready"), 1)
            dve.wait_ge(sig("gates_ready"), 2 * B)
            dve.wait_ge(sig("mask_steps"), 22)
            dve.wait_ge(sig("modT_ready"), 5)
            for i in range(GU):
                V.tensor_copy(yl[:, :, i], ident16[:].unsqueeze(1).broadcast_to([P, len(LEVELS), P])).then_inc(sig("yl_ready"), 1)

            def layernorm(n, src, bp, x2_count):
                if x2_count is None:
                    dve.wait_ge(sig("x_dma"), bp * 16 + 16)
                else:
                    dve.wait_ge(sig("x2_ready"), x2_count + OPEN)
                for t in range(TL):
                    V.bn_stats(stats[:, t, :], src[:, t, :]).then_inc(sig("ln_stats"), 1)
                dve.wait_ge(sig("ln_stats"), n * TL + TL)
                dve.wait_ge(sig("hT_ready"), n * 4 + OPEN)
                V.tensor_scalar(modc[:], modT[:, :, bass.ds(bp * BG, BG)], 1.0, None,
                                ALU.mult).then_inc(sig("modc_ready"), 1)
                for t in range(TL):
                    V.bn_aggr(mv[:, t, :], stats[:, t, :]).then_inc(sig("ln_aggr"), 1)
                dve.wait_ge(sig("ln_rstd"), n + 1)
                dve.wait_ge(sig("xnT_ps"), n * 2 + OPEN)
                for t in range(TL):
                    V.tensor_scalar(xn[:, t, :], src[:, t, :], mv[:, t, 0:1], rstd[:, t:t + 1], ALU.subtract,
                                    ALU.mult).then_inc(sig("xn_ready"), 1)

            def beta_parts(bp):
                dve.wait_ge(sig("ba_ps"), bp + 1)
                V.tensor_copy(ba[:], bank[1][:, 0:TL * 2 * NV].rearrange("p (t h) -> p t h", t=TL)).then_inc(sig("ba_ready"), 1)
                dve.wait_ge(sig("ba_ready"), bp * 2 + 1)
                av = ba[:, :, NV:2 * NV]
                V.tensor_tensor(av, av, dtb_b[:].unsqueeze(1).broadcast_to([P, TL, NV]), ALU.add).then_inc(sig("ba_ready"), 1)
                dve.wait_ge(sig("ba_ready"), bp * 2 + 2)
                V.scalar_tensor_tensor(ba_t[:, 1], av, -1.0, av, ALU.mult, ALU.min).then_inc(sig("ba_neg"), 1)
                V.tensor_scalar(ba_t[:, 3], av, 0.0, None, ALU.max).then_inc(sig("ba_neg"), 1)

            def beta_and_g(bp):
                dve.wait_ge(sig("ba_exp"), bp * 2 + 2)
                V.tensor_scalar(ba_t[:, 2], ba_t[:, 2], 1.0, None, ALU.add).then_inc(sig("ba_one"), 1)
                dve.wait_ge(sig("ba_one"), bp + 1)
                V.reciprocal(cols[:, BETA], ba_t[:, 2]).then_inc(sig("beta_ready"), 1)
                dve.wait_ge(sig("ba_neg"), bp * 2 + 2)
                dve.wait_ge(sig("ba_ln"), bp + 1)
                V.tensor_tensor(ba_t[:, 3], ba_t[:, 3], ba_t[:, 1], ALU.add).then_inc(sig("dt_ready"), 1)
                dve.wait_ge(sig("dt_ready"), bp + 1)
                V.scalar_tensor_tensor(cols[:, GLOG], ba_t[:, 3], -1.0,
                                       expA[:].unsqueeze(1).broadcast_to([P, TL, NV]), ALU.mult,
                                       ALU.mult).then_inc(sig("g_ready"), 1)

            def decay_factors(bp):
                dve.wait_ge(sig("h_split"), bp * 2 + 1)
                V.tensor_tensor(h16[:, 1], hT[:], h16[:, 0], ALU.subtract).then_inc(sig("h_split"), 1)
                dve.wait_ge(sig("cum_exp"), bp + 1)
                V.tensor_scalar(cols[:, NEGP], cols[:, NEGP], -1.0, None, ALU.mult).then_inc(sig("cols_ready"), 1)
                dve.wait_ge(sig("beta_ready"), bp + 1)
                V.tensor_tensor(cols[:, BSUF], cols[:, BSUF], cols[:, BETA], ALU.mult).then_inc(sig("cols_ready"), 1)
                dve.wait_ge(sig("cols_ready"), bp * 2 + 2)
                dve.wait_ge(sig("g_ready"), bp + 1)

            def head_cols(g, kh, kinds):
                h0 = kh * PV
                hs = slice(h0, h0 + PV) if isinstance(kh, int) else bass.ds(h0, PV)
                return cols[:, 0:kinds, CH * g:CH * g + CH, hs]

            def decay_rhs(g, J, kh):
                dve.wait_ge(sg("decay_beta", g), J + OPEN)
                V.tensor_scalar(cg[:, g], head_cols(g, kh, 2), 1.0, None, ALU.mult).then_inc(sg("g_le_ready", g), 1)

            def wq_low(J):
                dve.wait_ge(sig("wq_split"), J * 3 + 1 + OPEN)
                V.scalar_tensor_tensor(wq16[:, 1], wq_sb[:, 0:CK * NQ], W_SCALE, wq16[:, 0], ALU.mult,
                                       ALU.subtract).then_inc(sig("wq_split"), 1)
                dve.wait_ge(sg("conv_step", 1), J * 12 + OPEN)
                V.tensor_scalar(wc[:], wconv, 1.0 / W_SCALE, None, ALU.mult).then_inc(sig("wq_split"), 1)

            def wz_low(j):
                dve.wait_ge(sig("wz_split"), j * 2 + 1 + OPEN)
                V.scalar_tensor_tensor(wz16[:, 1], wz_sb[:], Z_SCALE, wz16[:, 0], ALU.mult,
                                       ALU.subtract).then_inc(sig("wz_split"), 1)

            def turned_low(g, j):
                dve.wait_ge(sg("goT_ready", g), j * 2 + 1 + OPEN)
                V.tensor_tensor(units(goT16[:, 1], g), grid(bank_p[0][:]), units(goT16[:, 0], g),
                                ALU.subtract).then_inc(sg("goT_ready", g), 1)

            def convolution(i, g, J, banks=bank_p):
                dve.wait_ge(sg("tap_last", g), J * 4 + i + 1)
                for s in range(1, TAPS):
                    if s > 1:
                        dve.wait_ge(sg("conv_step", g), J * 12 + 3 * i + s - 1 + OPEN)
                    V.scalar_tensor_tensor(cc[:, i, g, s:T], banks[1 - i % 2][:, 0:T - s], wc[:, i, 3 - s:4 - s],
                                           cc[:, i, g, s:T], ALU.mult, ALU.add).then_inc(sg("conv_step", g), 1)

            def sum_squares(g, J, banks=bank_p):
                dve.wait_ge(sg("ss_ps", g), J + 1 + OPEN)
                dve.wait_ge(sg("rn_ready", g), J + OPEN)
                V.tensor_scalar(n2[:, g], banks[0][:, 0:2 * CH].rearrange("p (b t) -> p b t", b=2), EPS_K2, None,
                                ALU.max).then_inc(sg("ss_max", g), 1)

            def z_gate(g, j):
                dve.wait_ge(sg("go_ready", g), j * 4 + OPEN)
                dve.wait_ge(sg("z_tanh", g), j + 1)
                V.scalar_tensor_tensor(zg[:, CH * g:CH * g + CH].rearrange("p t v d -> p (t v d)"),
                                       zth[:, CH * g:CH * g + CH].rearrange("p t d -> p (t d)"), 1.0, bank_p[1][:],
                                       ALU.add, ALU.mult).then_inc(sg("z_gate", g), 1)

            def level(s, g, j):
                l = s // 2
                if s % 2 == 0:
                    dve.wait_ge(sg("y_ps", g), j * 6 + l + 1)
                    n_ = LEVELS[l]
                    V.tensor_tensor(lefts(yl[:, l], l), halves(bank_a[g], l),
                                    left(mask[:, l + 1, :], l).unsqueeze(1).broadcast_to([P, GU, HP // n_, n_]),
                                    ALU.mult).then_inc(sg("ym_ready", g), 1)

            def pairs(ap):
                return ap.rearrange("p (t v) s -> p t v s", v=PV)

            def chunks(ap):
                return ap.rearrange("p (t s) -> p t s", s=P).unsqueeze(2).broadcast_to([P, CH, PV, P])

            def solve(s, g, j, kh):
                bA, bB = bank_a[g], bank_b[g]
                if s == 0:
                    dve.wait_ge(sg("us_ready", g), j * 2 + OPEN)
                    dve.wait_ge(sg("qs_ready", g), j * 2 + OPEN)
                    V.tensor_scalar(ck[:, g], head_cols(g, kh, KINDS), 1.0, None, ALU.mult).then_inc(sg("ck_ready", g), 1)
                    dve.wait_ge(sg("solve_ps", g), j * SOLVE_PS + H_PS + OPEN)
                    V.tensor_tensor(units(ym, g), twoI[:].unsqueeze(1).broadcast_to([P, GU, P]), grid(bA[:]),
                                    ALU.subtract).then_inc(sg("h_ready", g), 1)
                elif s == 4:
                    dve.wait_ge(sg("solve_ps", g), j * SOLVE_PS + QS_PS + OPEN)
                    for p_ in range(PV):
                        V.scalar_tensor_tensor(rr[:, g, p_], bB[:, p_ * P:p_ * P + P], ck[:, g, NEGP, 1, p_:p_ + 1],
                                               v[:, CH * g + 1, p_], ALU.mult, ALU.add).then_inc(sg("r_ready", g), 1)
                elif s == 6:
                    dve.wait_ge(sg("z_gate", g), j * 2 + OPEN)
                    dve.wait_ge(sg("osq_ready", g), j + OPEN)
                    dve.wait_ge(sg("qs_ready", g), j * 2 + 2 + OPEN)
                    dve.wait_ge(sg("solve_ps", g), j * SOLVE_PS + O1_PS + OPEN)
                    V.tensor_tensor(o[:, CH * g + 1].rearrange("p v d -> p (v d)"), bA[:, 256:512],
                                    qs[:, g].rearrange("p v d -> p (v d)"), ALU.add).then_inc(sg("o1_ready", g), 1)
                elif s == 7:
                    dve.wait_ge(sg("osc_ready", g), j * 6 + OPEN)
                    dve.wait_ge(sg("osq_ready", g), j + 1 + OPEN)
                    V.tensor_reduce(oss[:, g].rearrange("p t v -> p (t v)"), units(osq, g), AXX,
                                    ALU.add).then_inc(sg("oss_ready", g), 1)

            def begin(s, g, j):
                bA, bB = bank_a[g], bank_b[g]
                if s == 9:
                    dve.wait_ge(sg("decay_beta", g), j + 1 + OPEN)
                    dve.wait_ge(sg("alo_ready", g), j * 2 + OPEN)
                    dve.wait_ge(sg("begin_ps", g), j * BEGIN_PS + KQ_PS + OPEN)
                    V.tensor_tensor(pairs(units(at, g)), pairs(units(e_b, g)[:, :, 0:P]), chunks(bB[:, 0:256]),
                                    ALU.mult).then_inc(sg("a_ready", g), 1)
                    dve.wait_ge(sg("solve_ps", g), j * SOLVE_PS + OPEN)
                    V.tensor_tensor(pairs(units(pt, g)), pairs(units(e_b, g)[:, :, 1:P + 1]), chunks(bB[:, 256:512]),
                                    ALU.mult).then_inc(sg("pt_ready", g), 1)
                    dve.wait_ge(sg("f_ready", g), j * 2 + OPEN)
                    dve.wait_ge(sg("ahi_ready", g), j + 1)
                    V.tensor_tensor(units(f_hi, g), ident16[:].unsqueeze(1).broadcast_to([P, GU, P]), units(a_hi, g),
                                    ALU.subtract).then_inc(sg("f_ready", g), 1)
                elif s == 10:
                    dve.wait_ge(sg("begin_ps", g), j * BEGIN_PS + F_PS + OPEN)
                    V.tensor_tensor(units(inv, g), grid(bA[:]), mask[:, 0, :].unsqueeze(1).broadcast_to([P, GU, P]),
                                    ALU.mult).then_inc(sg("x1_ready", g), 1)

            def out_weights(j):
                dve.wait_ge(sig("wo_dma"), j * 16 + 16)
                dve.wait_ge(sig("wo_ready"), j * 3 + OPEN)
                V.tensor_scalar(wo_n[:], wo_sb[:], nw_sb[:, 0:1], 0.5 * P ** 0.5 * O_SCALE, ALU.mult, ALU.mult).then_inc(sig("wo_ready"), 1)

            def split_and_decays(j):
                wq_low(j)
                decay_rhs(0, j, 0)
                decay_rhs(1, j, 0)

            def start(j, bp):
                for i in range(2, QKV_BLK):
                    convolution(i, 0, j)
                sum_squares(0, j)
                convolution(0, 1, j, start_banks[1])
                convolution(1, 1, j, start_banks[1])
                begin(9, 0, j)
                convolution(2, 1, j, start_banks[1])
                begin(10, 0, j)
                convolution(3, 1, j, start_banks[1])
                sum_squares(1, j, start_banks[1])

            def half(h, j, kh, first, last):
                g, js = 1 - h, j - 1 + h

                def beside(n):
                    if n == DVE_AT["z_gate"] and (h == 1 or not first):
                        z_gate(g, js)
                    if n == DVE_AT["wq_low"] and h == 0 and not last:
                        wq_low(j + 1)
                    if n == DVE_AT["wz_low"] and h == 0:
                        wz_low(j)
                    if n == DVE_AT["turned"] and not first:
                        turned_low(h, j - 1)
                    if n == DVE_AT["decay_cols"] and not last:
                        decay_rhs(h, j + 1, kh + 1)
                    for i in range(QKV_BLK):
                        if n == DVE_AT[f"conv_{i}"] and not last:
                            convolution(i, h, j + 1)
                    if n == DVE_AT["sum_squares"] and not last:
                        sum_squares(h, j + 1)
                    if n == 2 * SLOTS - 1 and h == 1:
                        out_weights(j)

                for s in range(SLOTS):
                    level(s, h, j)
                    beside(2 * s)
                    if h == 1 or not first:
                        solve(s, g, js, kh - 1 + h)
                    if h == 0 or not last:
                        begin(s, g, js + 1)
                    beside(2 * s + 1)

            def finish(j):
                for s in range(SLOTS):
                    solve(s, 1, j, NK - 1)
                    if s == 2:
                        z_gate(1, j)
                    if s == 4:
                        turned_low(0, j)
                turned_low(1, j)

            def residual(bp):
                for g in range(BG):
                    gx = gates[:, bass.ds(bp * BG + g, 1), 0].rearrange("p a c -> p (a c)")
                    for c_ in range(CH):
                        t = CH * g + c_
                        if t == 0:
                            dve.wait_ge(sg("y_sum", 0), bp * NK + NK + OPEN)
                            dve.wait_ge(sg("y_sum", 1), bp * NK + NK + OPEN)
                            dve.wait_ge(sig("yo_ready"), bp * TL + OPEN)
                        V.scalar_tensor_tensor(x2[:, t], bank_y[g][:, c_ * C:c_ * C + C], 1.0 / (Z_SCALE * O_SCALE), gx,
                                               ALU.mult, ALU.mult).then_inc(sig("x2_mul"), 1)
                for t in range(TL):
                    dve.wait_ge(sig("x2_mul"), bp * TL + t + 1)
                    V.tensor_tensor(x2[:, t], x2[:, t], xs[:, t], ALU.add).then_inc(sig("x2_ready"), 1)

            def hidden(bp, t):
                n_ = bp * TL + t
                for hf in range(2):
                    dve.wait_ge(sig("f_tanh"), n_ * 2 + hf + 1)
                    fs = f_th[:, hf * 512:hf * 512 + 512]
                    V.scalar_tensor_tensor(f_a[:, hf * 512:hf * 512 + 512], fs, 1.0, bank[2 + hf][:], ALU.add,
                                           ALU.mult).then_inc(sig("f_silu"), 1)
                for hf in range(2):
                    dve.wait_ge(sig("f_silu"), n_ * 2 + hf + 1 + OPEN)
                    dve.wait_ge(sig("f_s_ready"), n_ * 4 + OPEN)
                    V.tensor_tensor(f_h[:, hf * 512:hf * 512 + 512], f_a[:, hf * 512:hf * 512 + 512],
                                    bank[4 + hf][:], ALU.mult).then_inc(sig("f_h_ready"), 1)

            def two_of_four(bp, t):
                n_ = bp * TL + t
                dve.wait_ge(sig("f_h_ready"), n_ * 2 + 2 + OPEN)
                V.scalar_tensor_tensor(f_a, f_h, -1.0, f_h, ALU.mult, ALU.max).then_inc(sig("f_rank"), 1)
                dve.wait_ge(sig("f_rank"), n_ * 12 + 1)
                a4 = f_a.rearrange("p (n f) -> p n f", f=4)
                V.tensor_tensor(f_c1[:].rearrange("p i n -> p n i"), a4[:, :, 0:3], a4[:, :, 1:4], ALU.is_ge).then_inc(sig("f_rank"), 1)
                V.tensor_tensor(f_c2[:].rearrange("p i n -> p n i"), a4[:, :, 0:2], a4[:, :, 2:4], ALU.is_ge).then_inc(sig("f_rank"), 1)
                V.tensor_tensor(f_c3[:], a4[:, :, 0], a4[:, :, 3], ALU.is_ge).then_inc(sig("f_rank"), 1)
                dve.wait_ge(sig("f_rank"), n_ * 12 + 4)
                c01, c12, c23 = (f_c1[:, i] for i in range(3))
                c02, c13 = (f_c2[:, i] for i in range(2))
                c03 = f_c3[:]
                w = f_w
                V.tensor_tensor(w[:, 0, 0], c01, c02, ALU.add).then_inc(sig("f_rank"), 1)
                V.tensor_tensor(w[:, 0, 1], c12, c13, ALU.add).then_inc(sig("f_rank"), 1)
                V.tensor_tensor(w[:, 0, 2], c23, c02, ALU.subtract).then_inc(sig("f_rank"), 1)
                V.tensor_tensor(w[:, 0, 3], c03, c13, ALU.add).then_inc(sig("f_rank"), 1)
                dve.wait_ge(sig("f_rank"), n_ * 12 + 8)
                V.tensor_tensor(w[:, 1, 0], w[:, 0, 0], c03, ALU.add).then_inc(sig("f_rank"), 1)
                V.tensor_tensor(w[:, 1, 1], w[:, 0, 1], c01, ALU.subtract).then_inc(sig("f_rank"), 1)
                V.tensor_tensor(w[:, 1, 2], w[:, 0, 2], c12, ALU.subtract).then_inc(sig("f_rank"), 1)
                V.tensor_tensor(w[:, 1, 3], w[:, 0, 3], c23, ALU.add).then_inc(sig("f_rank"), 1)
                dve.wait_ge(sig("f_rank"), n_ * 12 + 12)
                dve.wait_ge(sig("f_sT_ps"), n_ * 2 + OPEN)
                h4 = f_h.rearrange("p (n f) -> p n f", f=4)
                s4 = f_s.rearrange("p (n f) -> p n f", f=4)
                for i, (op, thr) in enumerate(((ALU.is_ge, 2.0), (ALU.is_ge, 1.0), (ALU.is_ge, 0.0), (ALU.is_le, 1.0))):
                    V.scalar_tensor_tensor(s4[:, :, i], w[:, 1, i], thr, h4[:, :, i], op,
                                           ALU.mult).then_inc(sig("f_s_ready"), 1)

            def add_down(bp, t):
                n_ = bp * TL + t
                dve.wait_ge(sig("down_ps"), n_ + 1 + OPEN)
                dve.wait_ge(sig("out_dma"), n_ * 16 + OPEN)
                gx = gates[:, bass.ds(bp * BG + t // CH, 1), 1].rearrange("p a c -> p (a c)")
                V.tensor_tensor(yo[:], bank[0][:, 0:C], gx, ALU.mult).then_inc(sig("yo_mul"), 1)
                dve.wait_ge(sig("yo_mul"), n_ + 1 + OPEN)
                V.tensor_tensor(yo[:], yo[:], x2[:, t], ALU.add).then_inc(sig("yo_ready"), 1)

            def whole_block(bp, last):
                schedule(dve, bp, start, half, finish)
                residual(bp)
                layernorm(bp * 2 + 1, x2, bp, bp * TL + TL)
                if not last:
                    layernorm(bp * 2 + 2, xs, bp + 1, None)
                hidden(bp, 0)
                for t in range(TL):
                    two_of_four(bp, t)
                    if t + 1 < TL:
                        hidden(bp, t + 1)
                    if not last and t == 1:
                        beta_parts(bp + 1)
                    if not last and t == 3:
                        for i in range(2):
                            convolution(i, 0, bp * NK + NK)
                    add_down(bp, t)
                    if not last and t == 1:
                        beta_and_g(bp + 1)
                    if not last and t == 2:
                        decay_factors(bp + 1)
                        split_and_decays(bp * NK + NK)

            layernorm(0, xs, 0, None)
            beta_parts(0)
            beta_and_g(0)
            decay_factors(0)
            split_and_decays(0)
            for i in range(2):
                convolution(i, 0, 0)
            with dve.Fori(0, NB - 1) as bp:
                whole_block(bp, False)
            whole_block(NB - 1, True)

_OUT = (B, T, C)


def kernel(**inputs):
    import numpy as np
    import concourse.bacc as bacc
    from concourse.bass_utils import run_bass_kernel_spmd

    a = {k.replace("L0_", ""): np.asarray(v) for k, v in inputs.items()}
    qd = NK * P

    def rows128(w):
        return np.ascontiguousarray(w.reshape(-1, P, w.shape[1]).transpose(1, 0, 2))

    wq = a["attn_W_qkv"]
    heads = []
    for h in range(NK):
        q, k = wq[h * P:(h + 1) * P], wq[qd + h * P:qd + (h + 1) * P]
        vv = wq[2 * qd + h * PV * P:2 * qd + (h + 1) * PV * P]
        cw = a["attn_conv_w"]
        cws = [cw[qd + h * P:qd + (h + 1) * P], cw[h * P:(h + 1) * P],
               cw[2 * qd + h * PV * P:2 * qd + h * PV * P + P], cw[2 * qd + h * PV * P + P:2 * qd + (h + 1) * PV * P]]
        w = rows128(np.concatenate([k, q, vv], 0).T).reshape(P, -1)
        heads.append(np.concatenate([w, np.stack(cws, 1).reshape(P, -1)], 1))
    arrays = {
        "x": a["attn_x"].reshape(B * T, C),
        "wqkv": np.stack(heads),
        "wz": np.stack([rows128(a["attn_W_z"][h * PV * P:(h + 1) * PV * P].T) for h in range(NK)]),
        "wout": np.ascontiguousarray(a["attn_W_out"].T.reshape(NK, PV, P, C).transpose(0, 2, 1, 3)),
        "nw": a["attn_norm_w"].reshape(P, 1),
        "wba": rows128(np.concatenate([a["attn_W_b"], a["attn_W_a"]], 0).T),
        "dtb": a["attn_dt_bias"].reshape(1, NV),
        "alog": a["attn_A_log"].reshape(1, NV),
        "wgate": rows128(a["ffn_w_gate"]),
        "wup": rows128(a["ffn_w_up"]),
        "wdown": rows128(a["ffn_w_down"]),
        "cT": rows128(a["c"].T),
        "wmod": rows128(a["wmod"]),
    }
    arrays = {f"in_{k}": np.ascontiguousarray(v) for k, v in arrays.items()}
    nc = bacc.Bacc("TRN2", target_bir_lowering=False, num_devices=1)
    args = [nc.dram_tensor(k, v.shape, mybir.dt.from_np(v.dtype), kind="ExternalInput").ap() for k, v in arrays.items()]
    args.append(nc.dram_tensor("out_0", (B * T, C), F32, kind="ExternalOutput").ap())
    adaln_deltanet_ffn(nc, *args)
    r = run_bass_kernel_spmd(nc, [arrays], core_ids=[0])
    return r.results[0]["out_0"].reshape(_OUT)
```
